# Optimizing a Trainium2 kernel written in Bass

```python
import numpy as np
import jax
import jax.numpy as jnp

def _softmax(x, axis=-1):
    return jax.nn.softmax(x, axis=axis)

def _gelu(x):
    return jax.nn.gelu(x, approximate=True)

def _silu(x):
    return jax.nn.silu(x)

def _sigmoid(x):
    return jax.nn.sigmoid(x)

def _layernorm(x, axis=-1, eps=1e-05):
    m = jnp.mean(x, axis=axis, keepdims=True)
    v = jnp.var(x, axis=axis, keepdims=True)
    return (x - m) / jnp.sqrt(v + eps)

def _scatter_add(tgt, idx, src, axis=0):
    return tgt.at[idx].add(src)

def _segment_sum(src, seg, n):
    return jax.ops.segment_sum(src, seg, n)
kernel_name = 'mk_decoder_postln_d1_seqx_r8_18f8ac'

def setup_inputs(seed: int=0):
    np.random.seed(seed)
    _w = jnp.asarray

    def _rec_inputs():
        import jax
        import jax.numpy as jnp
        _rk = jax.random.key(seed)
        x = 2.818e-05 + 1 * jax.random.normal(jax.random.fold_in(_rk, 1), (4, 256, 256), jnp.float32)
        _lenS = 256 - jax.random.randint(jax.random.fold_in(_rk, 7), (4,), 0, max(1, 256 // 4) + 1, jnp.int32)
        _lenS2 = 256 - jax.random.randint(jax.random.fold_in(_rk, 8), (4,), 0, max(1, 256 // 4) + 1, jnp.int32)
        _ctx_1024P = jax.random.normal(jax.random.fold_in(_rk, 11), (4, 16, 128), jnp.float32)
        _ctx_1024c = jax.random.dirichlet(jax.random.fold_in(_rk, 511), 0.3 * jnp.ones((16,), jnp.float32), (4, 256))
        _ctx_1024t = jnp.einsum('bsk,bkd->bsd', _ctx_1024c, _ctx_1024P)
        _ctx_1024t = _ctx_1024t * jax.lax.rsqrt(jnp.mean(jnp.square(_ctx_1024t)) + 1e-12) * 0.953939
        ctx_1024 = 7.22013e-05 + 1.00017 * (_ctx_1024t + 0.3 * jax.random.normal(jax.random.fold_in(_rk, 611), (4, 256, 128), jnp.float32))
        return (x, ctx_1024)
    x, ctx_1024 = _rec_inputs()

    def _L0_attn_setup():
        import jax, jax.numpy as jnp
        import numpy as np
        HIDDEN = 256
        HEADS = 32
        HEAD_DIM = HIDDEN // HEADS
        MAX_POS = 64
        TABLE = 2 * MAX_POS - 1

        def _rel_bias(rel_pos, seq_len):
            pos = jnp.arange(seq_len)
            rel = pos[None, :] - pos[:, None] + (MAX_POS - 1)
            rel = jnp.clip(rel, 0, TABLE - 1)
            return rel_pos[rel].mean(axis=-1)
        key = jax.random.key(seed)
        k = jax.random.split(key, 6)
        B, S = (16, 64)
        return {'hidden_states': jax.random.normal(k[0], (B, S, HIDDEN), dtype=jnp.float32), 'wq': jax.random.normal(k[1], (HIDDEN, HIDDEN), dtype=jnp.float32) * 0.02, 'wk': jax.random.normal(k[2], (HIDDEN, HIDDEN), dtype=jnp.float32) * 0.02, 'wv': jax.random.normal(k[3], (HIDDEN, HIDDEN), dtype=jnp.float32) * 0.02, 'wo': jax.random.normal(k[4], (HIDDEN, HIDDEN), dtype=jnp.float32) * 0.02, 'rel_pos': jax.random.normal(k[5], (TABLE, HEAD_DIM), dtype=jnp.float32)}
    _L0_attn_all = _L0_attn_setup()
    _L0_attn_in = {k: v for k, v in _L0_attn_all.items() if k in ('wq', 'wk', 'wv', 'wo', 'rel_pos')}
    del _L0_attn_all

    def _L0_xattn_setup():
        import jax, jax.numpy as jnp
        import numpy as np
        B_, L_, D_MODEL = (4, 256, 128)
        D_STATE, D_CONV, EXPAND = (16, 4, 2)
        D_INNER = EXPAND * D_MODEL
        DT_RANK = (D_MODEL + 15) // 16

        def silu(x):
            return x * jax.nn.sigmoid(x)
        key = jax.random.key(seed)
        ks = jax.random.split(key, 10)
        f32 = jnp.float32
        hidden_states = jax.random.normal(ks[0], (B_, L_, D_MODEL), dtype=f32)
        z = jax.random.normal(ks[1], (B_, D_INNER, L_), dtype=f32)
        in_proj_w = jax.random.normal(ks[2], (D_INNER, D_MODEL), dtype=f32) * 0.02
        conv_w = jax.random.normal(ks[3], (D_INNER, 1, D_CONV), dtype=f32) * 0.1
        conv_b = jax.random.normal(ks[4], (D_INNER,), dtype=f32) * 0.02
        x_proj_w = jax.random.normal(ks[5], (DT_RANK + 2 * D_STATE, D_INNER), dtype=f32) * 0.02
        dt_proj_w = jax.random.uniform(ks[6], (D_INNER, DT_RANK), dtype=f32, minval=-DT_RANK ** (-0.5), maxval=DT_RANK ** (-0.5))
        dt = jnp.exp(jax.random.uniform(ks[7], (D_INNER,), dtype=f32, minval=np.log(0.001), maxval=np.log(0.1)))
        dt_proj_b = jnp.log(jnp.expm1(dt))
        A_log = jnp.log(jnp.broadcast_to(jnp.arange(1, D_STATE + 1, dtype=f32), (D_INNER, D_STATE)))
        D = jnp.ones((D_INNER,), f32)
        return {'hidden_states': hidden_states, 'z': z, 'in_proj_w': in_proj_w, 'conv_w': conv_w, 'conv_b': conv_b, 'x_proj_w': x_proj_w, 'dt_proj_w': dt_proj_w, 'dt_proj_b': dt_proj_b, 'A_log': A_log, 'D': D}
    _L0_xattn_all = _L0_xattn_setup()
    _L0_xattn_in = {k: v for k, v in _L0_xattn_all.items() if k in ('in_proj_w', 'conv_w', 'conv_b', 'x_proj_w', 'dt_proj_w', 'dt_proj_b', 'A_log', 'D')}
    del _L0_xattn_all

    def _L0_ffn_setup():
        import jax, jax.numpy as jnp
        import numpy as np
        D_MODEL = 256
        D_FF = 1024
        N_EXPERTS = 4
        B, S = (2, 256)
        key = jax.random.key(seed)
        ks = jax.random.split(key, 6)
        scale = 0.02
        return {'hidden_states': jax.random.normal(ks[0], (B, S, D_MODEL), dtype=jnp.float32), 'Wr': jax.random.normal(ks[1], (D_MODEL, N_EXPERTS), dtype=jnp.float32) * scale, 'br': jnp.zeros((N_EXPERTS,), dtype=jnp.float32), 'Wg': jax.random.normal(ks[2], (N_EXPERTS, D_MODEL, D_FF), dtype=jnp.float32) * scale, 'Wu': jax.random.normal(ks[3], (N_EXPERTS, D_MODEL, D_FF), dtype=jnp.float32) * scale, 'Wd': jax.random.normal(ks[4], (N_EXPERTS, D_FF, D_MODEL), dtype=jnp.float32) * scale}
    _L0_ffn_all = _L0_ffn_setup()
    _L0_ffn_in = {k: v for k, v in _L0_ffn_all.items() if k in ('Wr', 'br', 'Wg', 'Wu', 'Wd')}
    del _L0_ffn_all
    return {'x': x, 'ctx_1024': ctx_1024, 'L0_attn_wq': _L0_attn_in['wq'], 'L0_attn_wk': _L0_attn_in['wk'], 'L0_attn_wv': _L0_attn_in['wv'], 'L0_attn_wo': _L0_attn_in['wo'], 'L0_attn_rel_pos': _L0_attn_in['rel_pos'], 'L0_xattn_in_proj_w': _L0_xattn_in['in_proj_w'], 'L0_xattn_conv_w': _L0_xattn_in['conv_w'], 'L0_xattn_conv_b': _L0_xattn_in['conv_b'], 'L0_xattn_x_proj_w': _L0_xattn_in['x_proj_w'], 'L0_xattn_dt_proj_w': _L0_xattn_in['dt_proj_w'], 'L0_xattn_dt_proj_b': _L0_xattn_in['dt_proj_b'], 'L0_xattn_A_log': _L0_xattn_in['A_log'], 'L0_xattn_D': _L0_xattn_in['D'], 'L0_ffn_Wr': _L0_ffn_in['Wr'], 'L0_ffn_br': _L0_ffn_in['br'], 'L0_ffn_Wg': _L0_ffn_in['Wg'], 'L0_ffn_Wu': _L0_ffn_in['Wu'], 'L0_ffn_Wd': _L0_ffn_in['Wd']}

def reference(x, ctx_1024, L0_attn_wq, L0_attn_wk, L0_attn_wv, L0_attn_wo, L0_attn_rel_pos, L0_xattn_in_proj_w, L0_xattn_conv_w, L0_xattn_conv_b, L0_xattn_x_proj_w, L0_xattn_dt_proj_w, L0_xattn_dt_proj_b, L0_xattn_A_log, L0_xattn_D, L0_ffn_Wr, L0_ffn_br, L0_ffn_Wg, L0_ffn_Wu, L0_ffn_Wd):
    import jax
    import jax.numpy as jnp

    def _L0_attn_ref(hidden_states, wq, wk, wv, wo, rel_pos):
        import jax, jax.numpy as jnp
        import numpy as np
        HIDDEN = 256
        HEADS = 32
        HEAD_DIM = HIDDEN // HEADS
        MAX_POS = 64
        TABLE = 2 * MAX_POS - 1

        def _rel_bias(rel_pos, seq_len):
            pos = jnp.arange(seq_len)
            rel = pos[None, :] - pos[:, None] + (MAX_POS - 1)
            rel = jnp.clip(rel, 0, TABLE - 1)
            return rel_pos[rel].mean(axis=-1)
        B, S, _ = hidden_states.shape
        scale = jnp.sqrt(jnp.float32(HEAD_DIM))
        q = (hidden_states @ wq.T).reshape(B, S, HEADS, HEAD_DIM).transpose(0, 2, 1, 3)
        k = (hidden_states @ wk.T).reshape(B, S, HEADS, HEAD_DIM).transpose(0, 2, 1, 3)
        v = (hidden_states @ wv.T).reshape(B, S, HEADS, HEAD_DIM).transpose(0, 2, 1, 3)
        scores = jnp.einsum('bhqd,bhkd->bhqk', q, k) / scale
        scores = scores + _rel_bias(rel_pos, S)[None, None]
        attn = jax.nn.softmax(scores, axis=-1)
        ctx = jnp.einsum('bhqk,bhkd->bhqd', attn, v)
        ctx = ctx.transpose(0, 2, 1, 3).reshape(B, S, HIDDEN)
        return ctx @ wo.T

    def _L0_xattn_ref(hidden_states, z, in_proj_w, conv_w, conv_b, x_proj_w, dt_proj_w, dt_proj_b, A_log, D):
        import jax, jax.numpy as jnp
        import numpy as np
        B_, L_, D_MODEL = (4, 256, 128)
        D_STATE, D_CONV, EXPAND = (16, 4, 2)
        D_INNER = EXPAND * D_MODEL
        DT_RANK = (D_MODEL + 15) // 16

        def silu(x):
            return x * jax.nn.sigmoid(x)
        Bsz, L, _ = hidden_states.shape
        d_inner, _, d_conv = conv_w.shape
        dt_rank = dt_proj_w.shape[1]
        d_state = A_log.shape[1]
        x = jnp.einsum('bld,ed->bel', hidden_states, in_proj_w)
        xc = jax.lax.conv_general_dilated(x, conv_w, window_strides=(1,), padding=[(d_conv - 1, 0)], feature_group_count=d_inner, dimension_numbers=('NCH', 'OIH', 'NCH'))
        x = silu(xc + conv_b[None, :, None])
        x_dbl = jnp.einsum('bdl,ed->bel', x, x_proj_w)
        dt_low, Bm, Cm = jnp.split(x_dbl, [dt_rank, dt_rank + d_state], axis=1)
        dt = jnp.einsum('brl,dr->bdl', dt_low, dt_proj_w)
        dt = jax.nn.softplus(dt + dt_proj_b[None, :, None])
        A = -jnp.exp(A_log)
        dt_t = jnp.moveaxis(dt, -1, 0)
        B_t = jnp.moveaxis(Bm, -1, 0)
        C_t = jnp.moveaxis(Cm, -1, 0)
        u_t = jnp.moveaxis(x, -1, 0)

        def step(state, inp):
            d, b, c, u = inp
            dA = jnp.exp(d[..., None] * A)
            state = state * dA + (d * u)[..., None] * b[:, None, :]
            y = jnp.einsum('bdn,bn->bd', state, c)
            return (state, y)
        state0 = jnp.zeros((Bsz, d_inner, d_state), x.dtype)
        _, ys = jax.lax.scan(step, state0, (dt_t, B_t, C_t, u_t))
        y = jnp.moveaxis(ys, 0, 2)
        y = y + D[None, :, None] * x
        y = y * silu(z)
        return jnp.swapaxes(y, 1, 2)

    def _L0_ffn_ref(hidden_states, Wr, br, Wg, Wu, Wd):
        import jax, jax.numpy as jnp
        import numpy as np
        D_MODEL = 256
        D_FF = 1024
        N_EXPERTS = 4
        B, S = (2, 256)
        b, s, d = hidden_states.shape
        x = hidden_states.reshape(-1, d)
        logits = x @ Wr + br
        probs = jax.nn.softmax(logits, axis=-1)
        top_w, top_idx = jax.lax.top_k(probs, 1)
        g = jnp.einsum('td,edf->tef', x, Wg)
        u = jnp.einsum('td,edf->tef', x, Wu)
        h = jax.nn.silu(g) * u
        y = jnp.einsum('tef,efd->ted', h, Wd)
        sel = jnp.take_along_axis(y, top_idx[:, :, None], axis=1)[:, 0]
        out = sel * top_w
        return out.reshape(b, s, d)
    x = _layernorm(x + _L0_attn_ref(x, L0_attn_wq, L0_attn_wk, L0_attn_wv, L0_attn_wo, L0_attn_rel_pos), axis=-1)
    x = _layernorm(x + _L0_xattn_ref(ctx_1024, x, L0_xattn_in_proj_w, L0_xattn_conv_w, L0_xattn_conv_b, L0_xattn_x_proj_w, L0_xattn_dt_proj_w, L0_xattn_dt_proj_b, L0_xattn_A_log, L0_xattn_D), axis=-1)
    x = _layernorm(x + _L0_ffn_ref(x, L0_ffn_Wr, L0_ffn_br, L0_ffn_Wg, L0_ffn_Wu, L0_ffn_Wd), axis=-1)
    return x

_drawn_inputs = setup_inputs


def setup_inputs(seed=0):
    import zlib

    import numpy as np

    out = dict(_drawn_inputs(seed))
    spreads = {'L0_xattn_D': (1.0, 0.6), 'L0_ffn_br': (0.0, 0.8)}
    factors = {'ctx_1024': 4.282,
     'L0_attn_wq': 8.0,
     'L0_attn_wk': 8.0,
     'L0_attn_wv': 8.0,
     'L0_attn_wo': 8.0,
     'L0_attn_rel_pos': 8.0,
     'L0_xattn_in_proj_w': 4.298,
     'L0_xattn_conv_w': 4.486,
     'L0_xattn_conv_b': 8.0,
     'L0_xattn_x_proj_w': 8.0,
     'L0_xattn_dt_proj_w': 8.0,
     'L0_xattn_dt_proj_b': 8.0,
     'L0_xattn_A_log': 8.0,
     'L0_ffn_Wr': 5.705,
     'L0_ffn_Wg': 4.805,
     'L0_ffn_Wu': 4.727,
     'L0_ffn_Wd': 4.749}
    for name, (base, spread) in spreads.items():
        noise = np.random.default_rng([zlib.crc32(name.encode()), seed]).standard_normal(out[name].shape)
        drawn = base * np.exp(spread * noise) if base else spread * noise
        out[name] = jnp.asarray(drawn.astype(out[name].dtype))
    for name, factor in factors.items():
        out[name] = (out[name] * factor).astype(out[name].dtype)
    return out
```

```python
from contextlib import ExitStack

import concourse.bass as bass
from concourse import mybir

F32 = mybir.dt.float32
BF16 = mybir.dt.bfloat16
F16 = mybir.dt.float16
I32 = mybir.dt.int32
U32 = mybir.dt.uint32
ALU = mybir.AluOpType
ACT = mybir.ActivationFunctionType
AX = mybir.AxisListType

P = 128
BATCH, SEQ, DM = 4, 256, 256
TOK = BATCH * SEQ
TT = TOK // P
KT = DM // P
HEADS, DH = 32, 8
HALF = 512
DC = 128
STATES, TAPS, RANK = 16, 4, 8
PAD = TAPS - 1
PB = PAD + SEQ
TABLE = 127
ROWS = 6 * DH
QUADS = HEADS // 4
VW = DH + 1
SPREAD = 2 * SEQ - 1
EXPERTS, DFF = 4, 1024
FT = DFF // P
SLOTS = TT + EXPERTS - 1
EPS = 1e-5
LOG1P = [1.0, -0.499998927, 0.333297104, -0.249516159, 0.196632743, -0.152696669, 0.105436236, -0.0563736148,
         0.0195425283, -0.00317605701]
RSQRT_SEED = 0x5F3759DF
XW = DM + 4
FAR = 2048


def decoder_layer(nc, x, ctx_in, wq, wk, wv, wo, rel_pos, in_proj_w, conv_w, conv_b, x_proj_w, dt_proj_w,
                  dt_proj_b, A_log, D, Wr, br, Wg, Wu, Wd, out):
    with ExitStack() as stack:
        def sb(name, shape, dt=F32):
            return stack.enter_context(nc.sbuf_tensor(name, shape, dt))

        def sem(name):
            return stack.enter_context(nc.semaphore(name))

        def dram(name, shape, dt):
            return nc.dram_tensor(name, shape, dt, kind="Internal").ap()

        diag_d = dram("diag_d", (1, SPREAD), F32)
        qp_d = [dram(f"qp{i}_d", (DM, TOK), BF16) for i in range(3)]
        kp_d = [dram(f"kp{i}_d", (DM, TOK), BF16) for i in range(3)]
        x2_d = dram("x2_d", (TOK, XW), F32)

        xres = sb("xres", [P, TT, DM])
        identf = sb("identf", [P, P])
        flip = sb("flip", [P, P], F16)
        woT = sb("woT", [P, KT, DM])
        vaug = sb("vaug", [P, TT, HEADS, VW])
        hankel = sb("hankel", [P, KT, SEQ])
        hank_hi = sb("hank_hi", [P, KT, SEQ], F16)
        hank_lo = sb("hank_lo", [P, KT, SEQ], F16)
        yT = sb("yT", [P, KT, TOK])
        wr_s = sb("wr_s", [P, KT, EXPERTS])
        br_s = sb("br_s", [P, EXPERTS])
        stats = sb("stats", [P, TT, 6])
        mv = sb("mv", [P, TT, 2])
        rstd = sb("rstd", [P, TT])
        nwt = sb("nwt", [P, TT])
        veps = sb("veps", [P, TT])
        ARENA = 41 * 1024
        arena = sb("arena", [P, ARENA])
        top = [0]

        def carve(cols, *shape, dt=F32, rows=P):
            a = arena[0:rows, top[0]:top[0] + cols]
            top[0] += cols
            assert top[0] <= ARENA, top[0]
            if dt != F32:
                a = a.bitcast(dt)
            if len(shape) == 2:
                a = a.rearrange("p (a b) -> p a b", a=shape[0])
            if len(shape) == 3:
                a = a.rearrange("p (a b c) -> p a b c", a=shape[0], b=shape[1])
            return a

        qst = [carve(HEADS // 2 * SEQ // 2, HEADS // 2, SEQ, dt=BF16) for _ in range(2)]
        kst = [carve(HEADS // 2 * SEQ // 2, HEADS // 2, SEQ, dt=BF16) for _ in range(2)]
        stacks_top = top[0]
        q_s = carve(KT * TOK, KT, TOK)
        k_s = carve(KT * TOK, KT, TOK)
        parts = [carve(KT * TOK // 2, KT, TOK, dt=BF16) for _ in range(3)]
        work_top = top[0]
        ctx_tok = carve(TT * DC, TT, DC)
        ctxT = carve(TOK)
        w_raw = carve(4 * KT * DM, 4 * KT, DM)
        wT = carve(3 * KT * DM, 3 * KT, DM)
        inw = carve(KT * DC, KT, DC)
        inwT = carve(DM)
        work_end = top[0]
        xT = carve(KT * TOK, KT, TOK)
        xpw = carve(DM, rows=RANK + 2 * STATES)
        xpB = carve(KT * 96, KT, 96)
        xpC = carve(KT * 96, KT, 96)
        xpD = carve(KT * RANK, KT, RANK)
        dtw = carve(KT * RANK, KT, RANK)
        dtwT = carve(DM, rows=RANK)
        cw = carve(KT * TAPS, KT, TAPS)
        cb = carve(KT)
        dtb = carve(KT)
        alog = carve(KT * STATES, KT, STATES)
        acol = carve(KT * STATES, KT, STATES)
        dcol = carve(KT)
        xin_at = top[0]
        xin = carve(KT * BATCH * PB, KT, BATCH, PB)
        u = carve(KT * TOK, KT, TOK)
        ta = carve(KT * TOK, KT, TOK)
        tb_at = top[0]
        tb = carve(KT * TOK, KT, TOK)
        dts = carve(KT * TOK, KT, TOK)
        dtlow = carve(TOK, rows=RANK)
        bc3 = carve(TOK, 2, TOK, dt=BF16, rows=96)
        sel = carve(STATES * P // 2, STATES, P, dt=BF16, rows=96)
        relrow = carve(TABLE * DH, TABLE, DH, rows=1)
        diag = carve(SPREAD + 1, rows=1)
        top[0] = xin_at
        spt = carve(KT * TOK, KT, TOK)
        top[0] = tb_at
        bct = [carve(TOK, 2, TOK, dt=BF16, rows=96) for _ in range(2)]
        top[0] = work_top
        dA = [carve(HALF, 2, SEQ) for _ in range(4)]
        dBu = [carve(HALF) for _ in range(2)]
        hst = [carve(HALF) for _ in range(2)]
        prod = [carve(HALF) for _ in range(4)]
        assert top[0] <= work_end
        top[0] = stacks_top
        prob = [carve(4 * SEQ) for _ in range(4)]
        ctxS = [carve(QUADS * SEQ, QUADS, SEQ) for _ in range(2)]
        ctxn = carve(DM)
        ctxnT = carve(KT * P, KT, P)
        negm = [carve(2 * HEADS, 2, HEADS) for _ in range(2)]
        negmT = carve(SEQ // 2, dt=BF16, rows=HEADS)
        rcp = carve(16)
        attn_end = top[0]
        top[0] = stacks_top + 4096 + 4096 + 1024
        assert attn_end <= top[0]
        wg_s = carve(KT * EXPERTS * DFF, KT, EXPERTS * DFF)
        wu_s = carve(KT * EXPERTS * DFF, KT, EXPERTS * DFF)
        wd_s = carve(FT * EXPERTS * DM, FT, EXPERTS * DM)
        weights_at = stacks_top + 4096 + 4096 + 1024
        top[0] = 0
        sg = carve(TT * DM, TT, DM)
        gated = carve(TT * DM, TT, DM)
        x2T = carve(KT * TOK, KT, TOK)
        x2 = carve(TT * XW, TT, XW)
        lg = carve(TT * EXPERTS, TT, EXPERTS)
        ex = carve(TT * EXPERTS, TT, EXPERTS)
        lmax = carve(TT)
        lsum = carve(TT)
        gate_w = carve(TT)
        oh = carve(TT * EXPERTS, TT, EXPERTS)
        ohb = carve(EXPERTS * TT // 2, EXPERTS, TT, dt=BF16)
        run = carve(TT)
        within = carve(EXPERTS * TT, EXPERTS, TT)
        total = carve(EXPERTS * TT, EXPERTS, TT)
        incl = carve(EXPERTS * TT, EXPERTS, TT)
        thr = carve(TT)
        over = carve(EXPERTS * TT, EXPERTS, TT)
        ntile = carve(EXPERTS)
        tile_incl = carve(EXPERTS)
        tile0 = carve(EXPERTS)
        ones32 = carve(32)
        pos = carve(TT)
        slot_no = carve(SLOTS)
        e_cmp = carve(SLOTS)
        e_of = carve(SLOTS)
        e_int = carve(SLOTS, dt=I32)
        idx = carve(SLOTS, dt=U32)
        ltri = carve(P // 2, dt=BF16)
        ones_b = carve(P // 2, dt=BF16)
        tokid = carve(TT, dt=F16)[:, 0:TT]
        iota16 = carve(SLOTS * P // 2, dt=F16)
        assert top[0] <= weights_at, (top[0], weights_at)
        top[0] = 0
        onehot = [carve(SLOTS * P // 2, dt=F16) for _ in range(TT)]
        assert top[0] <= 3 * TT * DM
        rows_s = sb("rows_s", [P, SLOTS, XW])
        top[0] = 0
        xsT = carve(KT * SLOTS * P, KT, SLOTS * P)
        xcur = carve(KT * P, KT, P)
        ge = carve(DFF)
        hcur = carve(DFF)
        hT = carve(FT * P, FT, P)
        zrow = carve(DM)
        assert top[0] <= weights_at
        ps = stack.enter_context(nc.psum_tensor("ps", [P, 8, HALF], F32))

        ld_ctx = sem("ld_ctx")
        ld_x = sem("ld_x")
        ld_w = sem("ld_w")
        ld_misc = sem("ld_misc")
        consts = sem("consts")
        pe_fill = sem("pe_fill")
        act_evac = sem("act_evac")
        dve_evac = sem("dve_evac")
        conv_done = sem("conv_done")
        u_ready = sem("u_ready")
        split_ready = sem("split_ready")
        dbu_ready = sem("dbu_ready")
        row_order = sem("row_order")
        sp_exp = sem("sp_exp")
        a_exp = sem("a_exp")
        scan_in = sem("scan_in")
        bc_ready = sem("bc_ready")
        da_ready = sem("da_ready")
        scanned = sem("scanned")
        prod_ready = sem("prod_ready")
        y_added = sem("y_added")
        pe_mark = sem("pe_mark")
        act_mark = sem("act_mark")
        dve_mark = sem("dve_mark")
        dve_order = sem("dve_order")
        act_order = sem("act_order")
        pool_order = sem("pool_order")
        mixer_done = sem("mixer_done")
        part_ready = sem("part_ready")
        part_out = [sem(f"part_out{i}") for i in range(3)]
        diag_ready = sem("diag_ready")
        diag_out = sem("diag_out")
        hank_in = sem("hank_in")
        hank_ready = sem("hank_ready")
        ones_rows = sem("ones_rows")
        stack_in = [[sem(f"stack_in{b}{h}") for h in range(2)] for b in range(2)]
        a_scores = sem("a_scores")
        a_max = sem("a_max")
        m_turned = sem("m_turned")
        m_ready = sem("m_ready")
        m_in = sem("m_in")
        b_scores = sem("b_scores")
        p_ready = sem("p_ready")
        pv_done = sem("pv_done")
        pv_out = sem("pv_out")
        tail_pe = sem("tail_pe")
        tail_dve = sem("tail_dve")
        x1_ready = sem("x1_ready")
        sg_ready = sem("sg_ready")
        gated_ready = sem("gated_ready")
        back_pe = sem("back_pe")
        x2_ready = sem("x2_ready")
        x2t_pe = sem("x2t_pe")
        x2t_out = sem("x2t_out")
        logit_pe = sem("logit_pe")
        logit_dve = sem("logit_dve")
        gate_exp = sem("gate_exp")
        oh_ready = sem("oh_ready")
        count_pe = sem("count_pe")
        hot_ready = sem("hot_ready")
        idx_pe = sem("idx_pe")
        x2_full = sem("x2_full")
        x2_out = sem("x2_out")
        idx_ready = sem("idx_ready")
        rows_in = [sem(f"rows_in{s}") for s in range(SLOTS)]
        xs_pe = sem("xs_pe")
        xs_out = sem("xs_out")
        w_in = sem("w_in")
        xcur_ready = sem("xcur_ready")
        gu_done = sem("gu_done")
        ge_ready = sem("ge_ready")
        h_ready = sem("h_ready")
        ht_pe = sem("ht_pe")
        ht_ready = sem("ht_ready")
        y_done = sem("y_done")
        z_ready = sem("z_ready")
        row_ready = sem("row_ready")
        out_done = sem("out_done")
        block = stack.enter_context(nc.Block())

        F_CTX, F_INW, F_DTW, F_XIN, F_XT, F_WT, F_Q, F_K, F_V, F_B, F_C, F_LOW, F_DT = \
            0, 2, 3, 4, 8, 12, 16, 20, 24, 28, 30, 32, 34
        FILLS = 38
        N_CTX = 9 * 16

        def wait_evac(eng, j):
            if j == F_INW:
                eng.wait_ge(dve_evac, 1)
            else:
                eng.wait_ge(act_evac, j + 1 - (j > F_INW))

        def a_units(b, qd):
            if b >= BATCH:
                return []
            per = {0: range(0, 4), 1: range(4, 8), 2: range(8, 12), 3: range(12, 16),
                   4: range(16, 22), 5: range(22, 28), 6: range(28, 32), 7: ()}[qd]
            return [(b, i // 2, i % 2, b * 32 + i) for i in per]

        QKC = [(0, 0), (1, 0), (2, 0), (0, 1), (1, 1), (0, 2)]
        SCALE = float(DH) ** -0.5

        @block.sync
        def _(sp):
            sp.dma_start(ctx_tok, ctx_in.rearrange("b (t p) d -> p (b t) d", p=P)).then_inc(ld_ctx, 16)
            sp.dma_start(inw, in_proj_w.rearrange("(k p) d -> p k d", p=P)).then_inc(ld_ctx, 16)
            sp.dma_start(xpw, x_proj_w).then_inc(ld_ctx, 16)
            sp.dma_start(dtw, dt_proj_w.rearrange("(k p) r -> p k r", p=P)).then_inc(ld_ctx, 16)
            sp.dma_start(cw, conv_w.rearrange("(k p) o t -> p k (o t)", p=P)).then_inc(ld_ctx, 16)
            sp.dma_start(alog, A_log.rearrange("(k p) n -> p k n", p=P)).then_inc(ld_ctx, 16)
            with nc.allow_non_contiguous_dma(reason="three short vectors"):
                sp.dma_start(cb, conv_b.rearrange("(k p) -> p k", p=P)).then_inc(ld_ctx, 16)
                sp.dma_start(dtb, dt_proj_b.rearrange("(k p) -> p k", p=P)).then_inc(ld_ctx, 16)
                sp.dma_start(dcol, D.rearrange("(k p) -> p k", p=P)).then_inc(ld_ctx, 16)
            sp.dma_start(xres[:, :, :], x.rearrange("b (t p) d -> p (b t) d", p=P)).then_inc(ld_x, 16)
            for n, w in enumerate((wq, wk, wv, wo)):
                sp.dma_start(w_raw[:, n * KT:(n + 1) * KT, :],
                             w.rearrange("(k p) d -> p k d", p=P)).then_inc(ld_w, 16)
            sp.dma_start(relrow, rel_pos.rearrange("(o t) d -> o t d", o=1)).then_inc(ld_misc, 16)
            sp.dma_start(wr_s[:, :, :], Wr.rearrange("(k p) e -> p k e", p=P)).then_inc(ld_misc, 16)
            sp.dma_start(br_s[:, :], br.rearrange("(o e) -> o e", o=1).partition_broadcast(P)
                         if False else br.rearrange("(o e) -> o e", o=1).broadcast_to([P, EXPERTS])
                         ).then_inc(ld_misc, 16)
            sp.wait_ge(diag_ready, 1)
            sp.dma_start(diag_d, diag[:, 0:SPREAD]).then_inc(diag_out, 16)
            sp.wait_ge(diag_out, 16)
            for qt in range(KT):
                sp.dma_start(hankel[:, qt, :],
                             bass.AP(tensor=diag_d.tensor, offset=P * (1 - qt),
                                     ap=[[1, P], [1, SEQ]])).then_inc(hank_in, 16)
            for n, dst in enumerate((qp_d, kp_d)):
                for i in range(3):
                    sp.wait_ge(part_ready, 3 * n + i + 1)
                    sp.dma_start(dst[i].rearrange("(m p) t -> p m t", p=P), parts[i]).then_inc(part_out[i], 16)
            for i in range(3):
                sp.wait_ge(part_out[i], 32)
            sp.wait_ge(ones_rows, 2)

            def load_stack(b, hh):
                for c, (qi, ki) in enumerate(QKC):
                    lo = 64 * hh + DH * c
                    for st, src, i in ((qst, qp_d, qi), (kst, kp_d, ki)):
                        sp.dma_start(st[b % 2][lo:lo + DH, :, :],
                                     src[i][hh * P:(hh + 1) * P, b * SEQ:(b + 1) * SEQ]
                                     .rearrange("(h d) t -> d h t", d=DH)).then_inc(stack_in[b % 2][hh], 16)

            def send_max(b):
                sp.wait_ge(m_ready, b + 1)
                for hh in range(2):
                    sp.dma_start(qst[b % 2][64 * hh + ROWS:64 * hh + ROWS + 1, :, :],
                                 negmT[16 * hh:16 * hh + 16, :]).then_inc(m_in, 16)

            for b in range(2):
                for hh in range(2):
                    load_stack(b, hh)
            send_max(0)
            chunks = [(w, e, k) for w, src in ((wg_s, Wg), (wu_s, Wu)) for e in range(EXPERTS) for k in [src]]
            chunks += [(wd_s, e, Wd) for e in range(EXPERTS)]
            sp.wait_ge(mixer_done, 1)

            def load_weights():
                dst, e, src = chunks.pop(0)
                width = DM if dst is wd_s else DFF
                sp.dma_start(dst[:, :, e * width:(e + 1) * width],
                             src[e].rearrange("(k p) f -> p k f", p=P)).then_inc(w_in, 16)

            for b in range(BATCH):
                for hh in range(2):
                    if b + 2 < BATCH:
                        sp.wait_ge(b_scores, 2 * (QUADS * b + 4 * (hh + 1)))
                        load_stack(b + 2, hh)
                    load_weights()
                if b + 1 < BATCH:
                    send_max(b + 1)
                load_weights()
            sp.wait_ge(x2_full, 1)
            sp.dma_start(x2_d.rearrange("(t p) c -> p t c", p=P), x2).then_inc(x2_out, 16)
            for s in range(SLOTS):
                pass
            sp.wait_ge(out_done, 16 * SLOTS)

        @block.gpsimd
        def _(pool):
            g = nc.gpsimd
            order = [0]

            def link(ins):
                order[0] += 1
                ins.then_inc(pool_order, 1)
                pool.wait_ge(pool_order, order[0])

            link(g.memset(identf[:, :], 0.0))
            g.affine_select(out=identf[:, :], in_=identf[:, :], compare_op=ALU.not_equal, fill=1.0, base=0,
                            pattern=[[-1, P]], channel_multiplier=1).then_inc(consts, 1)
            g.memset(xpB, 0.0)
            g.memset(xpC, 0.0)
            g.memset(xin[:, :, :, 0:PAD], 0.0).then_inc(consts, 1)
            link(g.memset(flip[:, :], 0.0))
            g.affine_select(out=flip[:, :], in_=flip[:, :], compare_op=ALU.not_equal, fill=1.0, base=-(P - 1),
                            pattern=[[1, P]], channel_multiplier=1)
            link(g.memset(sel, 0.0))
            for k in range(3):
                link(g.affine_select(out=sel, in_=sel, compare_op=ALU.not_equal, fill=1.0, base=-32 * k,
                                     pattern=[[-1, STATES], [0, P]], channel_multiplier=1))
            g.memset(vaug[:, :, :, DH:VW], 1.0)
            g.memset(rows_s[:, :, :], 0.0)
            for buf in range(2):
                g.memset(kst[buf], 1.0).then_inc(ones_rows, 1)
            g.memset(rstd[:, :], 0.0).then_inc(consts, 1)
            for n, (src, evac) in enumerate(((q_s, F_Q), (k_s, F_K))):
                wait_evac(pool, evac + 3)
                for i in range(3):
                    if n:
                        pool.wait_ge(part_out[i], 16)
                    g.tensor_copy(parts[i], src).then_inc(part_ready, 1)
                    if i < 2:
                        pool.wait_ge(part_ready, 3 * n + i + 1)
                        link(g.tensor_tensor(src, src, parts[i], ALU.subtract))
            pool.wait_ge(pe_fill, F_B)
            for i in range(4):
                g.memset(prod[i], 0.0).then_inc(prod_ready, 1)
            pool.wait_ge(x1_ready, 1)
            g.iota(thr, pattern=[[P, TT]], base=0, channel_multiplier=0, allow_small_or_imprecise_dtypes=True)
            g.iota(slot_no, pattern=[[1, SLOTS]], base=0, channel_multiplier=0,
                   allow_small_or_imprecise_dtypes=True)
            g.iota(iota16, pattern=[[1, SLOTS * P]], base=0, channel_multiplier=0,
                   allow_small_or_imprecise_dtypes=True)
            g.iota(tokid, pattern=[[P, TT]], base=-FAR, channel_multiplier=1,
                   allow_small_or_imprecise_dtypes=True)
            g.memset(ones32, 1.0)
            g.memset(ones_b, 1.0)
            link(g.memset(ltri, 1.0))
            g.affine_select(out=ltri, in_=ltri, compare_op=ALU.is_gt, fill=0.0, base=0,
                            pattern=[[1, P]], channel_multiplier=-1).then_inc(consts, 1)
            pool.wait_ge(x2_out, 16)
            pool.wait_ge(idx_ready, 1)
            for s in range(SLOTS):
                g.indirect_dma_start(out=rows_s[:, s, :], out_offset=None, in_=x2_d,
                                     in_offset=bass.IndirectOffsetOnAxis(ap=idx[:, s:s + 1], axis=0),
                                     bounds_check=TOK - 1, oob_is_err=False).then_inc(rows_in[s], 16)
            for s in range(SLOTS):
                pool.wait_ge(row_ready, s + 2)
                g.indirect_dma_start(out=out.rearrange("b s d -> (b s) d"),
                                     out_offset=bass.IndirectOffsetOnAxis(ap=idx[:, s:s + 1], axis=0),
                                     in_=rows_s[:, s, 0:DM], in_offset=None,
                                     bounds_check=TOK - 1, oob_is_err=False).then_inc(out_done, 16)

        @block.tensor
        def _(pe):
            mm = nc.tensor.matmul

            def begin(j):
                if j >= 8:
                    wait_evac(pe, j - 8)
                return j % 8

            pe.wait_ge(consts, 1)
            pe.wait_ge(ld_ctx, N_CTX)
            for j in range(2):
                for i in range(4):
                    last = nc.tensor.transpose(ps[:, j, i * P:(i + 1) * P], ctx_tok[:, 4 * j + i, :], identf[:, :])
                last.then_inc(pe_fill, 1)
            R = RANK + 2 * STATES
            for k in range(KT):
                nc.tensor.transpose(ps[:, 2, k * P:(k + 1) * P], inw[:, k, :], identf[:, :])
            for k in range(KT):
                last = nc.tensor.transpose(ps[:, 2, DM + k * R:DM + (k + 1) * R], xpw[:, k * P:(k + 1) * P],
                                           identf[0:R, 0:R])
            last.then_inc(pe_fill, 1)
            for k in range(KT):
                last = nc.tensor.transpose(ps[0:RANK, 3, k * P:(k + 1) * P], dtw[:, k, :], identf[:, :])
            last.then_inc(pe_fill, 1)
            wait_evac(pe, 1)
            wait_evac(pe, F_INW)
            for k in range(KT):
                for hf in range(2):
                    bank = begin(F_XIN + 2 * k + hf)
                    mm(ps[:, bank, :], inwT[:, k * P:(k + 1) * P], ctxT[:, hf * HALF:(hf + 1) * HALF],
                       start=True, stop=True).then_inc(pe_fill, 1)
            pe.wait_ge(ld_x, 16)
            for k in range(KT):
                for hf in range(2):
                    bank = begin(F_XT + 2 * k + hf)
                    for i in range(4):
                        last = nc.tensor.transpose(ps[:, bank, i * P:(i + 1) * P],
                                                   xres[:, 4 * hf + i, k * P:(k + 1) * P], identf[:, :])
                    last.then_inc(pe_fill, 1)
            pe.wait_ge(ld_w, 64)
            for w in range(4):
                bank = begin(F_WT + w)
                for k in range(KT):
                    for o in range(KT):
                        at = k * DM + o * P
                        last = nc.tensor.transpose(ps[:, bank, at:at + P],
                                                   w_raw[:, w * KT + o, k * P:(k + 1) * P], identf[:, :])
                last.then_inc(pe_fill, 1)
            wait_evac(pe, F_WT + 3)
            for w, f in ((0, F_Q), (1, F_K)):
                for m in range(KT):
                    for hf in range(2):
                        bank = begin(f + 2 * m + hf)
                        for k in range(KT):
                            last = mm(ps[:, bank, :], wT[:, w * KT + k, m * P:(m + 1) * P],
                                      xT[:, k, hf * HALF:(hf + 1) * HALF], start=(k == 0), stop=(k == KT - 1))
                        last.then_inc(pe_fill, 1)
            for j in range(4):
                bank = begin(F_V + j)
                for t in range(2):
                    for k in range(KT):
                        last = mm(ps[:, bank, t * DM:(t + 1) * DM], xT[:, k, (2 * j + t) * P:(2 * j + t + 1) * P],
                                  wT[:, 2 * KT + k, :], start=(k == 0), stop=(k == KT - 1))
                last.then_inc(pe_fill, 1)
            pe.wait_ge(u_ready, KT)
            for f, w, rows in ((F_B, xpB, 96), (F_C, xpC, 96), (F_LOW, xpD, RANK)):
                for hf in range(2):
                    bank = begin(f + hf)
                    for k in range(KT):
                        last = mm(ps[0:rows, bank, :], w[:, k, :], u[:, k, hf * HALF:(hf + 1) * HALF],
                                  start=(k == 0), stop=(k == KT - 1))
                    last.then_inc(pe_fill, 1)
            wait_evac(pe, F_LOW + 1)
            for k in range(KT):
                for hf in range(2):
                    bank = begin(F_DT + 2 * k + hf)
                    mm(ps[:, bank, :], dtwT[:, k * P:(k + 1) * P], dtlow[:, hf * HALF:(hf + 1) * HALF],
                       start=True, stop=True).then_inc(pe_fill, 1)
            pe.wait_ge(act_evac, FILLS - 1)
            pe.wait_ge(prod_ready, 4)
            for i in range(4):
                mm(ps[:, i, :], identf[:, :], prod[i], start=True, stop=True,
                   skip_group_check=True).then_inc(y_added, 1)
            pe.wait_ge(split_ready, 1)
            with pe.Fori(0, STATES) as n:
                for hf in range(2):
                    pe.wait_ge(prod_ready, n * 4 + 2 * hf + 2)
                    pe.sem_inc(pe_mark, 1)
                    for i in range(2):
                        last = mm(ps[:, 4 + 2 * i + hf, :], sel[:, bass.ds(n, 1), :].rearrange("r o m -> r (o m)"),
                                  bc3[:, i, hf * HALF:(hf + 1) * HALF], start=True, stop=True)
                    last.then_inc(bc_ready, 1)
                for i in range(4):
                    pe.wait_ge(prod_ready, n * 4 + 4 + i + 1)
                    mm(ps[:, i, :], identf[:, :], prod[i], start=False, stop=True,
                       skip_group_check=True).then_inc(y_added, 1)

            pe.wait_ge(mixer_done, 1)
            pe.wait_ge(hank_ready, 1)

            def scores_a(b, pair, qt, n):
                bank = n % 2
                hh, h0 = pair // 8, 2 * pair % 16
                if n >= 2:
                    pe.wait_ge(a_max, n - 1)
                lo = 64 * hh
                for i in range(2):
                    mm(ps[:, bank, i * SEQ:(i + 1) * SEQ], qst[b % 2][lo:lo + ROWS, h0 + i, qt * P:(qt + 1) * P],
                       kst[b % 2][lo:lo + ROWS, h0 + i, :], start=(i == 0), stop=False, skip_group_check=True)
                mm(ps[:, bank, :].rearrange("p (h k) -> p h k", h=2), flip[:, :],
                   hank_hi[:, qt:qt + 1, :].broadcast_to([P, 2, SEQ]), start=False, stop=True,
                   skip_group_check=True).then_inc(a_scores, 1)

            def scores_b(b, qd, kt):
                n = 2 * (QUADS * b + qd) + kt
                if n >= 2:
                    pe.wait_ge(p_ready, n - 1)
                hh, h0 = qd // 4, 4 * qd % 16
                lo, hi = 64 * hh, 64 * hh + ROWS + 1
                for pr in range(2):
                    bank = 2 + 2 * (n % 2) + pr
                    for i in range(2):
                        h = h0 + 2 * pr + i
                        mm(ps[:, bank, i * SEQ:(i + 1) * SEQ], kst[b % 2][lo:hi, h, kt * P:(kt + 1) * P],
                           qst[b % 2][lo:hi, h, :], start=(i == 0), stop=False, skip_group_check=True)
                    view = ps[:, bank, :].rearrange("p (h q) -> p h q", h=2)
                    for part in (hank_hi, hank_lo):
                        for qt in range(KT):
                            last = mm(view[:, :, qt * P:(qt + 1) * P], part[:, qt, kt * P:(kt + 1) * P],
                                      flip[:, :].rearrange("p (o k) -> p o k", o=1).broadcast_to([P, 2, P]),
                                      start=False, stop=True, skip_group_check=True)
                last.then_inc(b_scores, 1)

            def weigh(b, qd):
                n = QUADS * b + qd
                pe.wait_ge(pv_out, n + 1)
                pe.wait_ge(p_ready, 2 * n + 2)
                for kt in range(KT):
                    for j in range(4):
                        last = mm(ps[32 * j:32 * j + VW, 6, 0:SEQ], vaug[:, 2 * b + kt, 4 * qd + j, :],
                                  prob[2 * (n % 2) + kt][:, j * SEQ:(j + 1) * SEQ],
                                  start=(kt == 0), stop=(kt == KT - 1), skip_group_check=True)
                last.then_inc(pv_done, 1)

            misc = [0]

            def misc_begin():
                if misc[0]:
                    pe.wait_ge(tail_dve, misc[0])
                misc[0] += 1

            def turn_max(b):
                pe.wait_ge(a_max, 32 * (b + 1))
                misc_begin()
                for qt in range(KT):
                    last = nc.tensor.transpose(ps[0:HEADS, 7, qt * P:(qt + 1) * P], negm[b % 2][:, qt, :],
                                               identf[:, :])
                last.then_inc(tail_pe, 1)

            def tail(b, step):
                qt, k = step // 4, step % 4
                if k < 2:
                    pe.wait_ge(pv_out, QUADS * (b + 1) + 1)
                misc_begin()
                if k < 2:
                    for i in range(4):
                        last = nc.tensor.transpose(ps[:, 7, i * P:(i + 1) * P],
                                                   ctxS[b % 2][:, 4 * k + i, qt * P:(qt + 1) * P], identf[:, :])
                elif k == 2:
                    for i in range(KT):
                        last = nc.tensor.transpose(ps[:, 7, i * P:(i + 1) * P], ctxn[:, i * P:(i + 1) * P],
                                                   identf[:, :])
                else:
                    for i in range(KT):
                        last = mm(ps[:, 7, 0:DM], ctxnT[:, i, :], woT[:, i, :], start=(i == 0),
                                  stop=(i == KT - 1))
                last.then_inc(tail_pe, 1)

            for hh in range(2):
                pe.wait_ge(stack_in[0][hh], 16 * 12)
                for unit in [u_ for qd in range(QUADS) for u_ in a_units(0, qd) if u_[1] // 8 == hh]:
                    scores_a(*unit)
            turn_max(0)
            for b in range(BATCH):
                pe.wait_ge(m_in, 32 * (b + 1))
                for qd in range(QUADS):
                    if qd in (0, 4) and b + 1 < BATCH:
                        pe.wait_ge(stack_in[(b + 1) % 2][qd // 4], 16 * 12 * ((b + 1) // 2 + 1))
                    for unit in a_units(b + 1, qd):
                        scores_a(*unit)
                    for kt in range(KT):
                        scores_b(b, qd, kt)
                    if qd == 7 and b + 1 < BATCH:
                        turn_max(b + 1)
                    if b or qd:
                        weigh(b - (qd == 0), (qd - 1) % QUADS)
                    if b and qd >= 1:
                        for step in ([qd - 1] if qd < 7 else [6, 7]):
                            tail(b - 1, step)
            weigh(BATCH - 1, QUADS - 1)
            for step in range(8):
                tail(BATCH - 1, step)

            pe.wait_ge(gated_ready, 1)
            for j in range(4):
                for i in range(4):
                    t, k = 2 * j + i // 2, i % 2
                    b, lt = t // 2, t % 2
                    last = nc.tensor.transpose(ps[:, j, i * P:(i + 1) * P],
                                               gated[:, k * BATCH + b, lt * P:(lt + 1) * P], identf[:, :])
                last.then_inc(back_pe, 1)

            pe.wait_ge(x2_ready, 1)
            for j in range(4):
                for i in range(4):
                    t = 4 * (j % 2) + i
                    last = nc.tensor.transpose(ps[:, j, i * P:(i + 1) * P],
                                               x2[:, t, (j // 2) * P:(j // 2 + 1) * P], identf[:, :])
                last.then_inc(x2t_pe, 1)
            pe.wait_ge(x2t_out, 4)
            for t in range(TT):
                for k in range(KT):
                    last = mm(ps[:, 4, t * EXPERTS:(t + 1) * EXPERTS], x2T[:, k, t * P:(t + 1) * P], wr_s[:, k, :],
                              start=(k == 0), stop=(k == KT - 1))
            last.then_inc(logit_pe, 1)
            pe.wait_ge(oh_ready, 1)
            pe.wait_ge(consts, 4)
            oh_cols = ohb.rearrange("p e t -> p (e t)")
            mm(ps[:, 5, 0:EXPERTS * TT], ltri, oh_cols, start=True, stop=True)
            mm(ps[:, 6, 0:EXPERTS * TT], ones_b, oh_cols, start=True, stop=True).then_inc(count_pe, 1)
            pe.wait_ge(hot_ready, TT)
            for s in range(SLOTS):
                for t in range(TT):
                    last = mm(ps[:, 7, s:s + 1], onehot[t][:, s * P:(s + 1) * P], tokid[:, t:t + 1],
                              start=(t == 0), stop=(t == TT - 1))
            last.then_inc(idx_pe, 1)
            for j in range(2 * ((SLOTS + 3) // 4)):
                k, s0 = j % 2, 4 * (j // 2)
                for i in range(min(4, SLOTS - s0)):
                    pe.wait_ge(rows_in[s0 + i], 16)
                    last = nc.tensor.transpose(ps[:, j, i * P:(i + 1) * P],
                                               rows_s[:, s0 + i, k * P:(k + 1) * P], identf[:, :])
                last.then_inc(xs_pe, 1)
            pe.wait_ge(xs_out, 6)
            pe.wait_ge(w_in, 16 * 12)

            def gate_up(s, e):
                pe.wait_ge(xcur_ready, s + 1)
                for w, b0 in ((wg_s, 0), (wu_s, 2)):
                    for fh in range(2):
                        for k in range(KT):
                            last = mm(ps[:, b0 + fh, :], xcur[:, k, :],
                                      w[:, k, bass.ds(e * DFF + fh * HALF, HALF)], start=(k == 0), stop=(k == KT - 1))
                last.then_inc(gu_done, 1)

            def turn_h(s):
                pe.wait_ge(h_ready, s + 1)
                for f in range(FT):
                    last = nc.tensor.transpose(ps[:, 4 + f // 4, (f % 4) * P:(f % 4 + 1) * P],
                                               hcur[:, f * P:(f + 1) * P], identf[:, :])
                last.then_inc(ht_pe, 1)

            def down(s, e):
                pe.wait_ge(ht_ready, s + 1)
                pe.wait_ge(z_ready, s + 1)
                for f in range(FT):
                    last = mm(ps[:, 6, 0:DM], hT[:, f, :], wd_s[:, f, bass.ds(e * DM, DM)], start=(f == 0),
                              stop=(f == FT - 1))
                last.then_inc(y_done, 1)

            def expert_of(s):
                return pe.value_load(e_int[0:1, bass.ds(s, 1)], min_val=0, max_val=EXPERTS - 1)

            gate_up(0, expert_of(0))
            turn_h(0)
            with pe.Fori(1, SLOTS) as s:
                gate_up(s, expert_of(s))
                down(s - 1, expert_of(s - 1))
                turn_h(s)
            down(SLOTS - 1, expert_of(SLOTS - 1))

        @block.scalar
        def _(act):
            A = nc.scalar.activation

            def filled(j):
                act.wait_ge(pe_fill, j + 1)
                return j % 8

            for j in range(2):
                bank = filled(F_CTX + j)
                A(ctxT[:, j * HALF:(j + 1) * HALF], ps[:, bank, :], ACT.Copy).then_inc(act_evac, 1)
            bank = filled(F_DTW)
            A(dtwT, ps[0:RANK, bank, 0:DM], ACT.Copy).then_inc(act_evac, 1)
            act.wait_ge(consts, 2)
            for k in range(KT):
                for hf in range(2):
                    bank = filled(F_XIN + 2 * k + hf)
                    A(xin[:, k, 2 * hf:2 * hf + 2, PAD:PB], ps[:, bank, :].rearrange("p (b l) -> p b l", b=2),
                      ACT.Copy).then_inc(act_evac, 1)
            for k in range(KT):
                for hf in range(2):
                    bank = filled(F_XT + 2 * k + hf)
                    A(xT[:, k, hf * HALF:(hf + 1) * HALF], ps[:, bank, :], ACT.Copy).then_inc(act_evac, 1)
            for w in range(4):
                bank = filled(F_WT + w)
                dst = wT[:, w * KT:(w + 1) * KT, :] if w < 3 else woT[:, :, :]
                A(dst.rearrange("p k o -> p (k o)"), ps[:, bank, :], ACT.Copy).then_inc(act_evac, 1)
            for k in range(KT):
                act.wait_ge(conv_done, k + 1)
                A(u[:, k, :], ta[:, k, :], ACT.Silu).then_inc(u_ready, 1)
            for f, dst, sc in ((F_Q, q_s, SCALE), (F_K, k_s, 1.0)):
                for m in range(KT):
                    for hf in range(2):
                        bank = filled(f + 2 * m + hf)
                        A(dst[:, m, hf * HALF:(hf + 1) * HALF], ps[:, bank, :], ACT.Copy,
                          scale=sc).then_inc(act_evac, 1)
            for j in range(4):
                bank = filled(F_V + j)
                A(vaug[:, 2 * j:2 * j + 2, :, 0:DH].rearrange("p t h d -> p (t h) d"),
                  ps[:, bank, :].rearrange("p (h d) -> p h d", d=DH), ACT.Copy).then_inc(act_evac, 1)
            act.wait_ge(u_ready, KT)
            for i, f in enumerate((F_B, F_C)):
                for hf in range(2):
                    bank = filled(f + hf)
                    A(ta[0:96, i, hf * HALF:(hf + 1) * HALF], ps[0:96, bank, :], ACT.Copy).then_inc(act_evac, 1)
            for hf in range(2):
                bank = filled(F_LOW + hf)
                A(dtlow[:, hf * HALF:(hf + 1) * HALF], ps[0:RANK, bank, :], ACT.Copy).then_inc(act_evac, 1)
            for k in range(KT):
                for hf in range(2):
                    bank = filled(F_DT + 2 * k + hf)
                    cols = slice(hf * HALF, (hf + 1) * HALF)
                    A(spt[:, k, cols], ps[:, bank, :], ACT.Abs, bias=dtb[:, k:k + 1]).then_inc(act_order, 1)
                    A(dts[:, k, cols], ps[:, bank, :], ACT.Relu, bias=dtb[:, k:k + 1]).then_inc(act_evac, 1)
            A(acol, alog, ACT.Exp).then_inc(a_exp, 1)
            act.wait_ge(act_order, 4)
            for k in range(KT):
                A(spt[:, k, :], spt[:, k, :], ACT.Exp, scale=-1.0).then_inc(sp_exp, 1)
            act.wait_ge(scan_in, 1)
            with act.Fori(0, STATES) as n:
                for i in range(4):
                    hf, k = i // 2, i % 2
                    act.wait_ge(scanned, n * 4 + i + 1)
                    act.sem_inc(act_mark, 1)
                    dt3 = dts[:, k, :].rearrange("p (b l) -> p b l", b=BATCH)
                    A(dA[i][:, :, 1:SEQ], dt3[:, 2 * hf:2 * hf + 2, 1:SEQ], ACT.Exp,
                      scale=acol[:, k, bass.ds(n, 1)]).then_inc(da_ready, 1)

            act.wait_ge(mixer_done, 1)
            for n in range(2 * QUADS * BATCH):
                act.wait_ge(b_scores, n + 1)
                if n >= 4:
                    act.wait_ge(pv_done, n // 2 - 1)
                b0 = 2 + 2 * (n % 2)
                A(prob[n % 4], ps[:, b0:b0 + 2, :].rearrange("p b c -> p (b c)"), ACT.Exp).then_inc(p_ready, 1)

            act.wait_ge(x1_ready, 1)
            A(sg, xres[:, :, :], ACT.Silu).then_inc(sg_ready, 1)
            for j in range(4):
                act.wait_ge(x2t_pe, j + 1)
                A(x2T[:, j // 2, (j % 2) * HALF:(j % 2 + 1) * HALF], ps[:, j, :], ACT.Copy).then_inc(x2t_out, 1)
            act.wait_ge(logit_dve, 1)
            A(ex, lg, ACT.Exp).then_inc(gate_exp, 1)
            for j in range(2 * ((SLOTS + 3) // 4)):
                k, s0 = j % 2, 4 * (j // 2)
                w = min(4, SLOTS - s0) * P
                act.wait_ge(xs_pe, j + 1)
                A(xsT[:, k, s0 * P:s0 * P + w], ps[:, j, 0:w], ACT.Copy).then_inc(xs_out, 1)
            act.wait_ge(xs_out, 6)

            def take_x(s):
                A(xcur, xsT[:, :, bass.ds(s * P, P)], ACT.Copy).then_inc(xcur_ready, 1)

            def silu_gate(s):
                act.wait_ge(gu_done, s + 1)
                A(ge, ps[:, 0:2, :].rearrange("p b c -> p (b c)"), ACT.Silu).then_inc(ge_ready, 1)

            def put_hT(s):
                act.wait_ge(ht_pe, s + 1)
                A(hT.rearrange("p f t -> p (f t)"), ps[:, 4:6, :].rearrange("p b c -> p (b c)"),
                  ACT.Copy).then_inc(ht_ready, 1)

            take_x(0)
            silu_gate(0)
            act.wait_ge(gu_done, 1)
            act.sem_inc(act_mark, 1)
            take_x(1)
            put_hT(0)
            with act.Fori(1, SLOTS - 1) as s:
                silu_gate(s)
                act.wait_ge(gu_done, s + 1)
                act.sem_inc(act_mark, 1)
                take_x(s + 1)
                put_hT(s)
            silu_gate(SLOTS - 1)
            put_hT(SLOTS - 1)

        @block.vector
        def _(dve):
            v = nc.vector
            order = [0]

            def link(ins):
                order[0] += 1
                ins.then_inc(dve_order, 1)
                dve.wait_ge(dve_order, order[0])

            R = RANK + 2 * STATES
            dve.wait_ge(consts, 2)
            dve.wait_ge(pe_fill, F_INW + 1)
            xpt = ps[:, 2, DM:DM + KT * R].rearrange("p (k r) -> p k r", k=KT)
            v.tensor_copy(inwT, ps[:, 2, 0:DM])
            for c in range(3):
                v.tensor_copy(xpB[:, :, 32 * c:32 * c + STATES], xpt[:, :, RANK:RANK + STATES])
                v.tensor_copy(xpC[:, :, 32 * c:32 * c + STATES], xpt[:, :, RANK + STATES:R])
            v.tensor_copy(xpD, xpt[:, :, 0:RANK]).then_inc(dve_evac, 1)
            dve.wait_ge(ld_misc, 48)
            mid = diag[:, SEQ - 64:SEQ - 64 + TABLE]
            link(v.tensor_reduce(mid, relrow, axis=AX.X, op=ALU.add))
            link(v.tensor_scalar_mul(mid, mid, 1.0 / DH))
            lo = SEQ - 64
            v.tensor_copy(diag[:, 0:lo], diag[:, lo:lo + 1].broadcast_to([1, lo]))
            link(v.tensor_copy(diag[:, lo + TABLE:SPREAD],
                               diag[:, lo + TABLE - 1:lo + TABLE].broadcast_to([1, SPREAD - lo - TABLE])))
            v.tensor_copy(diag[:, SPREAD:SPREAD + 1], diag[:, 0:1]).then_inc(diag_ready, 1)
            for k in range(KT):
                dve.wait_ge(act_evac, F_XIN + 2 * k + 1)
                o = ta[:, k, :].rearrange("p (b l) -> p b l", b=BATCH)
                link(v.tensor_scalar(o, xin[:, k, :, PAD:PB], cw[:, k, PAD:TAPS], cb[:, k:k + 1], ALU.mult, ALU.add))
                for j in range(PAD):
                    ins = v.scalar_tensor_tensor(out=o, in0=xin[:, k, :, j:j + SEQ], scalar=cw[:, k, j:j + 1],
                                                 in1=o, op0=ALU.mult, op1=ALU.add)
                    if j < PAD - 1:
                        link(ins)
                    else:
                        ins.then_inc(conv_done, 1)
            dve.wait_ge(hank_in, 32)
            link(v.tensor_copy(hank_hi[:, :, :], hankel[:, :, :]))
            v.tensor_tensor(hank_lo[:, :, :], hankel[:, :, :], hank_hi[:, :, :],
                            ALU.subtract).then_inc(hank_ready, 1)
            dve.wait_ge(act_evac, F_C + 1)
            both = ta[0:96, :, :]
            link(v.tensor_copy(bct[0], both))
            v.tensor_copy(bc3[0:32, :, :], bct[0][0:32, :, :])
            link(v.tensor_tensor(both, both, bct[0], ALU.subtract))
            link(v.tensor_copy(bct[1], both))
            v.tensor_copy(bc3[32:64, :, :], bct[1][32:64, :, :])
            link(v.tensor_tensor(both, both, bct[1], ALU.subtract))
            link(v.tensor_copy(bc3[64:96, :, :], ta[64:96, :, :]))
            dve.sem_inc(split_ready, 1)
            dve.wait_ge(a_exp, 1)
            v.tensor_scalar_mul(acol, acol, -1.0)
            dve.wait_ge(act_evac, FILLS - 1)
            for k in range(KT):
                dve.wait_ge(sp_exp, k + 1)
                link(v.tensor_scalar_mul(tb[:, k, :], spt[:, k, :], LOG1P[-1]))
                for c in LOG1P[-2::-1]:
                    link(v.scalar_tensor_tensor(out=tb[:, k, :], in0=tb[:, k, :], scalar=c, in1=spt[:, k, :],
                                                op0=ALU.add, op1=ALU.mult))
                link(v.tensor_tensor(dts[:, k, :], dts[:, k, :], tb[:, k, :], ALU.add))
            dtu = ta
            link(v.tensor_tensor(dtu, dts, u, ALU.mult))
            for i in range(4):
                v.memset(dA[i][:, :, 0:1], 0.0).then_inc(scanned, 1)
            dve.sem_inc(scan_in, 1)
            with dve.Fori(0, STATES) as n:
                for hf in range(2):
                    cols = slice(hf * HALF, (hf + 1) * HALF)
                    dve.wait_ge(bc_ready, n * 2 + hf + 1)
                    for k in range(KT):
                        v.tensor_tensor(dBu[k], dtu[:, k, cols], ps[:, 4 + hf, :], ALU.mult).then_inc(dbu_ready, 1)
                    for k in range(KT):
                        i = 2 * hf + k
                        dve.wait_ge(dbu_ready, n * 4 + i + 1)
                        dve.wait_ge(da_ready, n * 4 + i + 1)
                        v.tensor_tensor_scan(out=hst[k], data0=dA[i].rearrange("p b l -> p (b l)"), data1=dBu[k],
                                             initial=0.0, op0=ALU.mult, op1=ALU.add).then_inc(scanned, 1)
                    for k in range(KT):
                        i = 2 * hf + k
                        dve.wait_ge(scanned, n * 4 + 4 + i + 1)
                        dve.wait_ge(y_added, n * 4 + i + 1)
                        v.tensor_tensor(prod[i], hst[k], ps[:, 6 + hf, :], ALU.mult).then_inc(prod_ready, 1)
            dve.wait_ge(y_added, 4 * STATES + 4)
            for i in range(4):
                hf, k = i // 2, i % 2
                cols = slice(hf * HALF, (hf + 1) * HALF)
                link(v.scalar_tensor_tensor(out=yT[:, k, cols], in0=u[:, k, cols], scalar=dcol[:, k:k + 1],
                                            in1=ps[:, i, :], op0=ALU.mult, op1=ALU.add))
            link(v.memset(ps[:, 6, :], 0.0))
            dve.sem_inc(pv_out, 1)
            dve.sem_inc(mixer_done, 1)

            def maxima(b, pair, qt, n):
                dve.wait_ge(a_scores, n + 1)
                v.tensor_reduce(negm[b % 2][:, qt, 2 * pair:2 * pair + 2],
                                ps[:, n % 2, :].rearrange("p (h k) -> p h k", h=2), axis=AX.X,
                                op=ALU.max).then_inc(a_max, 1)

            def copy_context(b, qd):
                n = QUADS * b + qd
                dve.wait_ge(pv_done, n + 1)
                if qd == 0 and b:
                    pass
                v.tensor_copy(ctxS[b % 2][:, qd, :], ps[:, 6, 0:SEQ]).then_inc(pv_out, 1)

            misc = [0]

            def misc_filled():
                misc[0] += 1
                dve.wait_ge(tail_pe, misc[0])

            def put_max(b):
                misc_filled()
                if b:
                    dve.wait_ge(m_in, 32 * b)
                link(v.tensor_scalar_mul(negmT, ps[0:HEADS, 7, 0:SEQ], -1.0))
                dve.sem_inc(m_ready, 1)
                dve.sem_inc(tail_dve, 1)

            def tail(b, step):
                qt, k = step // 4, step % 4
                misc_filled()
                if k < 2:
                    quad = ps[:, 7, :].rearrange("p (h c) -> p h c", c=32)
                    link(v.reciprocal(rcp.rearrange("p (h o) -> p h o", o=1), quad[:, :, DH:VW]))
                    v.tensor_tensor(ctxn[:, k * P:(k + 1) * P].rearrange("p (h d) -> p h d", d=DH),
                                    quad[:, :, 0:DH],
                                    rcp.rearrange("p (h o) -> p h o", o=1).broadcast_to([P, 16, DH]),
                                    ALU.mult).then_inc(tail_dve, 1)
                elif k == 2:
                    v.tensor_copy(ctxnT.rearrange("p k t -> p (k t)"), ps[:, 7, 0:DM]).then_inc(tail_dve, 1)
                else:
                    t = 2 * b + qt
                    v.tensor_tensor(xres[:, t, :], xres[:, t, :], ps[:, 7, 0:DM], ALU.add).then_inc(tail_dve, 1)
                    dve.wait_ge(tail_dve, misc[0])
                    link(v.bn_stats(stats[:, t, :], xres[:, t, :]))
                    link(v.bn_aggr(mv[:, t, :], stats[:, t, :]))

            for qd in range(QUADS):
                for unit in a_units(0, qd):
                    maxima(*unit)
            put_max(0)
            for b in range(BATCH):
                for qd in range(QUADS):
                    for unit in a_units(b + 1, qd):
                        maxima(*unit)
                    if qd == 7 and b + 1 < BATCH:
                        put_max(b + 1)
                    if b or qd:
                        copy_context(b - (qd == 0), (qd - 1) % QUADS)
                    if b and qd >= 1:
                        for step in ([qd - 1] if qd < 7 else [6, 7]):
                            tail(b - 1, step)
            copy_context(BATCH - 1, QUADS - 1)
            for step in range(8):
                tail(BATCH - 1, step)

            def inverse_root():
                link(v.tensor_scalar_add(veps[:, :], mv[:, :, 1], EPS))
                link(v.tensor_scalar(rstd[:, :].bitcast(I32), veps[:, :].bitcast(I32), 1, None,
                                     ALU.logical_shift_right))
                link(v.tensor_scalar(rstd[:, :].bitcast(I32), rstd[:, :].bitcast(I32), -1.0, float(RSQRT_SEED),
                                     ALU.mult, ALU.add))
                link(v.tensor_scalar_mul(veps[:, :], veps[:, :], -0.5))
                for _ in range(3):
                    link(v.tensor_tensor(nwt[:, :], rstd[:, :], rstd[:, :], ALU.mult))
                    link(v.tensor_tensor(nwt[:, :], nwt[:, :], veps[:, :], ALU.mult))
                    link(v.scalar_tensor_tensor(out=rstd[:, :], in0=nwt[:, :], scalar=1.5, in1=rstd[:, :],
                                                op0=ALU.add, op1=ALU.mult))

            def normalise(dst):
                inverse_root()
                for t in range(TT):
                    link(v.tensor_scalar(dst(t), xres[:, t, :], mv[:, t, 0:1], rstd[:, t:t + 1], ALU.subtract,
                                         ALU.mult))

            normalise(lambda t: xres[:, t, :])
            dve.sem_inc(x1_ready, 1)
            dve.wait_ge(sg_ready, 1)
            for k in range(KT):
                ins = v.tensor_tensor(gated[:, k * BATCH:(k + 1) * BATCH, :],
                                      sg.rearrange("p (b k) l -> p k b l", k=KT)[:, k],
                                      yT[:, k, :].rearrange("p (b l) -> p b l", b=BATCH), ALU.mult)
                link(ins)
            dve.sem_inc(gated_ready, 1)
            for j in range(4):
                dve.wait_ge(back_pe, j + 1)
                link(v.tensor_tensor(xres[:, 2 * j:2 * j + 2, :].rearrange("p t d -> p (t d)"),
                                     xres[:, 2 * j:2 * j + 2, :].rearrange("p t d -> p (t d)"), ps[:, j, :],
                                     ALU.add))
                for t in (2 * j, 2 * j + 1):
                    v.bn_stats(stats[:, t, :], xres[:, t, :])
                link(v.memset(nwt[:, 0:1], 0.0))
                for t in (2 * j, 2 * j + 1):
                    link(v.bn_aggr(mv[:, t, :], stats[:, t, :]))
            link(v.memset(x2, 0.0))
            normalise(lambda t: x2[:, t, 0:DM])
            dve.sem_inc(x2_ready, 1)

            dve.wait_ge(logit_pe, 1)
            link(v.tensor_tensor(lg, ps[:, 4, 0:TT * EXPERTS].rearrange("p (t e) -> p t e", e=EXPERTS),
                                 br_s[:, :].rearrange("p (o e) -> p o e", o=1).broadcast_to([P, TT, EXPERTS]),
                                 ALU.add))
            link(v.tensor_reduce(lmax, lg, axis=AX.X, op=ALU.max))
            lmax3 = lmax.rearrange("p (t o) -> p t o", o=1).broadcast_to([P, TT, EXPERTS])
            link(v.tensor_tensor(oh, lg, lmax3, ALU.is_ge))
            link(v.tensor_tensor(lg, lg, lmax3, ALU.subtract))
            link(v.tensor_copy(run, oh[:, :, 0]))
            v.tensor_copy(ohb[:, 0, :], oh[:, :, 0]).then_inc(logit_dve, 1)
            for e in range(1, EXPERTS):
                link(v.tensor_tensor(ohb[:, e, :], oh[:, :, e], run, ALU.is_gt))
                link(v.tensor_tensor(run, run, oh[:, :, e], ALU.max))
            dve.sem_inc(oh_ready, 1)
            dve.wait_ge(gate_exp, 1)
            link(v.tensor_reduce(lsum, ex, axis=AX.X, op=ALU.add))
            link(v.reciprocal(gate_w, lsum))
            link(v.tensor_copy(x2[:, :, DM:DM + 1], gate_w.rearrange("p (t o) -> p t o", o=1)))
            dve.sem_inc(x2_full, 1)
            dve.wait_ge(count_pe, 1)
            dve.wait_ge(consts, 4)
            v.tensor_copy(within.rearrange("p e t -> p (e t)"), ps[:, 5, 0:EXPERTS * TT])
            link(v.tensor_copy(total.rearrange("p e t -> p (e t)"), ps[:, 6, 0:EXPERTS * TT]))
            for e in range(EXPERTS):
                link(v.tensor_tensor_scan(out=incl[:, e, :], data0=ones32[:, 0:TT], data1=total[:, e, :],
                                          initial=0.0, op0=ALU.mult, op1=ALU.add))
            link(v.tensor_tensor(over, incl[:, :, TT - 1:TT].broadcast_to([P, EXPERTS, TT]),
                                 thr.rearrange("p (o t) -> p o t", o=1).broadcast_to([P, EXPERTS, TT]), ALU.is_gt))
            link(v.tensor_reduce(ntile, over, axis=AX.X, op=ALU.add))
            link(v.tensor_tensor_scan(out=tile_incl, data0=ones32[:, 0:EXPERTS], data1=ntile, initial=0.0,
                                      op0=ALU.mult, op1=ALU.add))
            link(v.tensor_tensor(tile0, tile_incl, ntile, ALU.subtract))
            link(v.tensor_tensor(within, within, incl, ALU.add))
            link(v.tensor_tensor(within, within, total, ALU.subtract))
            link(v.scalar_tensor_tensor(out=within, in0=tile0.rearrange("p (e o) -> p e o", o=1)
                                        .broadcast_to([P, EXPERTS, TT]), scalar=float(P), in1=within,
                                        op0=ALU.mult, op1=ALU.add))
            link(v.tensor_tensor(within, within, ohb, ALU.mult))
            link(v.tensor_reduce(pos, within.rearrange("p e t -> p t e"), axis=AX.X, op=ALU.add))
            for t in range(TT):
                v.tensor_scalar(onehot[t], iota16, pos[:, t:t + 1], None, ALU.is_equal).then_inc(hot_ready, 1)
            link(v.tensor_scalar(e_of, slot_no, tile0[:, 1:2], None, ALU.is_ge))
            for e in range(2, EXPERTS):
                link(v.scalar_tensor_tensor(out=e_of, in0=slot_no, scalar=tile0[:, e:e + 1], in1=e_of,
                                            op0=ALU.is_ge, op1=ALU.add))
            link(v.tensor_copy(e_int, e_of))
            dve.wait_ge(idx_pe, 1)
            link(v.tensor_scalar_add(idx, ps[:, 7, 0:SLOTS], float(FAR)))
            dve.sem_inc(idx_ready, 1)

            def make_h(s):
                dve.wait_ge(ge_ready, s + 1)
                v.tensor_tensor(hcur, ge, ps[:, 2:4, :].rearrange("p b c -> p (b c)"), ALU.mult).then_inc(h_ready, 1)

            def finish_rows(s):
                row = rows_s[:, bass.ds(s, 1), 0:DM].rearrange("p o d -> p (o d)")
                gate = rows_s[:, bass.ds(s, 1), DM:DM + 1].rearrange("p o d -> p (o d)")
                at = [ROW_STEPS * s]

                def step(ins):
                    at[0] = at[0] + 1
                    ins.then_inc(row_order, 1)
                    dve.wait_ge(row_order, at[0])

                dve.wait_ge(row_ready, s + 1)
                dve.wait_ge(y_done, s + 1)
                step(v.scalar_tensor_tensor(out=zrow, in0=ps[:, 6, 0:DM], scalar=gate, in1=row, op0=ALU.mult,
                                            op1=ALU.add))
                step(v.bn_stats(stats[:, 0, :], zrow))
                dve.sem_inc(dve_mark, 1)
                step(v.bn_aggr(mv[:, 0, :], stats[:, 0, :]))
                dve.sem_inc(z_ready, 1)
                step(v.tensor_scalar_add(ve, mv[:, 0, 1:2], EPS))
                step(v.tensor_scalar(rs.bitcast(I32), ve.bitcast(I32), 1, None, ALU.logical_shift_right))
                step(v.tensor_scalar(rs.bitcast(I32), rs.bitcast(I32), -1.0, float(RSQRT_SEED), ALU.mult, ALU.add))
                step(v.tensor_scalar_mul(ve, ve, -0.5))
                for _ in range(3):
                    step(v.scalar_tensor_tensor(out=nw, in0=rs, scalar=ve, in1=rs, op0=ALU.mult, op1=ALU.mult))
                    step(v.scalar_tensor_tensor(out=rs, in0=nw, scalar=1.5, in1=rs, op0=ALU.add, op1=ALU.mult))
                v.tensor_scalar(row, zrow, mv[:, 0, 0:1], rs, ALU.subtract, ALU.mult).then_inc(row_ready, 1)

            dve.sem_inc(row_ready, 1)
            dve.sem_inc(z_ready, 1)
            ve, rs, nw = veps[:, 0:1], rstd[:, 0:1], nwt[:, 0:1]
            ROW_STEPS = 13
            make_h(0)
            with dve.Fori(1, SLOTS) as s:
                make_h(s)
                finish_rows(s - 1)
            finish_rows(SLOTS - 1)


_INS = ["x", "ctx_1024", "L0_attn_wq", "L0_attn_wk", "L0_attn_wv", "L0_attn_wo", "L0_attn_rel_pos",
        "L0_xattn_in_proj_w", "L0_xattn_conv_w", "L0_xattn_conv_b", "L0_xattn_x_proj_w", "L0_xattn_dt_proj_w",
        "L0_xattn_dt_proj_b", "L0_xattn_A_log", "L0_xattn_D", "L0_ffn_Wr", "L0_ffn_br", "L0_ffn_Wg", "L0_ffn_Wu",
        "L0_ffn_Wd"]


def kernel(**inputs):
    import numpy as _np
    import concourse.bacc as _bacc
    from concourse.bass_utils import run_bass_kernel_spmd as _run

    nc = _bacc.Bacc("TRN2", target_bir_lowering=False, num_devices=1)
    arrays, args = {}, []
    for name in _INS:
        a = _np.ascontiguousarray(inputs[name])
        arrays[f"in_{name}"] = a
        args.append(nc.dram_tensor(f"in_{name}", a.shape, mybir.dt.from_np(a.dtype), kind="ExternalInput").ap())
    args.append(nc.dram_tensor("out_0", (BATCH, SEQ, DM), F32, kind="ExternalOutput").ap())
    decoder_layer(nc, *args)
    r = _run(nc, [arrays], core_ids=[0])
    return r.results[0]["out_0"]
```

```python
from contextlib import ExitStack

import concourse.bass as bass
from concourse import mybir

F32 = mybir.dt.float32
BF16 = mybir.dt.bfloat16
F16 = mybir.dt.float16
I32 = mybir.dt.int32
U32 = mybir.dt.uint32
ALU = mybir.AluOpType
ACT = mybir.ActivationFunctionType
AX = mybir.AxisListType

P = 128
BATCH, SEQ, DM = 4, 256, 256
TOK = BATCH * SEQ
TT = TOK // P
KT = DM // P
HEADS, DH = 32, 8
HALF = 512
DC = 128
STATES, TAPS, RANK = 16, 4, 8
PAD = TAPS - 1
PB = PAD + SEQ
TABLE = 127
ROWS = 6 * DH
QUADS = HEADS // 4
VW = DH + 1
SPREAD = 2 * SEQ - 1
EXPERTS, DFF = 4, 1024
FT = DFF // P
SLOTS = TT + EXPERTS - 1
EPS = 1e-5
LOG1P = [1.0, -0.499998927, 0.333297104, -0.249516159, 0.196632743, -0.152696669, 0.105436236, -0.0563736148,
         0.0195425283, -0.00317605701]
RSQRT_SEED = 0x5F3759DF
XW = DM + 4
FAR = 2048


def decoder_layer(nc, x, ctx_in, wq, wk, wv, wo, rel_pos, in_proj_w, conv_w, conv_b, x_proj_w, dt_proj_w,
                  dt_proj_b, A_log, D, Wr, br, Wg, Wu, Wd, out):
    with ExitStack() as stack:
        def sb(name, shape, dt=F32):
            return stack.enter_context(nc.sbuf_tensor(name, shape, dt))

        def sem(name):
            return stack.enter_context(nc.semaphore(name))

        def dram(name, shape, dt):
            return nc.dram_tensor(name, shape, dt, kind="Internal").ap()

        diag_d = dram("diag_d", (1, SPREAD), F32)
        qp_d = [dram(f"qp{i}_d", (DM, TOK), BF16) for i in range(3)]
        kp_d = [dram(f"kp{i}_d", (DM, TOK), BF16) for i in range(3)]
        x2_d = dram("x2_d", (TOK, XW), F32)

        xres = sb("xres", [P, TT, DM])
        identf = sb("identf", [P, P])
        flip = sb("flip", [P, P], F16)
        woT = sb("woT", [P, KT, DM])
        vaug = sb("vaug", [P, TT, HEADS, VW])
        hankel = sb("hankel", [P, KT, SEQ])
        hank_hi = sb("hank_hi", [P, KT, SEQ], F16)
        hank_lo = sb("hank_lo", [P, KT, SEQ], F16)
        yT = sb("yT", [P, KT, TOK])
        wr_s = sb("wr_s", [P, KT, EXPERTS])
        br_s = sb("br_s", [P, EXPERTS])
        stats = sb("stats", [P, TT, 6])
        mv = sb("mv", [P, TT, 2])
        rstd = sb("rstd", [P, TT])
        nwt = sb("nwt", [P, TT])
        veps = sb("veps", [P, TT])
        ARENA = 41 * 1024
        arena = sb("arena", [P, ARENA])
        top = [0]

        def carve(cols, *shape, dt=F32, rows=P):
            a = arena[0:rows, top[0]:top[0] + cols]
            top[0] += cols
            assert top[0] <= ARENA, top[0]
            if dt != F32:
                a = a.bitcast(dt)
            if len(shape) == 2:
                a = a.rearrange("p (a b) -> p a b", a=shape[0])
            if len(shape) == 3:
                a = a.rearrange("p (a b c) -> p a b c", a=shape[0], b=shape[1])
            return a

        stacks = [carve(HEADS // 2 * SEQ // 2, HEADS // 2, SEQ, dt=BF16) for _ in range(4)]
        qst, kst = stacks[0::2], stacks[1::2]
        stacks_top = top[0]
        prob = [carve(4 * SEQ) for _ in range(4)]
        ctxS = [carve(QUADS * SEQ, QUADS, SEQ) for _ in range(2)]
        ctxn = carve(DM)
        ctxnT = carve(KT * P, KT, P)
        negm = [carve(2 * HEADS, 2, HEADS) for _ in range(2)]
        negmT = carve(SEQ // 2, dt=BF16, rows=HEADS)
        rcp = carve(16)
        acol = carve(KT * STATES, KT, STATES)
        weights_at = stacks_top + 4096 + 4096 + 1024
        assert top[0] <= weights_at
        top[0] = weights_at
        wg_s = carve(EXPERTS * KT * DFF)
        wu_s = carve(EXPERTS * KT * DFF)
        wd_s = carve(EXPERTS * FT * DM)
        weights_end = top[0]
        late_at = weights_at + EXPERTS * KT * DFF + 2 * KT * DFF
        top[0] = late_at
        dts = carve(KT * TOK, KT, TOK)
        dtu_at = top[0]
        dtu = carve(KT * TOK, KT, TOK)
        bc3 = carve(TOK, 2, TOK, dt=BF16, rows=96)
        sel = carve(STATES * P // 2, STATES, P, dt=BF16, rows=96)
        tiles_at = top[0]
        dA = [carve(HALF, KT, SEQ) for _ in range(4)]
        dBu = [carve(HALF, KT, SEQ) for _ in range(2)]
        hst = [carve(HALF, KT, SEQ) for _ in range(2)]
        prod = [carve(HALF, KT, SEQ) for _ in range(4)]
        assert top[0] <= weights_end
        top[0] = stacks_top // 2
        w_raw = carve(4 * KT * DM, 4 * KT, DM)
        ctx_tok = carve(TT * DC, TT, DC)
        ctxT = carve(TOK)
        top[0] = stacks_top
        parts = [[carve(KT * TOK // 2, KT, TOK, dt=BF16) for _ in range(3)] for _ in range(2)]
        relrow = carve(TABLE * DH, TABLE, DH, rows=1)
        diag = carve(SPREAD + 1, rows=1)
        xpw = carve(DM, rows=RANK + 2 * STATES)
        xpB = carve(KT * 96, KT, 96)
        xpC = carve(KT * 96, KT, 96)
        xpD = carve(KT * RANK, KT, RANK)
        dtw = carve(KT * RANK, KT, RANK)
        dtwT = carve(DM, rows=RANK)
        cw = carve(KT * TAPS, KT, TAPS)
        cb = carve(KT)
        dtb = carve(KT)
        alog = carve(KT * STATES, KT, STATES)
        dcol = carve(KT)
        assert top[0] <= weights_at - 256
        top[0] = weights_at
        xin = carve(KT * BATCH * PB, KT, BATCH, PB)
        u = carve(KT * TOK, KT, TOK)
        ta = carve(KT * TOK, KT, TOK)
        tb = carve(KT * TOK, KT, TOK)
        bcf = carve(2 * TOK, 2, TOK, rows=96)
        dtlow = carve(TOK, rows=RANK)
        assert top[0] <= late_at
        top[0] = weights_at
        spt = carve(KT * TOK, KT, TOK)
        top[0] = dtu_at
        wT = carve(3 * KT * DM, 3 * KT, DM)
        inw = carve(KT * DC, KT, DC)
        inwT = carve(DM)
        assert top[0] <= dtu_at + KT * TOK
        top[0] = tiles_at
        rest = [carve(KT * TOK, KT, TOK) for _ in range(2)]
        xT = carve(KT * TOK, KT, TOK)
        assert top[0] <= weights_end
        top[0] = 0
        sg = carve(TT * DM, TT, DM)
        gated = carve(TT * DM, TT, DM)
        x2T = carve(KT * TOK, KT, TOK)
        x2 = carve(TT * XW, TT, XW)
        lg = carve(TT * EXPERTS, TT, EXPERTS)
        ex = carve(TT * EXPERTS, TT, EXPERTS)
        lmax = carve(TT)
        lsum = carve(TT)
        gate_w = carve(TT)
        oh = carve(TT * EXPERTS, TT, EXPERTS)
        ohb = carve(EXPERTS * TT // 2, EXPERTS, TT, dt=BF16)
        run = carve(TT)
        within = carve(EXPERTS * TT, EXPERTS, TT)
        total = carve(EXPERTS * TT, EXPERTS, TT)
        incl = carve(EXPERTS * TT, EXPERTS, TT)
        thr = carve(TT)
        over = carve(EXPERTS * TT, EXPERTS, TT)
        ntile = carve(EXPERTS)
        tile_incl = carve(EXPERTS)
        tile0 = carve(EXPERTS)
        ones32 = carve(32)
        pos = carve(TT)
        slot_no = carve(SLOTS)
        e_cmp = carve(SLOTS)
        e_of = carve(SLOTS)
        e_int = carve(SLOTS, dt=I32)
        idx = carve(SLOTS, dt=U32)
        ltri = carve(P // 2, dt=BF16)
        ones_b = carve(P // 2, dt=BF16)
        tokid = carve(TT, dt=F16)[:, 0:TT]
        iota16 = carve(SLOTS * P // 2, dt=F16)
        assert top[0] <= weights_at, (top[0], weights_at)
        top[0] = 0
        onehot = [carve(SLOTS * P // 2, dt=F16) for _ in range(TT)]
        assert top[0] <= 3 * TT * DM
        rows_s = sb("rows_s", [P, SLOTS, XW])
        top[0] = 0
        xsT = carve(KT * SLOTS * P, KT, SLOTS * P)
        xcur = carve(KT * P, KT, P)
        ge = carve(DFF)
        hcur = carve(DFF)
        hT = carve(FT * P, FT, P)
        zrow = carve(DM)
        assert top[0] <= weights_at
        ps = stack.enter_context(nc.psum_tensor("ps", [P, 8, HALF], F32))

        ld_ctx = sem("ld_ctx")
        ld_x = sem("ld_x")
        ld_w = sem("ld_w")
        ld_misc = sem("ld_misc")
        consts = sem("consts")
        pe_fill = sem("pe_fill")
        act_evac = sem("act_evac")
        dve_evac = sem("dve_evac")
        conv_done = sem("conv_done")
        u_ready = sem("u_ready")
        split_ready = sem("split_ready")
        dbu_ready = sem("dbu_ready")
        row_order = sem("row_order")
        sp_exp = sem("sp_exp")
        a_exp = sem("a_exp")
        scan_in = sem("scan_in")
        bc_ready = sem("bc_ready")
        da_ready = sem("da_ready")
        scanned = sem("scanned")
        prod_ready = sem("prod_ready")
        y_added = sem("y_added")
        pe_mark = sem("pe_mark")
        act_mark = sem("act_mark")
        dve_mark = sem("dve_mark")
        dve_order = sem("dve_order")
        act_order = sem("act_order")
        pool_order = sem("pool_order")
        mixer_done = sem("mixer_done")
        part_ready = [[sem(f"part_ready{n}{i}") for i in range(3)] for n in range(2)]
        part_out = [sem(f"part_out{i}") for i in range(3)]
        diag_ready = sem("diag_ready")
        diag_out = sem("diag_out")
        hank_in = sem("hank_in")
        hank_ready = sem("hank_ready")
        ones_rows = sem("ones_rows")
        stack_in = [[sem(f"stack_in{b}{h}") for h in range(2)] for b in range(2)]
        a_scores = sem("a_scores")
        a_max = sem("a_max")
        m_turned = sem("m_turned")
        m_ready = sem("m_ready")
        m_in = sem("m_in")
        b_scores = sem("b_scores")
        p_ready = sem("p_ready")
        pv_done = sem("pv_done")
        pv_out = sem("pv_out")
        tail_pe = sem("tail_pe")
        tail_dve = sem("tail_dve")
        x1_ready = sem("x1_ready")
        sg_ready = sem("sg_ready")
        gated_ready = sem("gated_ready")
        back_pe = sem("back_pe")
        x2_ready = sem("x2_ready")
        x2t_pe = sem("x2t_pe")
        x2t_out = sem("x2t_out")
        logit_pe = sem("logit_pe")
        logit_dve = sem("logit_dve")
        gate_exp = sem("gate_exp")
        oh_ready = sem("oh_ready")
        count_pe = sem("count_pe")
        hot_ready = sem("hot_ready")
        idx_pe = sem("idx_pe")
        x2_full = sem("x2_full")
        x2_out = sem("x2_out")
        idx_ready = sem("idx_ready")
        rows_in = [sem(f"rows_in{s}") for s in range(SLOTS)]
        xs_pe = sem("xs_pe")
        xs_out = sem("xs_out")
        w_in = sem("w_in")
        xcur_ready = sem("xcur_ready")
        gu_done = sem("gu_done")
        ge_ready = sem("ge_ready")
        h_ready = sem("h_ready")
        ht_pe = sem("ht_pe")
        ht_ready = sem("ht_ready")
        y_done = sem("y_done")
        z_ready = sem("z_ready")
        row_ready = sem("row_ready")
        out_done = sem("out_done")
        block = stack.enter_context(nc.Block())

        F_CTX, F_INW, F_DTW, F_XIN, F_XT, F_WT, F_Q, F_K, F_LOW, F_DT, F_V, F_B, F_C = \
            0, 2, 3, 4, 8, 12, 16, 20, 24, 26, 30, 34, 36
        FILLS = 38
        DVE_FILLS = [F_INW] + list(range(F_Q, F_LOW))
        N_CTX = 9 * 16

        def wait_evac(eng, j):
            if j in DVE_FILLS:
                eng.wait_ge(dve_evac, DVE_FILLS.index(j) + 1)
            else:
                eng.wait_ge(act_evac, j + 1 - sum(i < j for i in DVE_FILLS))

        def a_units(b, qd):
            if b >= BATCH:
                return []
            per = {0: range(0, 4), 1: range(4, 8), 2: range(8, 12), 3: range(12, 16),
                   4: range(16, 22), 5: range(22, 28), 6: range(28, 32), 7: ()}[qd]
            return [(b, i // 2, i % 2, b * 32 + i) for i in per]

        def quarter(units, i):
            return units[len(units) * i // 4:len(units) * (i + 1) // 4]

        QKC = [(0, 0), (1, 0), (2, 0), (0, 1), (1, 1), (0, 2)]
        SCALE = float(DH) ** -0.5

        @block.sync
        def _(sp):
            sp.dma_start(ctx_tok, ctx_in.rearrange("b (t p) d -> p (b t) d", p=P)).then_inc(ld_ctx, 16)
            sp.dma_start(inw, in_proj_w.rearrange("(k p) d -> p k d", p=P)).then_inc(ld_ctx, 16)
            sp.dma_start(xpw, x_proj_w).then_inc(ld_ctx, 16)
            sp.dma_start(dtw, dt_proj_w.rearrange("(k p) r -> p k r", p=P)).then_inc(ld_ctx, 16)
            sp.dma_start(cw, conv_w.rearrange("(k p) o t -> p k (o t)", p=P)).then_inc(ld_ctx, 16)
            sp.dma_start(alog, A_log.rearrange("(k p) n -> p k n", p=P)).then_inc(ld_ctx, 16)
            with nc.allow_non_contiguous_dma(reason="three short vectors"):
                sp.dma_start(cb, conv_b.rearrange("(k p) -> p k", p=P)).then_inc(ld_ctx, 16)
                sp.dma_start(dtb, dt_proj_b.rearrange("(k p) -> p k", p=P)).then_inc(ld_ctx, 16)
                sp.dma_start(dcol, D.rearrange("(k p) -> p k", p=P)).then_inc(ld_ctx, 16)
            sp.dma_start(xres[:, :, :], x.rearrange("b (t p) d -> p (b t) d", p=P)).then_inc(ld_x, 16)
            for n, w in enumerate((wq, wk, wv, wo)):
                sp.dma_start(w_raw[:, n * KT:(n + 1) * KT, :],
                             w.rearrange("(k p) d -> p k d", p=P)).then_inc(ld_w, 16)
            sp.dma_start(relrow, rel_pos.rearrange("(o t) d -> o t d", o=1)).then_inc(ld_misc, 16)
            sp.dma_start(wr_s[:, :, :], Wr.rearrange("(k p) e -> p k e", p=P)).then_inc(ld_misc, 16)
            sp.dma_start(br_s[:, :], br.rearrange("(o e) -> o e", o=1).partition_broadcast(P)
                         if False else br.rearrange("(o e) -> o e", o=1).broadcast_to([P, EXPERTS])
                         ).then_inc(ld_misc, 16)
            sp.wait_ge(diag_ready, 1)
            sp.dma_start(diag_d, diag[:, 0:SPREAD]).then_inc(diag_out, 16)
            sp.wait_ge(diag_out, 16)
            for qt in range(KT):
                sp.dma_start(hankel[:, qt, :],
                             bass.AP(tensor=diag_d.tensor, offset=P * (1 - qt),
                                     ap=[[1, P], [1, SEQ]])).then_inc(hank_in, 16)
            for n, dst in enumerate((qp_d, kp_d)):
                for i in range(3):
                    sp.wait_ge(part_ready[n][i], 4 if i == 0 else 1)
                    sp.dma_start(dst[i].rearrange("(m p) t -> p m t", p=P), parts[n][i]).then_inc(part_out[i], 16)
            for i in range(3):
                sp.wait_ge(part_out[i], 32)

            def load_stack(b, hh):
                for c, (qi, ki) in enumerate(QKC):
                    lo = 64 * hh + DH * c
                    for st, src, i in ((qst, qp_d, qi), (kst, kp_d, ki)):
                        sp.dma_start(st[b % 2][lo:lo + DH, :, :],
                                     src[i][hh * P:(hh + 1) * P, b * SEQ:(b + 1) * SEQ]
                                     .rearrange("(h d) t -> d h t", d=DH)).then_inc(stack_in[b % 2][hh], 16)

            def send_max(b):
                sp.wait_ge(m_ready, b + 1)
                for hh in range(2):
                    sp.dma_start(qst[b % 2][64 * hh + ROWS:64 * hh + ROWS + 1, :, :],
                                 negmT[16 * hh:16 * hh + 16, :]).then_inc(m_in, 16)

            for b in range(2):
                sp.wait_ge(ones_rows, b + 1)
                for hh in range(2):
                    load_stack(b, hh)
            send_max(0)
            sp.wait_ge(scan_in, 1)
            sp.wait_ge(split_ready, BATCH)

            def load_gate_up(dst, src, e):
                for k in range(KT):
                    sp.dma_start(dst[:, (e * KT + k) * DFF:(e * KT + k + 1) * DFF],
                                 src[e, k * P:(k + 1) * P, :]).then_inc(w_in, 16)

            early = [(wg_s, Wg, e) for e in range(EXPERTS)] + [(wu_s, Wu, e) for e in range(2)]
            for b in range(BATCH):
                for hh in range(2):
                    if b + 2 < BATCH:
                        sp.wait_ge(b_scores, 4 * (QUADS * b + 4 * (hh + 1)))
                        load_stack(b + 2, hh)
                    if early:
                        load_gate_up(*early.pop(0))
                if b + 1 < BATCH:
                    send_max(b + 1)
            sp.wait_ge(y_added, STATES * BATCH)
            for e in range(2, EXPERTS):
                load_gate_up(wu_s, Wu, e)
            for e in range(EXPERTS):
                sp.dma_start(wd_s[:, e * FT * DM:(e + 1) * FT * DM].rearrange("p (k f) -> p k f", k=FT),
                             Wd[e].rearrange("(k p) f -> p k f", p=P)).then_inc(w_in, 16)
            sp.wait_ge(x2_full, 1)
            sp.dma_start(x2_d.rearrange("(t p) c -> p t c", p=P), x2).then_inc(x2_out, 16)
            sp.wait_ge(out_done, 16 * SLOTS)

        @block.gpsimd
        def _(pool):
            g = nc.gpsimd
            order = [0]

            def link(ins):
                order[0] += 1
                ins.then_inc(pool_order, 1)
                pool.wait_ge(pool_order, order[0])

            link(g.memset(identf[:, :], 0.0))
            g.affine_select(out=identf[:, :], in_=identf[:, :], compare_op=ALU.not_equal, fill=1.0, base=0,
                            pattern=[[-1, P]], channel_multiplier=1).then_inc(consts, 1)
            g.memset(xpB, 0.0)
            g.memset(xpC, 0.0)
            g.memset(xin[:, :, :, 0:PAD], 0.0).then_inc(consts, 1)
            link(g.memset(flip[:, :], 0.0))
            g.affine_select(out=flip[:, :], in_=flip[:, :], compare_op=ALU.not_equal, fill=1.0, base=-(P - 1),
                            pattern=[[1, P]], channel_multiplier=1)
            link(g.memset(sel, 0.0))
            for k in range(3):
                link(g.affine_select(out=sel, in_=sel, compare_op=ALU.not_equal, fill=1.0, base=-32 * k,
                                     pattern=[[-1, STATES], [0, P]], channel_multiplier=1))
            g.memset(vaug[:, :, :, DH:VW], 1.0)
            link(g.memset(rows_s[:, :, :], 0.0))
            for buf in range(2):
                if buf:
                    pool.wait_ge(pe_fill, F_Q)
                for lo in (32, 96):
                    ins = g.memset(kst[buf][lo:lo + 32, :, :], 1.0)
                    link(ins)
                pool.sem_inc(ones_rows, 1)
                if buf == 0:
                    pool.sem_inc(consts, 1)
            for b in range(BATCH):
                cols = slice(b * SEQ, (b + 1) * SEQ)
                if b % 2 == 0:
                    wait_evac(pool, F_C + b // 2)
                link(g.tensor_copy(bc3[:, :, cols], bcf[:, :, cols]))
                link(g.tensor_tensor(bcf[:, :, cols], bcf[:, :, cols], bc3[:, :, cols], ALU.subtract))
                link(g.tensor_copy(bc3[32:64, :, cols], bcf[32:64, :, cols]))
                link(g.tensor_copy(bc3[64:96, :, cols], bcf[64:96, :, cols]))
                link(g.tensor_tensor(bc3[64:96, :, cols], bcf[64:96, :, cols], bc3[64:96, :, cols], ALU.subtract))
                pool.sem_inc(split_ready, 1)
            for m in range(STATES * BATCH):
                b = m // STATES
                pool.wait_ge(prod_ready, m + 1)
                y = yT[:, :, b * SEQ:(b + 1) * SEQ]
                if m:
                    pool.wait_ge(y_added, m)
                g.tensor_tensor(y, y, prod[m % 4], ALU.add).then_inc(y_added, 1)
            pool.wait_ge(x1_ready, 1)
            g.iota(thr, pattern=[[P, TT]], base=0, channel_multiplier=0, allow_small_or_imprecise_dtypes=True)
            g.iota(slot_no, pattern=[[1, SLOTS]], base=0, channel_multiplier=0,
                   allow_small_or_imprecise_dtypes=True)
            g.iota(iota16, pattern=[[1, SLOTS * P]], base=0, channel_multiplier=0,
                   allow_small_or_imprecise_dtypes=True)
            g.iota(tokid, pattern=[[P, TT]], base=-FAR, channel_multiplier=1,
                   allow_small_or_imprecise_dtypes=True)
            g.memset(ones32, 1.0)
            g.memset(ones_b, 1.0)
            link(g.memset(ltri, 1.0))
            g.affine_select(out=ltri, in_=ltri, compare_op=ALU.is_gt, fill=0.0, base=0,
                            pattern=[[1, P]], channel_multiplier=-1).then_inc(consts, 1)
            pool.wait_ge(x2_out, 16)
            pool.wait_ge(idx_ready, 1)
            for s in range(SLOTS):
                g.indirect_dma_start(out=rows_s[:, s, :], out_offset=None, in_=x2_d,
                                     in_offset=bass.IndirectOffsetOnAxis(ap=idx[:, s:s + 1], axis=0),
                                     bounds_check=TOK - 1, oob_is_err=False).then_inc(rows_in[s], 16)
            for s in range(SLOTS):
                pool.wait_ge(row_ready, s + 2)
                g.indirect_dma_start(out=out.rearrange("b s d -> (b s) d"),
                                     out_offset=bass.IndirectOffsetOnAxis(ap=idx[:, s:s + 1], axis=0),
                                     in_=rows_s[:, s, 0:DM], in_offset=None,
                                     bounds_check=TOK - 1, oob_is_err=False).then_inc(out_done, 16)

        @block.tensor
        def _(pe):
            mm = nc.tensor.matmul

            def begin(j):
                if j >= 8:
                    wait_evac(pe, j - 8)
                return j % 8

            pe.wait_ge(consts, 1)
            pe.wait_ge(ld_ctx, N_CTX)
            for j in range(2):
                for i in range(4):
                    last = nc.tensor.transpose(ps[:, j, i * P:(i + 1) * P], ctx_tok[:, 4 * j + i, :], identf[:, :])
                last.then_inc(pe_fill, 1)
            R = RANK + 2 * STATES
            for k in range(KT):
                nc.tensor.transpose(ps[:, 2, k * P:(k + 1) * P], inw[:, k, :], identf[:, :])
            for k in range(KT):
                last = nc.tensor.transpose(ps[:, 2, DM + k * R:DM + (k + 1) * R], xpw[:, k * P:(k + 1) * P],
                                           identf[0:R, 0:R])
            last.then_inc(pe_fill, 1)
            for k in range(KT):
                last = nc.tensor.transpose(ps[0:RANK, 3, k * P:(k + 1) * P], dtw[:, k, :], identf[:, :])
            last.then_inc(pe_fill, 1)
            wait_evac(pe, 1)
            wait_evac(pe, F_INW)
            for k in range(KT):
                for hf in range(2):
                    bank = begin(F_XIN + 2 * k + hf)
                    mm(ps[:, bank, :], inwT[:, k * P:(k + 1) * P], ctxT[:, hf * HALF:(hf + 1) * HALF],
                       start=True, stop=True).then_inc(pe_fill, 1)
            pe.wait_ge(ld_x, 16)
            for k in range(KT):
                for hf in range(2):
                    bank = begin(F_XT + 2 * k + hf)
                    for i in range(4):
                        last = nc.tensor.transpose(ps[:, bank, i * P:(i + 1) * P],
                                                   xres[:, 4 * hf + i, k * P:(k + 1) * P], identf[:, :])
                    last.then_inc(pe_fill, 1)
            pe.wait_ge(ld_w, 64)
            for w in range(4):
                bank = begin(F_WT + w)
                for k in range(KT):
                    for o in range(KT):
                        at = k * DM + o * P
                        last = nc.tensor.transpose(ps[:, bank, at:at + P],
                                                   w_raw[:, w * KT + o, k * P:(k + 1) * P], identf[:, :])
                last.then_inc(pe_fill, 1)
            wait_evac(pe, F_WT + 3)
            for w, f in ((0, F_Q), (1, F_K)):
                for m in range(KT):
                    for hf in range(2):
                        bank = begin(f + 2 * m + hf)
                        for k in range(KT):
                            last = mm(ps[:, bank, :], wT[:, w * KT + k, m * P:(m + 1) * P],
                                      xT[:, k, hf * HALF:(hf + 1) * HALF], start=(k == 0), stop=(k == KT - 1))
                        last.then_inc(pe_fill, 1)
            pe.wait_ge(u_ready, KT)

            def project_u(f, w, rows):
                for hf in range(2):
                    bank = begin(f + hf)
                    for k in range(KT):
                        last = mm(ps[0:rows, bank, :], w[:, k, :], u[:, k, hf * HALF:(hf + 1) * HALF],
                                  start=(k == 0), stop=(k == KT - 1))
                    last.then_inc(pe_fill, 1)

            project_u(F_LOW, xpD, RANK)
            wait_evac(pe, F_LOW + 1)
            for k in range(KT):
                for hf in range(2):
                    bank = begin(F_DT + 2 * k + hf)
                    mm(ps[:, bank, :], dtwT[:, k * P:(k + 1) * P], dtlow[:, hf * HALF:(hf + 1) * HALF],
                       start=True, stop=True).then_inc(pe_fill, 1)
            for j in range(4):
                bank = begin(F_V + j)
                for t in range(2):
                    for k in range(KT):
                        last = mm(ps[:, bank, t * DM:(t + 1) * DM], xT[:, k, (2 * j + t) * P:(2 * j + t + 1) * P],
                                  wT[:, 2 * KT + k, :], start=(k == 0), stop=(k == KT - 1))
                last.then_inc(pe_fill, 1)
            project_u(F_B, xpB, 96)
            project_u(F_C, xpC, 96)
            wait_evac(pe, FILLS - 1)

            def spread(m):
                b, n = m // STATES, m % STATES
                if m >= 2:
                    pe.wait_ge(prod_ready, m - 1)
                if n == 0:
                    pe.wait_ge(split_ready, b + 1)
                for i in range(2):
                    last = mm(ps[:, 4 + m % 2, i * SEQ:(i + 1) * SEQ], sel[:, n, :],
                              bc3[:, i, b * SEQ:(b + 1) * SEQ], start=True, stop=True)
                last.then_inc(bc_ready, 1)

            pe.wait_ge(hank_ready, 1)

            def scores_a(b, pair, qt, n):
                bank = n % 2
                hh, h0 = pair // 8, 2 * pair % 16
                if n >= 2:
                    pe.wait_ge(a_max, n - 1)
                lo = 64 * hh
                for i in range(2):
                    mm(ps[:, bank, i * SEQ:(i + 1) * SEQ], qst[b % 2][lo:lo + ROWS, h0 + i, qt * P:(qt + 1) * P],
                       kst[b % 2][lo:lo + ROWS, h0 + i, :], start=(i == 0), stop=False, skip_group_check=True)
                mm(ps[:, bank, :].rearrange("p (h k) -> p h k", h=2), flip[:, :],
                   hank_hi[:, qt:qt + 1, :].broadcast_to([P, 2, SEQ]), start=False, stop=True,
                   skip_group_check=True).then_inc(a_scores, 1)

            def scores_b(b, qd, kt, pr):
                n = 4 * (QUADS * b + qd) + 2 * kt + pr
                if n >= 2:
                    pe.wait_ge(p_ready, n - 1)
                hh, h0 = qd // 4, 4 * qd % 16
                lo, hi = 64 * hh, 64 * hh + ROWS + 1
                bank = 2 + n % 2
                for i in range(2):
                    h = h0 + 2 * pr + i
                    mm(ps[:, bank, i * SEQ:(i + 1) * SEQ], kst[b % 2][lo:hi, h, kt * P:(kt + 1) * P],
                       qst[b % 2][lo:hi, h, :], start=(i == 0), stop=False, skip_group_check=True)
                view = ps[:, bank, :].rearrange("p (h q) -> p h q", h=2)
                for part in (hank_hi, hank_lo):
                    for qt in range(KT):
                        last = mm(view[:, :, qt * P:(qt + 1) * P], part[:, qt, kt * P:(kt + 1) * P],
                                  flip[:, :].rearrange("p (o k) -> p o k", o=1).broadcast_to([P, 2, P]),
                                  start=False, stop=True, skip_group_check=True)
                last.then_inc(b_scores, 1)

            def weigh(b, qd):
                n = QUADS * b + qd
                pe.wait_ge(pv_out, n + 1)
                pe.wait_ge(p_ready, 4 * n + 4)
                for kt in range(KT):
                    for j in range(4):
                        last = mm(ps[32 * j:32 * j + VW, 6, 0:SEQ], vaug[:, 2 * b + kt, 4 * qd + j, :],
                                  prob[2 * (n % 2) + kt][:, j * SEQ:(j + 1) * SEQ],
                                  start=(kt == 0), stop=(kt == KT - 1), skip_group_check=True)
                last.then_inc(pv_done, 1)

            misc = [0]

            def misc_begin():
                if misc[0]:
                    pe.wait_ge(tail_dve, misc[0])
                misc[0] += 1

            def turn_max(b):
                pe.wait_ge(a_max, 32 * (b + 1))
                misc_begin()
                for qt in range(KT):
                    last = nc.tensor.transpose(ps[0:HEADS, 7, qt * P:(qt + 1) * P], negm[b % 2][:, qt, :],
                                               identf[:, :])
                last.then_inc(tail_pe, 1)

            def tail(b, step):
                qt, k = step // 4, step % 4
                if k < 2:
                    pe.wait_ge(pv_out, QUADS * (b + 1) + 1)
                misc_begin()
                if k < 2:
                    for i in range(4):
                        last = nc.tensor.transpose(ps[:, 7, i * P:(i + 1) * P],
                                                   ctxS[b % 2][:, 4 * k + i, qt * P:(qt + 1) * P], identf[:, :])
                elif k == 2:
                    for i in range(KT):
                        last = nc.tensor.transpose(ps[:, 7, i * P:(i + 1) * P], ctxn[:, i * P:(i + 1) * P],
                                                   identf[:, :])
                else:
                    for i in range(KT):
                        last = mm(ps[:, 7, 0:DM], ctxnT[:, i, :], woT[:, i, :], start=(i == 0),
                                  stop=(i == KT - 1))
                last.then_inc(tail_pe, 1)

            for hh in range(2):
                pe.wait_ge(stack_in[0][hh], 16 * 12)
                for unit in [u_ for qd in range(QUADS) for u_ in a_units(0, qd) if u_[1] // 8 == hh]:
                    scores_a(*unit)
            turn_max(0)
            spread(0)
            for b in range(BATCH):
                pe.wait_ge(m_in, 32 * (b + 1))
                for qd in range(QUADS):
                    if qd in (0, 4) and b + 1 < BATCH:
                        pe.wait_ge(stack_in[(b + 1) % 2][qd // 4], 16 * 12 * ((b + 1) // 2 + 1))
                    for i in range(4):
                        m = 2 * (QUADS * b + qd) + i // 2 + 1
                        if i % 2 == 0 and m < STATES * BATCH:
                            spread(m)
                        for unit in quarter(a_units(b + 1, qd), i):
                            scores_a(*unit)
                        scores_b(b, qd, i // 2, i % 2)
                        if i == 1 and (b or qd):
                            weigh(b - (qd == 0), (qd - 1) % QUADS)
                    if qd == 7 and b + 1 < BATCH:
                        turn_max(b + 1)
                    if b and qd >= 1:
                        for step in ([qd - 1] if qd < 7 else [6, 7]):
                            tail(b - 1, step)
            weigh(BATCH - 1, QUADS - 1)
            for step in range(8):
                tail(BATCH - 1, step)

            pe.wait_ge(gated_ready, 1)
            for j in range(4):
                for i in range(4):
                    t, k = 2 * j + i // 2, i % 2
                    b, lt = t // 2, t % 2
                    last = nc.tensor.transpose(ps[:, j, i * P:(i + 1) * P],
                                               gated[:, k * BATCH + b, lt * P:(lt + 1) * P], identf[:, :])
                last.then_inc(back_pe, 1)

            pe.wait_ge(x2_ready, 1)
            for j in range(4):
                for i in range(4):
                    t = 4 * (j % 2) + i
                    last = nc.tensor.transpose(ps[:, j, i * P:(i + 1) * P],
                                               x2[:, t, (j // 2) * P:(j // 2 + 1) * P], identf[:, :])
                last.then_inc(x2t_pe, 1)
            pe.wait_ge(x2t_out, 4)
            for t in range(TT):
                for k in range(KT):
                    last = mm(ps[:, 4, t * EXPERTS:(t + 1) * EXPERTS], x2T[:, k, t * P:(t + 1) * P], wr_s[:, k, :],
                              start=(k == 0), stop=(k == KT - 1))
            last.then_inc(logit_pe, 1)
            pe.wait_ge(oh_ready, 1)
            pe.wait_ge(consts, 4)
            oh_cols = ohb.rearrange("p e t -> p (e t)")
            mm(ps[:, 5, 0:EXPERTS * TT], ltri, oh_cols, start=True, stop=True)
            mm(ps[:, 6, 0:EXPERTS * TT], ones_b, oh_cols, start=True, stop=True).then_inc(count_pe, 1)
            pe.wait_ge(hot_ready, TT)
            for s in range(SLOTS):
                for t in range(TT):
                    last = mm(ps[:, 7, s:s + 1], onehot[t][:, s * P:(s + 1) * P], tokid[:, t:t + 1],
                              start=(t == 0), stop=(t == TT - 1))
            last.then_inc(idx_pe, 1)
            for j in range(2 * ((SLOTS + 3) // 4)):
                k, s0 = j % 2, 4 * (j // 2)
                for i in range(min(4, SLOTS - s0)):
                    pe.wait_ge(rows_in[s0 + i], 16)
                    last = nc.tensor.transpose(ps[:, j, i * P:(i + 1) * P],
                                               rows_s[:, s0 + i, k * P:(k + 1) * P], identf[:, :])
                last.then_inc(xs_pe, 1)
            pe.wait_ge(xs_out, 6)
            pe.wait_ge(w_in, 16 * 20)

            def gate_up(s, e):
                pe.wait_ge(xcur_ready, s + 1)
                for w, b0 in ((wg_s, 0), (wu_s, 2)):
                    for fh in range(2):
                        for k in range(KT):
                            last = mm(ps[:, b0 + fh, :], xcur[:, k, :],
                                      w[:, bass.ds((e * KT + k) * DFF + fh * HALF, HALF)], start=(k == 0), stop=(k == KT - 1))
                last.then_inc(gu_done, 1)

            def turn_h(s):
                pe.wait_ge(h_ready, s + 1)
                for f in range(FT):
                    last = nc.tensor.transpose(ps[:, 4 + f // 4, (f % 4) * P:(f % 4 + 1) * P],
                                               hcur[:, f * P:(f + 1) * P], identf[:, :])
                last.then_inc(ht_pe, 1)

            def down(s, e):
                pe.wait_ge(ht_ready, s + 1)
                pe.wait_ge(z_ready, s + 1)
                for f in range(FT):
                    last = mm(ps[:, 6, 0:DM], hT[:, f, :], wd_s[:, bass.ds((e * FT + f) * DM, DM)], start=(f == 0),
                              stop=(f == FT - 1))
                last.then_inc(y_done, 1)

            def expert_of(s):
                return pe.value_load(e_int[0:1, bass.ds(s, 1)], min_val=0, max_val=EXPERTS - 1)

            gate_up(0, expert_of(0))
            turn_h(0)
            with pe.Fori(1, SLOTS) as s:
                gate_up(s, expert_of(s))
                down(s - 1, expert_of(s - 1))
                turn_h(s)
            down(SLOTS - 1, expert_of(SLOTS - 1))

        @block.scalar
        def _(act):
            A = nc.scalar.activation

            def filled(j):
                act.wait_ge(pe_fill, j + 1)
                return j % 8

            for j in range(2):
                bank = filled(F_CTX + j)
                A(ctxT[:, j * HALF:(j + 1) * HALF], ps[:, bank, :], ACT.Copy).then_inc(act_evac, 1)
            bank = filled(F_DTW)
            A(dtwT, ps[0:RANK, bank, 0:DM], ACT.Copy).then_inc(act_evac, 1)
            act.wait_ge(consts, 2)
            for k in range(KT):
                for hf in range(2):
                    bank = filled(F_XIN + 2 * k + hf)
                    A(xin[:, k, 2 * hf:2 * hf + 2, PAD:PB], ps[:, bank, :].rearrange("p (b l) -> p b l", b=2),
                      ACT.Copy).then_inc(act_evac, 1)
            for k in range(KT):
                for hf in range(2):
                    bank = filled(F_XT + 2 * k + hf)
                    A(xT[:, k, hf * HALF:(hf + 1) * HALF], ps[:, bank, :], ACT.Copy).then_inc(act_evac, 1)
            for w in range(4):
                bank = filled(F_WT + w)
                dst = wT[:, w * KT:(w + 1) * KT, :] if w < 3 else woT[:, :, :]
                A(dst.rearrange("p k o -> p (k o)"), ps[:, bank, :], ACT.Copy).then_inc(act_evac, 1)
            for k in range(KT):
                act.wait_ge(conv_done, k + 1)
                A(u[:, k, :], ta[:, k, :], ACT.Silu).then_inc(u_ready, 1)
            for n, (f, sc) in enumerate(((F_Q, SCALE), (F_K, 1.0))):
                for m in range(KT):
                    for hf in range(2):
                        bank = filled(f + 2 * m + hf)
                        A(parts[n][0][:, m, hf * HALF:(hf + 1) * HALF], ps[:, bank, :], ACT.Copy,
                          scale=sc).then_inc(part_ready[n][0], 1)
            for hf in range(2):
                bank = filled(F_LOW + hf)
                A(dtlow[:, hf * HALF:(hf + 1) * HALF], ps[0:RANK, bank, :], ACT.Copy).then_inc(act_evac, 1)
            for n in range(2):
                act.wait_ge(dve_evac, 1 + 4 * (n + 1))
                A(parts[n][1], rest[n], ACT.Copy).then_inc(part_ready[n][1], 1)
            for k in range(KT):
                for hf in range(2):
                    bank = filled(F_DT + 2 * k + hf)
                    cols = slice(hf * HALF, (hf + 1) * HALF)
                    A(spt[:, k, cols], ps[:, bank, :], ACT.Abs, bias=dtb[:, k:k + 1]).then_inc(act_order, 1)
                    A(dts[:, k, cols], ps[:, bank, :], ACT.Relu, bias=dtb[:, k:k + 1]).then_inc(act_evac, 1)
            A(acol, alog, ACT.Exp).then_inc(a_exp, 1)
            for k in range(KT):
                act.wait_ge(act_order, 2 * k + 2)
                A(spt[:, k, :], spt[:, k, :], ACT.Exp, scale=-1.0).then_inc(sp_exp, 1)
            act.wait_ge(consts, 3)
            for j in range(4):
                bank = filled(F_V + j)
                A(vaug[:, 2 * j:2 * j + 2, :, 0:DH].rearrange("p t h d -> p (t h) d"),
                  ps[:, bank, :].rearrange("p (h d) -> p h d", d=DH), ACT.Copy).then_inc(act_evac, 1)
            for i, f in enumerate((F_B, F_C)):
                for hf in range(2):
                    bank = filled(f + hf)
                    A(bcf[:, i, hf * HALF:(hf + 1) * HALF], ps[0:96, bank, :], ACT.Copy).then_inc(act_evac, 1)

            def decay(m):
                b, n = m // STATES, m % STATES
                act.wait_ge(scanned, m + 1 if m >= 4 else 4)
                for k in range(KT):
                    A(dA[m % 4][:, k, 1:SEQ], dts[:, k, b * SEQ + 1:(b + 1) * SEQ], ACT.Exp,
                      scale=acol[:, k, n:n + 1]).then_inc(da_ready, 1)

            act.wait_ge(scan_in, 1)
            decay(0)
            decay(1)
            for n in range(4 * QUADS * BATCH):
                slot, kt, pr = n // 4, n // 2 % 2, n % 2
                act.wait_ge(b_scores, n + 1)
                if slot >= 2:
                    act.wait_ge(pv_done, slot - 1)
                A(prob[2 * (slot % 2) + kt][:, pr * HALF:(pr + 1) * HALF], ps[:, 2 + n % 2, :],
                  ACT.Exp).then_inc(p_ready, 1)
                if n % 2 == 0 and n // 2 + 2 < STATES * BATCH:
                    decay(n // 2 + 2)

            act.wait_ge(x1_ready, 1)
            A(sg, xres[:, :, :], ACT.Silu).then_inc(sg_ready, 1)
            for j in range(4):
                act.wait_ge(x2t_pe, j + 1)
                A(x2T[:, j // 2, (j % 2) * HALF:(j % 2 + 1) * HALF], ps[:, j, :], ACT.Copy).then_inc(x2t_out, 1)
            act.wait_ge(logit_dve, 1)
            A(ex, lg, ACT.Exp).then_inc(gate_exp, 1)
            for j in range(2 * ((SLOTS + 3) // 4)):
                k, s0 = j % 2, 4 * (j // 2)
                w = min(4, SLOTS - s0) * P
                act.wait_ge(xs_pe, j + 1)
                A(xsT[:, k, s0 * P:s0 * P + w], ps[:, j, 0:w], ACT.Copy).then_inc(xs_out, 1)
            act.wait_ge(xs_out, 6)

            def take_x(s):
                A(xcur, xsT[:, :, bass.ds(s * P, P)], ACT.Copy).then_inc(xcur_ready, 1)

            def silu_gate(s):
                act.wait_ge(gu_done, s + 1)
                A(ge, ps[:, 0:2, :].rearrange("p b c -> p (b c)"), ACT.Silu).then_inc(ge_ready, 1)

            def put_hT(s):
                act.wait_ge(ht_pe, s + 1)
                A(hT.rearrange("p f t -> p (f t)"), ps[:, 4:6, :].rearrange("p b c -> p (b c)"),
                  ACT.Copy).then_inc(ht_ready, 1)

            take_x(0)
            silu_gate(0)
            act.wait_ge(gu_done, 1)
            act.sem_inc(act_mark, 1)
            take_x(1)
            put_hT(0)
            with act.Fori(1, SLOTS - 1) as s:
                silu_gate(s)
                act.wait_ge(gu_done, s + 1)
                act.sem_inc(act_mark, 1)
                take_x(s + 1)
                put_hT(s)
            silu_gate(SLOTS - 1)
            put_hT(SLOTS - 1)

        @block.vector
        def _(dve):
            v = nc.vector
            order = [0]

            def link(ins):
                order[0] += 1
                ins.then_inc(dve_order, 1)
                dve.wait_ge(dve_order, order[0])

            R = RANK + 2 * STATES
            dve.wait_ge(consts, 2)
            dve.wait_ge(pe_fill, F_INW + 1)
            xpt = ps[:, 2, DM:DM + KT * R].rearrange("p (k r) -> p k r", k=KT)
            v.tensor_copy(inwT, ps[:, 2, 0:DM])
            for c in range(3):
                v.tensor_copy(xpB[:, :, 32 * c:32 * c + STATES], xpt[:, :, RANK:RANK + STATES])
                v.tensor_copy(xpC[:, :, 32 * c:32 * c + STATES], xpt[:, :, RANK + STATES:R])
            v.tensor_copy(xpD, xpt[:, :, 0:RANK]).then_inc(dve_evac, 1)
            dve.wait_ge(ld_misc, 48)
            mid = diag[:, SEQ - 64:SEQ - 64 + TABLE]
            link(v.tensor_reduce(mid, relrow, axis=AX.X, op=ALU.add))
            link(v.tensor_scalar_mul(mid, mid, 1.0 / DH))
            lo = SEQ - 64
            v.tensor_copy(diag[:, 0:lo], diag[:, lo:lo + 1].broadcast_to([1, lo]))
            link(v.tensor_copy(diag[:, lo + TABLE:SPREAD],
                               diag[:, lo + TABLE - 1:lo + TABLE].broadcast_to([1, SPREAD - lo - TABLE])))
            v.tensor_copy(diag[:, SPREAD:SPREAD + 1], diag[:, 0:1]).then_inc(diag_ready, 1)
            for k in range(KT):
                dve.wait_ge(act_evac, F_XIN + 2 * k + 1)
                o = ta[:, k, :].rearrange("p (b l) -> p b l", b=BATCH)
                link(v.tensor_scalar(o, xin[:, k, :, PAD:PB], cw[:, k, PAD:TAPS], cb[:, k:k + 1], ALU.mult, ALU.add))
                for j in range(PAD):
                    ins = v.scalar_tensor_tensor(out=o, in0=xin[:, k, :, j:j + SEQ], scalar=cw[:, k, j:j + 1],
                                                 in1=o, op0=ALU.mult, op1=ALU.add)
                    if j < PAD - 1:
                        link(ins)
                    else:
                        ins.then_inc(conv_done, 1)
            for n, (f, sc) in enumerate(((F_Q, SCALE), (F_K, 1.0))):
                for i in range(4):
                    m, cols = i // 2, slice(i % 2 * HALF, (i % 2 + 1) * HALF)
                    dve.wait_ge(part_ready[n][0], i + 1)
                    v.scalar_tensor_tensor(out=rest[n][:, m, cols], in0=ps[:, (f + i) % 8, :], scalar=sc,
                                           in1=parts[n][0][:, m, cols], op0=ALU.mult,
                                           op1=ALU.subtract).then_inc(dve_evac, 1)
            dve.wait_ge(hank_in, 32)
            link(v.tensor_copy(hank_hi[:, :, :], hankel[:, :, :]))
            v.tensor_tensor(hank_lo[:, :, :], hankel[:, :, :], hank_hi[:, :, :],
                            ALU.subtract).then_inc(hank_ready, 1)
            for k in range(KT):
                dve.wait_ge(u_ready, k + 1)
                v.tensor_scalar_mul(yT[:, k, :], u[:, k, :], dcol[:, k:k + 1])
            for n in range(2):
                dve.wait_ge(part_ready[n][1], 1)
                v.tensor_tensor(parts[n][2], rest[n], parts[n][1], ALU.subtract).then_inc(part_ready[n][2], 1)
            dve.wait_ge(a_exp, 1)
            v.tensor_scalar_mul(acol, acol, -1.0)
            wait_evac(dve, F_DT + 3)
            for k in range(KT):
                dve.wait_ge(sp_exp, k + 1)
                link(v.tensor_scalar_mul(tb[:, k, :], spt[:, k, :], LOG1P[-1]))
                for c in LOG1P[-2::-1]:
                    link(v.scalar_tensor_tensor(out=tb[:, k, :], in0=tb[:, k, :], scalar=c, in1=spt[:, k, :],
                                                op0=ALU.add, op1=ALU.mult))
                link(v.tensor_tensor(dts[:, k, :], dts[:, k, :], tb[:, k, :], ALU.add))
            dve.wait_ge(pe_fill, F_B)
            link(v.tensor_tensor(dtu, dts, u, ALU.mult))
            for i in range(4):
                v.memset(dA[i][:, :, 0:1], 0.0).then_inc(scanned, 1)
            wait_evac(dve, F_V)
            link(v.memset(ps[:, 6, :], 0.0))
            dve.sem_inc(pv_out, 1)
            dve.sem_inc(scan_in, 1)

            def inject(m):
                b = m // STATES
                dve.wait_ge(bc_ready, m + 1)
                v.tensor_tensor(dBu[m % 2], dtu[:, :, b * SEQ:(b + 1) * SEQ],
                                ps[:, 4 + m % 2, 0:SEQ].rearrange("p (o l) -> p o l", o=1)
                                .broadcast_to([P, KT, SEQ]), ALU.mult).then_inc(dbu_ready, 1)

            def scan(m):
                flat = "p k l -> p (k l)"
                dve.wait_ge(dbu_ready, m + 1)
                dve.wait_ge(da_ready, 2 * m + 2)
                v.tensor_tensor_scan(out=hst[m % 2].rearrange(flat), data0=dA[m % 4].rearrange(flat),
                                     data1=dBu[m % 2].rearrange(flat), initial=0.0, op0=ALU.mult,
                                     op1=ALU.add).then_inc(scanned, 1)

            def read_out(m):
                dve.wait_ge(scanned, m + 5)
                if m >= 4:
                    dve.wait_ge(y_added, m - 3)
                v.tensor_tensor(prod[m % 4], hst[m % 2],
                                ps[:, 4 + m % 2, SEQ:2 * SEQ].rearrange("p (o l) -> p o l", o=1)
                                .broadcast_to([P, KT, SEQ]), ALU.mult).then_inc(prod_ready, 1)

            def maxima(b, pair, qt, n):
                dve.wait_ge(a_scores, n + 1)
                v.tensor_reduce(negm[b % 2][:, qt, 2 * pair:2 * pair + 2],
                                ps[:, n % 2, :].rearrange("p (h k) -> p h k", h=2), axis=AX.X,
                                op=ALU.max).then_inc(a_max, 1)

            def copy_context(b, qd):
                n = QUADS * b + qd
                dve.wait_ge(pv_done, n + 1)
                v.tensor_copy(ctxS[b % 2][:, qd, :], ps[:, 6, 0:SEQ]).then_inc(pv_out, 1)

            misc = [0]

            def misc_filled():
                misc[0] += 1
                dve.wait_ge(tail_pe, misc[0])

            def put_max(b):
                misc_filled()
                if b:
                    dve.wait_ge(m_in, 32 * b)
                link(v.tensor_scalar_mul(negmT, ps[0:HEADS, 7, 0:SEQ], -1.0))
                dve.sem_inc(m_ready, 1)
                dve.sem_inc(tail_dve, 1)

            def tail(b, step):
                qt, k = step // 4, step % 4
                misc_filled()
                if k < 2:
                    quad = ps[:, 7, :].rearrange("p (h c) -> p h c", c=32)
                    link(v.reciprocal(rcp.rearrange("p (h o) -> p h o", o=1), quad[:, :, DH:VW]))
                    v.tensor_tensor(ctxn[:, k * P:(k + 1) * P].rearrange("p (h d) -> p h d", d=DH),
                                    quad[:, :, 0:DH],
                                    rcp.rearrange("p (h o) -> p h o", o=1).broadcast_to([P, 16, DH]),
                                    ALU.mult).then_inc(tail_dve, 1)
                elif k == 2:
                    v.tensor_copy(ctxnT.rearrange("p k t -> p (k t)"), ps[:, 7, 0:DM]).then_inc(tail_dve, 1)
                else:
                    t = 2 * b + qt
                    v.tensor_tensor(xres[:, t, :], xres[:, t, :], ps[:, 7, 0:DM], ALU.add).then_inc(tail_dve, 1)
                    dve.wait_ge(tail_dve, misc[0])
                    link(v.bn_stats(stats[:, t, :], xres[:, t, :]))
                    link(v.bn_aggr(mv[:, t, :], stats[:, t, :]))

            for qd in range(QUADS):
                for unit in a_units(0, qd):
                    maxima(*unit)
            put_max(0)
            for b in range(BATCH):
                for qd in range(QUADS):
                    for i in range(4):
                        m = 2 * (QUADS * b + qd) + i // 2
                        if i % 2 == 0:
                            inject(m)
                        for unit in quarter(a_units(b + 1, qd), i):
                            maxima(*unit)
                        if i % 2 == 0:
                            scan(m)
                        else:
                            read_out(m)
                        if i == 1 and (b or qd):
                            copy_context(b - (qd == 0), (qd - 1) % QUADS)
                    if qd == 7 and b + 1 < BATCH:
                        put_max(b + 1)
                    if b and qd >= 1:
                        for step in ([qd - 1] if qd < 7 else [6, 7]):
                            tail(b - 1, step)
            copy_context(BATCH - 1, QUADS - 1)
            for step in range(8):
                tail(BATCH - 1, step)

            def inverse_root():
                link(v.tensor_scalar_add(veps[:, :], mv[:, :, 1], EPS))
                link(v.tensor_scalar(rstd[:, :].bitcast(I32), veps[:, :].bitcast(I32), 1, None,
                                     ALU.logical_shift_right))
                link(v.tensor_scalar(rstd[:, :].bitcast(I32), rstd[:, :].bitcast(I32), -1.0, float(RSQRT_SEED),
                                     ALU.mult, ALU.add))
                link(v.tensor_scalar_mul(veps[:, :], veps[:, :], -0.5))
                for _ in range(3):
                    link(v.tensor_tensor(nwt[:, :], rstd[:, :], rstd[:, :], ALU.mult))
                    link(v.tensor_tensor(nwt[:, :], nwt[:, :], veps[:, :], ALU.mult))
                    link(v.scalar_tensor_tensor(out=rstd[:, :], in0=nwt[:, :], scalar=1.5, in1=rstd[:, :],
                                                op0=ALU.add, op1=ALU.mult))

            def normalise(dst):
                inverse_root()
                for t in range(TT):
                    link(v.tensor_scalar(dst(t), xres[:, t, :], mv[:, t, 0:1], rstd[:, t:t + 1], ALU.subtract,
                                         ALU.mult))

            normalise(lambda t: xres[:, t, :])
            dve.sem_inc(x1_ready, 1)
            dve.wait_ge(sg_ready, 1)
            dve.wait_ge(y_added, STATES * BATCH)
            for k in range(KT):
                ins = v.tensor_tensor(gated[:, k * BATCH:(k + 1) * BATCH, :],
                                      sg.rearrange("p (b k) l -> p k b l", k=KT)[:, k],
                                      yT[:, k, :].rearrange("p (b l) -> p b l", b=BATCH), ALU.mult)
                link(ins)
            dve.sem_inc(gated_ready, 1)
            for j in range(4):
                dve.wait_ge(back_pe, j + 1)
                link(v.tensor_tensor(xres[:, 2 * j:2 * j + 2, :].rearrange("p t d -> p (t d)"),
                                     xres[:, 2 * j:2 * j + 2, :].rearrange("p t d -> p (t d)"), ps[:, j, :],
                                     ALU.add))
                for t in (2 * j, 2 * j + 1):
                    v.bn_stats(stats[:, t, :], xres[:, t, :])
                link(v.memset(nwt[:, 0:1], 0.0))
                for t in (2 * j, 2 * j + 1):
                    link(v.bn_aggr(mv[:, t, :], stats[:, t, :]))
            link(v.memset(x2, 0.0))
            normalise(lambda t: x2[:, t, 0:DM])
            dve.sem_inc(x2_ready, 1)

            dve.wait_ge(logit_pe, 1)
            link(v.tensor_tensor(lg, ps[:, 4, 0:TT * EXPERTS].rearrange("p (t e) -> p t e", e=EXPERTS),
                                 br_s[:, :].rearrange("p (o e) -> p o e", o=1).broadcast_to([P, TT, EXPERTS]),
                                 ALU.add))
            link(v.tensor_reduce(lmax, lg, axis=AX.X, op=ALU.max))
            lmax3 = lmax.rearrange("p (t o) -> p t o", o=1).broadcast_to([P, TT, EXPERTS])
            link(v.tensor_tensor(oh, lg, lmax3, ALU.is_ge))
            link(v.tensor_tensor(lg, lg, lmax3, ALU.subtract))
            link(v.tensor_copy(run, oh[:, :, 0]))
            v.tensor_copy(ohb[:, 0, :], oh[:, :, 0]).then_inc(logit_dve, 1)
            for e in range(1, EXPERTS):
                link(v.tensor_tensor(ohb[:, e, :], oh[:, :, e], run, ALU.is_gt))
                link(v.tensor_tensor(run, run, oh[:, :, e], ALU.max))
            dve.sem_inc(oh_ready, 1)
            dve.wait_ge(gate_exp, 1)
            link(v.tensor_reduce(lsum, ex, axis=AX.X, op=ALU.add))
            link(v.reciprocal(gate_w, lsum))
            link(v.tensor_copy(x2[:, :, DM:DM + 1], gate_w.rearrange("p (t o) -> p t o", o=1)))
            dve.sem_inc(x2_full, 1)
            dve.wait_ge(count_pe, 1)
            dve.wait_ge(consts, 4)
            v.tensor_copy(within.rearrange("p e t -> p (e t)"), ps[:, 5, 0:EXPERTS * TT])
            link(v.tensor_copy(total.rearrange("p e t -> p (e t)"), ps[:, 6, 0:EXPERTS * TT]))
            for e in range(EXPERTS):
                link(v.tensor_tensor_scan(out=incl[:, e, :], data0=ones32[:, 0:TT], data1=total[:, e, :],
                                          initial=0.0, op0=ALU.mult, op1=ALU.add))
            link(v.tensor_tensor(over, incl[:, :, TT - 1:TT].broadcast_to([P, EXPERTS, TT]),
                                 thr.rearrange("p (o t) -> p o t", o=1).broadcast_to([P, EXPERTS, TT]), ALU.is_gt))
            link(v.tensor_reduce(ntile, over, axis=AX.X, op=ALU.add))
            link(v.tensor_tensor_scan(out=tile_incl, data0=ones32[:, 0:EXPERTS], data1=ntile, initial=0.0,
                                      op0=ALU.mult, op1=ALU.add))
            link(v.tensor_tensor(tile0, tile_incl, ntile, ALU.subtract))
            link(v.tensor_tensor(within, within, incl, ALU.add))
            link(v.tensor_tensor(within, within, total, ALU.subtract))
            link(v.scalar_tensor_tensor(out=within, in0=tile0.rearrange("p (e o) -> p e o", o=1)
                                        .broadcast_to([P, EXPERTS, TT]), scalar=float(P), in1=within,
                                        op0=ALU.mult, op1=ALU.add))
            link(v.tensor_tensor(within, within, ohb, ALU.mult))
            link(v.tensor_reduce(pos, within.rearrange("p e t -> p t e"), axis=AX.X, op=ALU.add))
            for t in range(TT):
                v.tensor_scalar(onehot[t], iota16, pos[:, t:t + 1], None, ALU.is_equal).then_inc(hot_ready, 1)
            link(v.tensor_scalar(e_of, slot_no, tile0[:, 1:2], None, ALU.is_ge))
            for e in range(2, EXPERTS):
                link(v.scalar_tensor_tensor(out=e_of, in0=slot_no, scalar=tile0[:, e:e + 1], in1=e_of,
                                            op0=ALU.is_ge, op1=ALU.add))
            link(v.tensor_copy(e_int, e_of))
            dve.wait_ge(idx_pe, 1)
            link(v.tensor_scalar_add(idx, ps[:, 7, 0:SLOTS], float(FAR)))
            dve.sem_inc(idx_ready, 1)

            def make_h(s):
                dve.wait_ge(ge_ready, s + 1)
                v.tensor_tensor(hcur, ge, ps[:, 2:4, :].rearrange("p b c -> p (b c)"), ALU.mult).then_inc(h_ready, 1)

            def finish_rows(s):
                row = rows_s[:, bass.ds(s, 1), 0:DM].rearrange("p o d -> p (o d)")
                gate = rows_s[:, bass.ds(s, 1), DM:DM + 1].rearrange("p o d -> p (o d)")
                at = [ROW_STEPS * s]

                def step(ins):
                    at[0] = at[0] + 1
                    ins.then_inc(row_order, 1)
                    dve.wait_ge(row_order, at[0])

                dve.wait_ge(row_ready, s + 1)
                dve.wait_ge(y_done, s + 1)
                step(v.scalar_tensor_tensor(out=zrow, in0=ps[:, 6, 0:DM], scalar=gate, in1=row, op0=ALU.mult,
                                            op1=ALU.add))
                step(v.bn_stats(stats[:, 0, :], zrow))
                dve.sem_inc(dve_mark, 1)
                step(v.bn_aggr(mv[:, 0, :], stats[:, 0, :]))
                dve.sem_inc(z_ready, 1)
                step(v.tensor_scalar_add(ve, mv[:, 0, 1:2], EPS))
                step(v.tensor_scalar(rs.bitcast(I32), ve.bitcast(I32), 1, None, ALU.logical_shift_right))
                step(v.tensor_scalar(rs.bitcast(I32), rs.bitcast(I32), -1.0, float(RSQRT_SEED), ALU.mult, ALU.add))
                step(v.tensor_scalar_mul(ve, ve, -0.5))
                for _ in range(3):
                    step(v.scalar_tensor_tensor(out=nw, in0=rs, scalar=ve, in1=rs, op0=ALU.mult, op1=ALU.mult))
                    step(v.scalar_tensor_tensor(out=rs, in0=nw, scalar=1.5, in1=rs, op0=ALU.add, op1=ALU.mult))
                v.tensor_scalar(row, zrow, mv[:, 0, 0:1], rs, ALU.subtract, ALU.mult).then_inc(row_ready, 1)

            dve.sem_inc(row_ready, 1)
            dve.sem_inc(z_ready, 1)
            ve, rs, nw = veps[:, 0:1], rstd[:, 0:1], nwt[:, 0:1]
            ROW_STEPS = 13
            make_h(0)
            with dve.Fori(1, SLOTS) as s:
                make_h(s)
                finish_rows(s - 1)
            finish_rows(SLOTS - 1)


_INS = ["x", "ctx_1024", "L0_attn_wq", "L0_attn_wk", "L0_attn_wv", "L0_attn_wo", "L0_attn_rel_pos",
        "L0_xattn_in_proj_w", "L0_xattn_conv_w", "L0_xattn_conv_b", "L0_xattn_x_proj_w", "L0_xattn_dt_proj_w",
        "L0_xattn_dt_proj_b", "L0_xattn_A_log", "L0_xattn_D", "L0_ffn_Wr", "L0_ffn_br", "L0_ffn_Wg", "L0_ffn_Wu",
        "L0_ffn_Wd"]


def kernel(**inputs):
    import numpy as _np
    import concourse.bacc as _bacc
    from concourse.bass_utils import run_bass_kernel_spmd as _run

    nc = _bacc.Bacc("TRN2", target_bir_lowering=False, num_devices=1)
    arrays, args = {}, []
    for name in _INS:
        a = _np.ascontiguousarray(inputs[name])
        arrays[f"in_{name}"] = a
        args.append(nc.dram_tensor(f"in_{name}", a.shape, mybir.dt.from_np(a.dtype), kind="ExternalInput").ap())
    args.append(nc.dram_tensor("out_0", (BATCH, SEQ, DM), F32, kind="ExternalOutput").ap())
    decoder_layer(nc, *args)
    r = _run(nc, [arrays], core_ids=[0])
    return r.results[0]["out_0"]
```

```python
from contextlib import ExitStack

import concourse.bass as bass
from concourse import mybir

F32 = mybir.dt.float32
BF16 = mybir.dt.bfloat16
F16 = mybir.dt.float16
I32 = mybir.dt.int32
U32 = mybir.dt.uint32
ALU = mybir.AluOpType
ACT = mybir.ActivationFunctionType
AX = mybir.AxisListType

P = 128
BATCH, SEQ, DM = 4, 256, 256
TOK = BATCH * SEQ
TT = TOK // P
KT = DM // P
HEADS, DH = 32, 8
HALF = 512
DC = 128
STATES, TAPS, RANK = 16, 4, 8
PAD = TAPS - 1
PB = PAD + SEQ
TABLE = 127
ROWS = 6 * DH
QUADS = HEADS // 4
VW = DH + 1
SPREAD = 2 * SEQ - 1
QB = P // 2
EXPERTS, DFF = 4, 1024
FT = DFF // P
SLOTS = TT + EXPERTS - 1
EPS = 1e-5
POOL_UNITS = 3 * STATES
KEEP_WARM = 60
LOG1P = [0.99999994, -0.499994934, 0.333190948, -0.24842976, 0.191059828, -0.136631951, 0.0782253519,
         -0.0295048691, 0.00523260189]
RSQRT_SEED = 0x5F3759DF
FAR = 2048


def decoder_layer(nc, x, ctx_in, wq, wk, wv, wo, rel_pos, in_proj_w, conv_w, conv_b, x_proj_w, dt_proj_w,
                  dt_proj_b, A_log, D, Wr, br, Wg, Wu, Wd, out):
    with ExitStack() as stack:
        def sb(name, shape, dt=F32):
            return stack.enter_context(nc.sbuf_tensor(name, shape, dt))

        def sem(name):
            return stack.enter_context(nc.semaphore(name))

        def dram(name, shape, dt):
            return nc.dram_tensor(name, shape, dt, kind="Internal").ap()

        diag_d = dram("diag_d", (1, SPREAD), F32)
        qp_d = [dram(f"qp{i}_d", (DM, TOK), BF16) for i in range(3)]
        kp_d = [dram(f"kp{i}_d", (DM, TOK), BF16) for i in range(3)]
        x2_d = dram("x2_d", (TOK, DM), F32)

        xres = sb("xres", [P, TT, DM])
        identf = sb("identf", [P, P])
        flip = sb("flip", [P, P], F16)
        woT = sb("woT", [P, KT, DM])
        vaug = sb("vaug", [P, TT, HEADS, VW])
        flip2 = sb("flip2", [P, QB], F16)
        hank_hi = sb("hank_hi", [P, KT, SEQ], F16)
        hank2 = sb("hank2", [P, SEQ // QB, SEQ], F16)
        yT = sb("yT", [P, KT, TOK])
        wr_s = sb("wr_s", [P, KT, EXPERTS])
        br_s = sb("br_s", [P, EXPERTS])
        stats = sb("stats", [P, TT, 6])
        mv = sb("mv", [P, TT, 2])
        rstd = sb("rstd", [P, TT])
        nwt = sb("nwt", [P, TT])
        veps = sb("veps", [P, TT])
        ARENA = 41 * 1024
        arena = sb("arena", [P, ARENA])
        top = [0]

        def carve(cols, *shape, dt=F32, rows=P):
            a = arena[0:rows, top[0]:top[0] + cols]
            top[0] += cols
            assert top[0] <= ARENA, top[0]
            if dt != F32:
                a = a.bitcast(dt)
            if len(shape) == 2:
                a = a.rearrange("p (a b) -> p a b", a=shape[0])
            if len(shape) == 3:
                a = a.rearrange("p (a b c) -> p a b c", a=shape[0], b=shape[1])
            return a

        stacks = [carve(HEADS // 2 * SEQ // 2, HEADS // 2, SEQ, dt=BF16) for _ in range(4)]
        qst, kst = stacks[0::2], stacks[1::2]
        stacks_top = top[0]
        prob = [carve(4 * SEQ) for _ in range(4)]
        ctxS = [carve(QUADS * SEQ, QUADS, SEQ) for _ in range(2)]
        ctxn = carve(DM)
        ctxnT = carve(KT * P)
        negm = [carve(2 * HEADS, 2, HEADS) for _ in range(2)]
        negmT = [carve(SEQ // 2, dt=BF16, rows=HEADS // 2) for _ in range(2)]
        rcp = carve(16)
        acol = carve(KT * STATES, KT, STATES)
        lg = carve(TT * EXPERTS, TT, EXPERTS)
        weights_at = stacks_top + 4096 + 4096 + 1024
        assert top[0] <= weights_at
        top[0] = weights_at
        wg_s = carve(EXPERTS * KT * DFF)
        wu_s = carve(EXPERTS * KT * DFF)
        wd_s = carve(EXPERTS * FT * DM)
        weights_end = top[0]
        late_at = weights_at + (EXPERTS + 1) * KT * DFF
        top[0] = late_at
        dts = carve(KT * TOK, KT, TOK)
        dtu_at = top[0]
        dtu = carve(KT * TOK, KT, TOK)
        bc3 = carve(TOK, 2, TOK, dt=BF16, rows=96)
        sel = carve(STATES * P // 2, STATES, P, dt=BF16, rows=96)
        tiles_at = top[0]
        dA = [carve(HALF, KT, SEQ) for _ in range(4)]
        dBu = [carve(HALF, KT, SEQ) for _ in range(2)]
        hst = [carve(HALF, KT, SEQ) for _ in range(4)]
        bcs = [carve(2 * SEQ, 2, SEQ) for _ in range(3)]
        gate_at = weights_end - 3 * KT * SEQ
        assert top[0] <= gate_at and gate_at >= weights_end - FT * DM
        top[0] = gate_at
        sg = carve(KT * SEQ, KT, SEQ)
        gated = carve(KT * SEQ, KT, SEQ)
        x2T = carve(KT * SEQ, KT, SEQ)
        top[0] = stacks_top // 2
        w_raw = carve(4 * KT * DM, 4 * KT, DM)
        top[0] = stacks_top // 2
        hankel = carve(KT * SEQ, KT, SEQ)
        hankel2 = carve(SEQ // QB * SEQ, SEQ // QB, SEQ)
        assert top[0] <= stacks_top // 2 + 4 * KT * DM
        top[0] = stacks_top // 2 + 4 * KT * DM
        ctx_tok = carve(TT * DC, TT, DC)
        ctxT = carve(TOK)
        top[0] = stacks_top
        parts = [[carve(KT * TOK // 2, KT, TOK, dt=BF16) for _ in range(3)] for _ in range(2)]
        relrow = carve(TABLE * DH, TABLE, DH, rows=1)
        diag = carve(SPREAD + 1, rows=1)
        xpw = carve(DM, rows=RANK + 2 * STATES)
        xpB = carve(KT * 96, KT, 96)
        xpC = carve(KT * 96, KT, 96)
        xpD = carve(KT * RANK, KT, RANK)
        dtw = carve(KT * RANK, KT, RANK)
        dtwT = carve(DM, rows=RANK)
        cw = carve(KT * TAPS, KT, TAPS)
        cb = carve(KT)
        dtb = carve(KT)
        alog = carve(KT * STATES, KT, STATES)
        dcol = carve(KT)
        assert top[0] <= weights_at - 256
        top[0] = weights_at
        xin = carve(KT * BATCH * PB, KT, BATCH, PB)
        u = carve(KT * TOK, KT, TOK)
        ta = carve(KT * TOK, KT, TOK)
        bcf = carve(2 * TOK, 2, TOK, rows=96)
        dtlow = carve(TOK, rows=RANK)
        assert top[0] <= late_at
        top[0] = weights_at
        spt = carve(KT * TOK, KT, TOK)
        top[0] = dtu_at
        wT = carve(3 * KT * DM, 3 * KT, DM)
        inw = carve(KT * DC, KT, DC)
        inwT = carve(DM)
        assert top[0] <= dtu_at + KT * TOK
        top[0] = tiles_at
        rest = [carve(KT * TOK, KT, TOK) for _ in range(2)]
        xT = carve(KT * TOK, KT, TOK)
        tb = carve(KT * TOK, KT, TOK)
        assert top[0] <= weights_end
        top[0] = 0
        ex = carve(TT * EXPERTS, TT, EXPERTS)
        lmax = carve(TT)
        lsum = carve(TT)
        gate_w = carve(TT)
        oh = carve(TT * EXPERTS, TT, EXPERTS)
        ohb = carve(EXPERTS * TT // 2, EXPERTS, TT, dt=BF16)
        run = carve(TT)
        within = carve(EXPERTS * TT, EXPERTS, TT)
        total = carve(EXPERTS * TT, EXPERTS, TT)
        incl = carve(EXPERTS * TT, EXPERTS, TT)
        thr = carve(TT)
        over = carve(EXPERTS * TT, EXPERTS, TT)
        ntile = carve(EXPERTS)
        tile_incl = carve(EXPERTS)
        tile0 = carve(EXPERTS)
        ones32 = carve(32)
        pos = carve(TT)
        tile_no = carve(SLOTS)
        e_of = carve(SLOTS)
        e_int = carve(SLOTS, dt=I32)
        idx = carve(SLOTS, dt=U32)
        ltri = carve(P // 2, dt=BF16)
        ones_b = carve(P // 2, dt=BF16)
        tokg = carve(2 * TT * 2, TT, 4, dt=F16)
        gslot = carve(SLOTS)
        iota16 = carve(SLOTS * P // 2, dt=F16)
        assert top[0] <= stacks_top // 2
        top[0] = stacks_top // 2
        onehot = [carve(SLOTS * P // 2, dt=F16) for _ in range(TT)]
        xrow = carve(DM)
        xcur = carve(KT * P, KT, P)
        ge = carve(DFF)
        hcur = carve(DFF)
        hT = carve(FT * P, FT, P)
        zrow = carve(DM)
        assert top[0] <= weights_at
        rows_s = sb("rows_s", [P, SLOTS, DM])
        ps = stack.enter_context(nc.psum_tensor("ps", [P, 8, HALF], F32))

        ld_ctx = sem("ld_ctx")
        ld_x = sem("ld_x")
        ld_w = sem("ld_w")
        ld_misc = sem("ld_misc")
        consts = sem("consts")
        pe_fill = sem("pe_fill")
        act_evac = sem("act_evac")
        dve_evac = sem("dve_evac")
        conv_done = sem("conv_done")
        conv_tanh = sem("conv_tanh")
        u_ready = sem("u_ready")
        split_ready = sem("split_ready")
        dbu_ready = sem("dbu_ready")
        dbu_shared = sem("dbu_shared")
        row_order = sem("row_order")
        sp_exp = sem("sp_exp")
        hc_ready = sem("hc_ready")
        a_exp = sem("a_exp")
        dt_ready = sem("dt_ready")
        scan_in = sem("scan_in")
        bc_ready = sem("bc_ready")
        bc_taken = sem("bc_taken")
        da_ready = sem("da_ready")
        scanned = sem("scanned")
        y_added = sem("y_added")
        dve_mark = sem("dve_mark")
        dve_order = sem("dve_order")
        act_order = sem("act_order")
        pool_order = sem("pool_order")
        part_ready = [[sem(f"part_ready{n}{i}") for i in range(3)] for n in range(2)]
        part_out = [sem(f"part_out{i}") for i in range(3)]
        diag_ready = sem("diag_ready")
        diag_out = sem("diag_out")
        hank_in = sem("hank_in")
        hank_ready = sem("hank_ready")
        ones_rows = sem("ones_rows")
        stack_in = [[sem(f"stack_in{b}{h}") for h in range(2)] for b in range(2)]
        a_scores = sem("a_scores")
        a_max = sem("a_max")
        m_ready = [sem(f"m_ready{h}") for h in range(2)]
        m_in = [sem(f"m_in{h}") for h in range(2)]
        b_scores = sem("b_scores")
        p_ready = sem("p_ready")
        pv_done = sem("pv_done")
        pv_out = sem("pv_out")
        tail_pe = sem("tail_pe")
        tail_dve = sem("tail_dve")
        x1_ready = sem("x1_ready")
        sg_ready = sem("sg_ready")
        gated_ready = sem("gated_ready")
        x2_ready = sem("x2_ready")
        logit_dve = sem("logit_dve")
        gate_exp = sem("gate_exp")
        oh_ready = sem("oh_ready")
        count_pe = sem("count_pe")
        hot_ready = sem("hot_ready")
        idx_pe = sem("idx_pe")
        x2_out = sem("x2_out")
        idx_ready = sem("idx_ready")
        rows_in = [sem(f"rows_in{s}") for s in range(SLOTS)]
        xrow_ready = sem("xrow_ready")
        xt_pe = sem("xt_pe")
        w_in = sem("w_in")
        xcur_ready = sem("xcur_ready")
        gu_done = sem("gu_done")
        ge_ready = sem("ge_ready")
        h_ready = sem("h_ready")
        ht_pe = sem("ht_pe")
        ht_ready = sem("ht_ready")
        y_done = sem("y_done")
        z_ready = sem("z_ready")
        row_ready = sem("row_ready")
        out_done = sem("out_done")
        block = stack.enter_context(nc.Block())

        F_CTX, F_INW, F_DTW, F_XIN, F_XT, F_WT, F_Q, F_V, F_LOW, F_DT, F_K, F_B, F_C = \
            0, 2, 3, 4, 8, 12, 16, 20, 24, 26, 30, 34, 36
        FILLS = 38
        DVE_FILLS = [F_INW] + list(range(F_Q, F_V)) + list(range(F_K, F_B))
        N_CTX = 9 * 16

        def wait_evac(eng, j):
            if j in DVE_FILLS:
                eng.wait_ge(dve_evac, DVE_FILLS.index(j) + 1)
            else:
                eng.wait_ge(act_evac, j + 1 - sum(i < j for i in DVE_FILLS))

        A_UNITS = {slot: [] for slot in [(0, -2), (0, -1)] + [(b, qd) for b in range(BATCH) for qd in range(QUADS)]}
        for b in range(BATCH):
            for i in range(32):
                if b == 0:
                    slot = (0, (-2, -2, -1, 0, 1)[i // 8 if i < 16 else 2 + (i - 16) // 6])
                else:
                    slot = (b - 1, i // 4 if i < 16 else 4 + (i - 16) // 6)
                A_UNITS[slot].append((b, i // 2, i % 2))
        A_DONE, count = {}, 0
        for slot in A_UNITS:
            for n, (b, pair, qt) in enumerate(A_UNITS[slot]):
                A_UNITS[slot][n] = (b, pair, qt, count)
                count += 1
                A_DONE[b, pair // 8] = count

        def quarter(units, i):
            return units[len(units) * i // 4:len(units) * (i + 1) // 4]

        END_BANKS = (7, 0, 1)

        def by_pool(m):
            return m % 4 == 3 and m < POOL_UNITS

        def wait_dbu(eng, m):
            if by_pool(m):
                eng.wait_ge(dbu_shared, m // 4 + 1)
            else:
                eng.wait_ge(dbu_ready, m + 1 - sum(by_pool(i) for i in range(m)))

        QKC = [(0, 0), (1, 0), (2, 0), (0, 1), (1, 1), (0, 2)]
        SCALE = float(DH) ** -0.5

        @block.sync
        def _(sp):
            sp.dma_start(ctx_tok, ctx_in.rearrange("b (t p) d -> p (b t) d", p=P)).then_inc(ld_ctx, 16)
            sp.dma_start(inw, in_proj_w.rearrange("(k p) d -> p k d", p=P)).then_inc(ld_ctx, 16)
            sp.dma_start(xpw, x_proj_w).then_inc(ld_ctx, 16)
            sp.dma_start(dtw, dt_proj_w.rearrange("(k p) r -> p k r", p=P)).then_inc(ld_ctx, 16)
            sp.dma_start(cw, conv_w.rearrange("(k p) o t -> p k (o t)", p=P)).then_inc(ld_ctx, 16)
            sp.dma_start(alog, A_log.rearrange("(k p) n -> p k n", p=P)).then_inc(ld_ctx, 16)
            with nc.allow_non_contiguous_dma(reason="three short vectors"):
                sp.dma_start(cb, conv_b.rearrange("(k p) -> p k", p=P)).then_inc(ld_ctx, 16)
                sp.dma_start(dtb, dt_proj_b.rearrange("(k p) -> p k", p=P)).then_inc(ld_ctx, 16)
                sp.dma_start(dcol, D.rearrange("(k p) -> p k", p=P)).then_inc(ld_ctx, 16)
            sp.dma_start(xres[:, :, :], x.rearrange("b (t p) d -> p (b t) d", p=P)).then_inc(ld_x, 16)
            for n, w in enumerate((wq, wk, wv, wo)):
                sp.dma_start(w_raw[:, n * KT:(n + 1) * KT, :],
                             w.rearrange("(k p) d -> p k d", p=P)).then_inc(ld_w, 16)
            sp.dma_start(relrow, rel_pos.rearrange("(o t) d -> o t d", o=1)).then_inc(ld_misc, 16)
            sp.dma_start(wr_s[:, :, :], Wr.rearrange("(k p) e -> p k e", p=P)).then_inc(ld_misc, 16)
            sp.dma_start(br_s[:, :],
                         br.rearrange("(o e) -> o e", o=1).broadcast_to([P, EXPERTS])).then_inc(ld_misc, 16)
            sp.wait_ge(diag_ready, 1)
            sp.dma_start(diag_d, diag[:, 0:SPREAD]).then_inc(diag_out, 16)
            sp.wait_ge(diag_out, 16)
            sp.wait_ge(pe_fill, F_WT + 4)
            for half in range(2):
                sp.dma_start(hankel2[QB * half:QB * (half + 1), :, :],
                             bass.AP(tensor=diag_d.tensor, offset=0,
                                     ap=[[1, QB], [QB, SEQ // QB], [1, SEQ]])).then_inc(hank_in, 16)
            for qt in range(KT):
                sp.dma_start(hankel[:, qt, :],
                             bass.AP(tensor=diag_d.tensor, offset=P * (1 - qt),
                                     ap=[[1, P], [1, SEQ]])).then_inc(hank_in, 16)
            for n, dst in enumerate((qp_d, kp_d)):
                for i in range(3):
                    sp.wait_ge(part_ready[n][i], 4 if i == 0 else 1)
                    sp.dma_start(dst[i].rearrange("(m p) t -> p m t", p=P), parts[n][i]).then_inc(part_out[i], 16)
            for i in range(3):
                sp.wait_ge(part_out[i], 32)

            def load_stack(b, hh):
                for c, (qi, ki) in enumerate(QKC):
                    lo = 64 * hh + DH * c
                    for st, src, i in ((qst, qp_d, qi), (kst, kp_d, ki)):
                        sp.dma_start(st[b % 2][lo:lo + DH, :, :],
                                     src[i][hh * P:(hh + 1) * P, b * SEQ:(b + 1) * SEQ]
                                     .rearrange("(h d) t -> d h t", d=DH)).then_inc(stack_in[b % 2][hh], 16)

            def send_max(b, hh):
                sp.wait_ge(m_ready[hh], b + 1)
                sp.dma_start(qst[b % 2][64 * hh + ROWS:64 * hh + ROWS + 1, :, :], negmT[hh]).then_inc(m_in[hh], 16)

            for b in range(2):
                sp.wait_ge(ones_rows, b + 1)
                if b:
                    sp.wait_ge(hank_ready, 1)
                for hh in range(2):
                    load_stack(b, hh)
            send_max(0, 0)
            sp.wait_ge(scan_in, 1)
            sp.wait_ge(split_ready, BATCH)

            def load_gate_up(dst, src, e):
                for k in range(KT):
                    sp.dma_start(dst[:, (e * KT + k) * DFF:(e * KT + k + 1) * DFF],
                                 src[e, k * P:(k + 1) * P, :]).then_inc(w_in, 16)

            early = [(wg_s, Wg, e) for e in range(EXPERTS)] + [(wu_s, Wu, 0)]

            def load_down(e):
                sp.dma_start(wd_s[:, e * FT * DM:(e + 1) * FT * DM].rearrange("p (k f) -> p k f", k=FT),
                             Wd[e].rearrange("(k p) f -> p k f", p=P)).then_inc(w_in, 16)

            def store_x2(b):
                sp.wait_ge(x2_ready, b + 1)
                sp.dma_start(x2_d.rearrange("(t p) c -> p t c", p=P)[:, 2 * b:2 * b + 2, :],
                             xres[:, 2 * b:2 * b + 2, :]).then_inc(x2_out, 16)

            for b in range(BATCH):
                if b >= 2:
                    store_x2(b - 2)
                for hh in range(2):
                    if hh == 1 and b + 1 < BATCH:
                        send_max(b + 1, 0)
                        send_max(b + 1, 1)
                    if (b, hh) == (0, 0):
                        send_max(0, 1)
                    if b + 2 < BATCH:
                        sp.wait_ge(b_scores, 4 * (QUADS * b + 4 * (hh + 1)))
                        load_stack(b + 2, hh)
                    if early:
                        load_gate_up(*early.pop(0))
            sp.wait_ge(y_added, STATES * BATCH)
            for e in range(1, EXPERTS):
                load_gate_up(wu_s, Wu, e)
            for e in range(EXPERTS - 1):
                load_down(e)
            store_x2(BATCH - 2)
            store_x2(BATCH - 1)
            sp.wait_ge(oh_ready, 1)
            load_down(EXPERTS - 1)
            sp.wait_ge(out_done, 16 * SLOTS)

        @block.gpsimd
        def _(pool):
            g = nc.gpsimd
            order = [0]

            def link(ins):
                order[0] += 1
                ins.then_inc(pool_order, 1)
                pool.wait_ge(pool_order, order[0])

            link(g.memset(identf[:, :], 0.0))
            g.affine_select(out=identf[:, :], in_=identf[:, :], compare_op=ALU.not_equal, fill=1.0, base=0,
                            pattern=[[-1, P]], channel_multiplier=1).then_inc(consts, 1)
            g.memset(xpB, 0.0)
            g.memset(xpC, 0.0)
            g.memset(xin[:, :, :, 0:PAD], 0.0).then_inc(consts, 1)
            link(g.memset(flip[:, :], 0.0))
            g.affine_select(out=flip[:, :], in_=flip[:, :], compare_op=ALU.not_equal, fill=1.0, base=-(P - 1),
                            pattern=[[1, P]], channel_multiplier=1)
            link(g.memset(flip2[:, :], 0.0))
            for base in (1 - QB, 1 - 2 * QB):
                link(g.affine_select(out=flip2[:, :], in_=flip2[:, :], compare_op=ALU.not_equal, fill=1.0,
                                     base=base, pattern=[[1, QB]], channel_multiplier=1))
            link(g.memset(sel, 0.0))
            for k in range(3):
                link(g.affine_select(out=sel, in_=sel, compare_op=ALU.not_equal, fill=1.0, base=-32 * k,
                                     pattern=[[-1, STATES], [0, P]], channel_multiplier=1))
            g.memset(vaug[:, :, :, DH:VW], 1.0)
            link(g.memset(rows_s[:, :, :], 0.0))
            for buf in range(2):
                if buf:
                    pool.wait_ge(pe_fill, F_Q)
                for lo in (32, 96):
                    ins = g.memset(kst[buf][lo:lo + 32, :, :], 1.0)
                    link(ins)
                pool.sem_inc(ones_rows, 1)
                if buf == 0:
                    pool.sem_inc(consts, 1)
            for k in range(KT):
                pool.wait_ge(u_ready, k + 1)
                link(g.tensor_scalar(yT[:, k, :], u[:, k, :], dcol[:, k:k + 1], None, ALU.mult))

            def routing_constants():
                pool.wait_ge(b_scores, 4 * 3 * QUADS)
                link(g.iota(thr, pattern=[[P, TT]], base=0, channel_multiplier=0,
                            allow_small_or_imprecise_dtypes=True))
                link(g.iota(tile_no, pattern=[[1, SLOTS]], base=0, channel_multiplier=0,
                            allow_small_or_imprecise_dtypes=True))
                link(g.iota(iota16, pattern=[[1, SLOTS * P]], base=0, channel_multiplier=0,
                            allow_small_or_imprecise_dtypes=True))
                link(g.iota(tokg[:, :, 0], pattern=[[P, TT]], base=-FAR, channel_multiplier=1,
                            allow_small_or_imprecise_dtypes=True))
                link(g.memset(ones32, 1.0))
                link(g.memset(ones_b, 1.0))
                link(g.memset(ltri, 1.0))
                g.affine_select(out=ltri, in_=ltri, compare_op=ALU.is_gt, fill=0.0, base=0,
                                pattern=[[1, P]], channel_multiplier=-1).then_inc(consts, 1)

            for b in range(BATCH):
                cols = slice(b * SEQ, (b + 1) * SEQ)
                if b % 2 == 0:
                    wait_evac(pool, F_C + b // 2)
                link(g.tensor_tensor(bcf[:, :, cols], bcf[:, :, cols], bc3[:, :, cols], ALU.subtract))
                link(g.tensor_copy(bc3[32:64, :, cols], bcf[32:64, :, cols]))
                link(g.tensor_copy(bc3[64:96, :, cols], bcf[64:96, :, cols]))
                link(g.tensor_tensor(bc3[64:96, :, cols], bcf[64:96, :, cols], bc3[64:96, :, cols], ALU.subtract))
                if b:
                    pool.wait_ge(dt_ready, 1)
                    link(g.tensor_tensor(dtu[:, :, cols], dts[:, :, cols], u[:, :, cols], ALU.mult))
                pool.sem_inc(split_ready, 1)
            pool.wait_ge(scan_in, 1)
            for m in range(STATES * BATCH):
                b = m // STATES
                if m == 3 * STATES + 8:
                    routing_constants()
                if by_pool(m + 1):
                    n = m + 1
                    pool.wait_ge(bc_taken, n + 1)
                    if n >= 2:
                        pool.wait_ge(scanned, n + 3)
                    cols = slice(n // STATES * SEQ, (n // STATES + 1) * SEQ)
                    g.tensor_tensor(dBu[n % 2], dtu[:, :, cols], bcs[n % 3][:, 0:1, :].broadcast_to([P, KT, SEQ]),
                                    ALU.mult).then_inc(dbu_shared, 1)
                h = hst[m % 4]
                pool.wait_ge(scanned, m + 5)
                pool.wait_ge(bc_taken, m + 1)
                g.tensor_tensor(h, h, bcs[m % 3][:, 1, :].rearrange("p (o l) -> p o l", o=1).broadcast_to([P, KT, SEQ]),
                                ALU.mult).then_inc(hc_ready, 1)
                pool.wait_ge(hc_ready, m + 1)
                y = yT[:, :, b * SEQ:(b + 1) * SEQ]
                if m:
                    pool.wait_ge(y_added, m)
                g.tensor_tensor(y, y, h, ALU.add).then_inc(y_added, 1)

            def gather(s):
                g.indirect_dma_start(out=rows_s[:, s, :], out_offset=None, in_=x2_d,
                                     in_offset=bass.IndirectOffsetOnAxis(ap=idx[:, s:s + 1], axis=0),
                                     bounds_check=TOK - 1, oob_is_err=False).then_inc(rows_in[s], 16)

            def hand_row(s):
                pool.wait_ge(rows_in[s], 16)
                if s:
                    pool.wait_ge(xt_pe, s)
                g.tensor_copy(xrow, rows_s[:, s, :]).then_inc(xrow_ready, 1)

            def scatter(s):
                pool.wait_ge(row_ready, s + 2)
                g.indirect_dma_start(out=out.rearrange("b s d -> (b s) d"),
                                     out_offset=bass.IndirectOffsetOnAxis(ap=idx[:, s:s + 1], axis=0),
                                     in_=rows_s[:, s, :], in_offset=None,
                                     bounds_check=TOK - 1, oob_is_err=False).then_inc(out_done, 16)

            pool.wait_ge(x2_out, 16 * BATCH)
            pool.wait_ge(idx_ready, 1)
            for s in range(3):
                gather(s)
            hand_row(0)
            for s in range(3, 7):
                gather(s)
            hand_row(1)
            for s in range(7, SLOTS):
                gather(s)
            for s in range(2, SLOTS):
                hand_row(s)
                if s >= 3:
                    scatter(s - 3)
            for s in range(SLOTS - 3, SLOTS):
                scatter(s)

        @block.tensor
        def _(pe):
            mm = nc.tensor.matmul

            def begin(j):
                if j >= 8:
                    wait_evac(pe, j - 8)
                return j % 8

            pe.wait_ge(consts, 1)
            pe.wait_ge(ld_ctx, N_CTX)
            for j in range(2):
                for i in range(4):
                    last = nc.tensor.transpose(ps[:, j, i * P:(i + 1) * P], ctx_tok[:, 4 * j + i, :], identf[:, :])
                last.then_inc(pe_fill, 1)
            R = RANK + 2 * STATES
            for k in range(KT):
                nc.tensor.transpose(ps[:, 2, k * P:(k + 1) * P], inw[:, k, :], identf[:, :])
            for k in range(KT):
                last = nc.tensor.transpose(ps[:, 2, DM + k * R:DM + (k + 1) * R], xpw[:, k * P:(k + 1) * P],
                                           identf[0:R, 0:R])
            last.then_inc(pe_fill, 1)
            for k in range(KT):
                last = nc.tensor.transpose(ps[0:RANK, 3, k * P:(k + 1) * P], dtw[:, k, :], identf[:, :])
            last.then_inc(pe_fill, 1)
            wait_evac(pe, 1)
            wait_evac(pe, F_INW)
            for k in range(KT):
                for hf in range(2):
                    bank = begin(F_XIN + 2 * k + hf)
                    mm(ps[:, bank, :], inwT[:, k * P:(k + 1) * P], ctxT[:, hf * HALF:(hf + 1) * HALF],
                       start=True, stop=True).then_inc(pe_fill, 1)
            pe.wait_ge(ld_x, 16)
            for k in range(KT):
                for hf in range(2):
                    bank = begin(F_XT + 2 * k + hf)
                    for i in range(4):
                        last = nc.tensor.transpose(ps[:, bank, i * P:(i + 1) * P],
                                                   xres[:, 4 * hf + i, k * P:(k + 1) * P], identf[:, :])
                    last.then_inc(pe_fill, 1)
            pe.wait_ge(ld_w, 64)
            for w in range(4):
                bank = begin(F_WT + w)
                for k in range(KT):
                    for o in range(KT):
                        at = k * DM + o * P
                        last = nc.tensor.transpose(ps[:, bank, at:at + P],
                                                   w_raw[:, w * KT + o, k * P:(k + 1) * P], identf[:, :])
                last.then_inc(pe_fill, 1)
            def project_x(w, f):
                for m in range(KT):
                    for hf in range(2):
                        bank = begin(f + 2 * m + hf)
                        for k in range(KT):
                            last = mm(ps[:, bank, :], wT[:, w * KT + k, m * P:(m + 1) * P],
                                      xT[:, k, hf * HALF:(hf + 1) * HALF], start=(k == 0), stop=(k == KT - 1))
                        last.then_inc(pe_fill, 1)

            wait_evac(pe, F_WT + 3)
            project_x(0, F_Q)
            for j in range(4):
                bank = begin(F_V + j)
                for t in range(2):
                    for k in range(KT):
                        last = mm(ps[:, bank, t * DM:(t + 1) * DM], xT[:, k, (2 * j + t) * P:(2 * j + t + 1) * P],
                                  wT[:, 2 * KT + k, :], start=(k == 0), stop=(k == KT - 1))
                last.then_inc(pe_fill, 1)
            pe.wait_ge(u_ready, KT)

            def project_u(f, w, rows):
                for hf in range(2):
                    bank = begin(f + hf)
                    for k in range(KT):
                        last = mm(ps[0:rows, bank, :], w[:, k, :], u[:, k, hf * HALF:(hf + 1) * HALF],
                                  start=(k == 0), stop=(k == KT - 1))
                    last.then_inc(pe_fill, 1)

            project_u(F_LOW, xpD, RANK)
            wait_evac(pe, F_LOW + 1)
            for k in range(KT):
                for hf in range(2):
                    bank = begin(F_DT + 2 * k + hf)
                    mm(ps[:, bank, :], dtwT[:, k * P:(k + 1) * P], dtlow[:, hf * HALF:(hf + 1) * HALF],
                       start=True, stop=True).then_inc(pe_fill, 1)
            project_x(1, F_K)
            project_u(F_B, xpB, 96)
            project_u(F_C, xpC, 96)
            wait_evac(pe, F_K + 3)
            pe.wait_ge(hank_ready, 1)

            def keep_warm(count, bank=7):
                for _ in range(count):
                    mm(ps[:, bank, :], flip[:, :], hank_hi[:, :, :].rearrange("p q k -> p (q k)"), start=True,
                       stop=True)

            keep_warm(KEEP_WARM)
            wait_evac(pe, FILLS - 1)

            def spread(m):
                b, n = m // STATES, m % STATES
                if m:
                    pe.wait_ge(bc_taken, m)
                if n == 0:
                    pe.wait_ge(split_ready, b + 1)
                for i in range(2):
                    last = mm(ps[:, 5, i * SEQ:(i + 1) * SEQ], sel[:, n, :],
                              bc3[:, i, b * SEQ:(b + 1) * SEQ], start=True, stop=True)
                last.then_inc(bc_ready, 1)

            pe.wait_ge(hank_ready, 1)

            def scores_a(b, pair, qt, n):
                bank = n % 2
                hh, h0 = pair // 8, 2 * pair % 16
                if n >= 2:
                    pe.wait_ge(a_max, n - 1)
                lo = 64 * hh
                for i in range(2):
                    mm(ps[:, bank, i * SEQ:(i + 1) * SEQ], qst[b % 2][lo:lo + ROWS, h0 + i, qt * P:(qt + 1) * P],
                       kst[b % 2][lo:lo + ROWS, h0 + i, :], start=(i == 0), stop=False, skip_group_check=True)
                mm(ps[:, bank, :].rearrange("p (h k) -> p h k", h=2), flip[:, :],
                   hank_hi[:, qt:qt + 1, :].broadcast_to([P, 2, SEQ]), start=False, stop=True,
                   skip_group_check=True).then_inc(a_scores, 1)

            def scores_b(b, qd, kt, pr):
                n = 4 * (QUADS * b + qd) + 2 * kt + pr
                if n >= 3:
                    pe.wait_ge(p_ready, n - 2)
                hh, h0 = qd // 4, 4 * qd % 16
                lo, hi = 64 * hh, 64 * hh + ROWS + 1
                bank = 2 + n % 3
                for i in range(2):
                    h = h0 + 2 * pr + i
                    mm(ps[:, bank, i * SEQ:(i + 1) * SEQ], kst[b % 2][lo:hi, h, kt * P:(kt + 1) * P],
                       qst[b % 2][lo:hi, h, :], start=(i == 0), stop=False, skip_group_check=True)
                view = ps[:, bank, :].rearrange("p (h q) -> p h q", h=2)
                for c in range(SEQ // QB):
                    last = mm(view[:, :, c * QB:(c + 1) * QB],
                              hank2[:, SEQ // QB - 1 - c, kt * P:(kt + 1) * P],
                              flip2[:, :].rearrange("p (o k) -> p o k", o=1).broadcast_to([P, 2, QB]),
                              start=False, stop=True, skip_group_check=True)
                last.then_inc(b_scores, 1)

            def weigh(b, qd):
                n = QUADS * b + qd
                pe.wait_ge(pv_out, n + 1)
                pe.wait_ge(p_ready, 4 * n + 4)
                for kt in range(KT):
                    for j in range(4):
                        last = mm(ps[32 * j:32 * j + VW, 6, 0:SEQ], vaug[:, 2 * b + kt, 4 * qd + j, :],
                                  prob[2 * (n % 2) + kt][:, j * SEQ:(j + 1) * SEQ],
                                  start=(kt == 0), stop=(kt == KT - 1), skip_group_check=True)
                last.then_inc(pv_done, 1)

            misc, ending = [0], [0]

            def misc_begin():
                if ending[0]:
                    ending[0] += 1
                    pe.wait_ge(tail_dve, misc[0] - (len(END_BANKS) - 1 if ending[0] > len(END_BANKS) else 0))
                elif misc[0]:
                    pe.wait_ge(tail_dve, misc[0])
                misc[0] += 1

            def bank():
                return END_BANKS[(ending[0] - 2) % len(END_BANKS)] if ending[0] else 7

            def all_out():
                pe.wait_ge(tail_dve, misc[0])

            def turn_max(b, hh):
                pe.wait_ge(a_max, A_DONE[b, hh])
                misc_begin()
                for qt in range(KT):
                    last = nc.tensor.transpose(ps[0:HEADS // 2, bank(), qt * P:(qt + 1) * P],
                                               negm[b % 2][:, qt, 16 * hh:16 * hh + 16], identf[:, :])
                last.then_inc(tail_pe, 1)

            def tail(b, step):
                qt, k = step // 4, step % 4
                if k < 2:
                    pe.wait_ge(pv_out, QUADS * (b + 1) + 1)
                else:
                    all_out()
                misc_begin()
                if k < 2:
                    for i in range(4):
                        last = nc.tensor.transpose(ps[:, bank(), i * P:(i + 1) * P],
                                                   ctxS[b % 2][:, 4 * k + i, qt * P:(qt + 1) * P], identf[:, :])
                elif k == 2:
                    for i in range(KT):
                        last = nc.tensor.transpose(ps[:, bank(), i * P:(i + 1) * P], ctx_rows(qt)[:, i * P:(i + 1) * P],
                                                   identf[:, :])
                else:
                    for i in range(KT):
                        last = mm(ps[:, bank(), 0:DM], ctx_cols(qt)[:, i * P:(i + 1) * P], woT[:, i, :], start=(i == 0),
                                  stop=(i == KT - 1))
                last.then_inc(tail_pe, 1)

            def ctx_rows(qt):
                return (prob[0] if qt and ending[0] else ctxn)[:, 0:DM]

            def ctx_cols(qt):
                return prob[0][:, DM:2 * DM] if qt and ending[0] else ctxnT

            def turn_back(b):
                pe.wait_ge(gated_ready, b + 1)
                misc_begin()
                for i in range(4):
                    lt, k = i // 2, i % 2
                    last = nc.tensor.transpose(ps[:, bank(), i * P:(i + 1) * P], gated[:, k, lt * P:(lt + 1) * P],
                                               identf[:, :])
                last.then_inc(tail_pe, 1)

            def turn_x2(b):
                pe.wait_ge(x2_ready, b + 1)
                misc_begin()
                for i in range(4):
                    k, lt = i // 2, i % 2
                    last = nc.tensor.transpose(ps[:, bank(), i * P:(i + 1) * P], xres[:, 2 * b + lt, k * P:(k + 1) * P],
                                               identf[:, :])
                last.then_inc(tail_pe, 1)

            def route(b):
                all_out()
                misc_begin()
                for lt in range(2):
                    for k in range(KT):
                        last = mm(ps[:, bank(), lt * EXPERTS:(lt + 1) * EXPERTS], x2T[:, k, lt * P:(lt + 1) * P],
                                  wr_s[:, k, :], start=(k == 0), stop=(k == KT - 1))
                last.then_inc(tail_pe, 1)

            pe.wait_ge(stack_in[0][0], 16 * 12)
            for unit in A_UNITS[0, -2]:
                scores_a(*unit)
                keep_warm(1)
            turn_max(0, 0)
            spread(0)
            pe.wait_ge(stack_in[0][1], 16 * 12)
            for unit in A_UNITS[0, -1]:
                scores_a(*unit)
            pe.wait_ge(tail_dve, 1)
            keep_warm(9)
            for b in range(BATCH):
                for qd in range(QUADS):
                    if qd % 4 == 0:
                        pe.wait_ge(m_in[qd // 4], 16 * (b + 1))
                    if qd in (0, 4) and b + 1 < BATCH:
                        pe.wait_ge(stack_in[(b + 1) % 2][qd // 4], 16 * 12 * ((b + 1) // 2 + 1))
                    for i in range(4):
                        m = 2 * (QUADS * b + qd) + i // 2 + 1
                        if i % 2 == 1 and m < STATES * BATCH:
                            spread(m)
                        for unit in quarter(A_UNITS[b, qd], i):
                            scores_a(*unit)
                        scores_b(b, qd, i // 2, i % 2)
                        if i == 1 and (b or qd):
                            weigh(b - (qd == 0), (qd - 1) % QUADS)
                        if b and 1 <= qd <= 4 and i % 2 == 1:
                            tail(b - 1, 2 * (qd - 1) + i // 2)
                        if b and (qd, i) == (6, 3):
                            turn_back(b - 1)
                        if (b, qd, i) == (0, 2, 3):
                            turn_max(0, 1)
                        if b + 1 < BATCH and (qd, i) in ((5, 1), (7, 1)):
                            turn_max(b + 1, qd // 7)
                        if b >= 2 and (qd, i) == (0, 3):
                            turn_x2(b - 2)
                        if b >= 2 and (qd, i) == (1, 2):
                            route(b - 2)
            weigh(BATCH - 1, QUADS - 1)
            ending[0] = 1
            for step in (0, 1, 4, 5):
                tail(BATCH - 1, step)
            turn_x2(BATCH - 2)
            for step in (2, 6, 3, 7):
                tail(BATCH - 1, step)
            route(BATCH - 2)
            pe.wait_ge(p_ready, 4 * QUADS * BATCH)
            keep_warm(16, 4)
            turn_back(BATCH - 1)
            keep_warm(16, 4)
            turn_x2(BATCH - 1)
            route(BATCH - 1)
            keep_warm(8, 4)

            pe.wait_ge(oh_ready, 1)
            pe.wait_ge(consts, 4)
            oh_cols = ohb.rearrange("p e t -> p (e t)")
            mm(ps[:, 5, 0:EXPERTS * TT], ltri, oh_cols, start=True, stop=True)
            mm(ps[:, 6, 0:EXPERTS * TT], ones_b, oh_cols, start=True, stop=True).then_inc(count_pe, 1)
            keep_warm(20, 4)
            for t in range(TT):
                pe.wait_ge(hot_ready, t + 1)
                for s in range(SLOTS):
                    last = mm(ps[:, 7, 4 * s:4 * s + 3], onehot[t][:, s * P:(s + 1) * P], tokg[:, t, 0:3],
                              start=(t == 0 and s == 0), stop=(t == TT - 1), skip_group_check=True)
            last.then_inc(idx_pe, 1)

            def turn_x(s):
                pe.wait_ge(xrow_ready, s + 1)
                pe.wait_ge(xcur_ready, s + 1)
                for k in range(KT):
                    last = nc.tensor.transpose(ps[:, 7, k * P:(k + 1) * P], xrow[:, k * P:(k + 1) * P],
                                               identf[:, :])
                last.then_inc(xt_pe, 1)

            def gate_up(s, e):
                pe.wait_ge(xcur_ready, s + 2)
                for w, b0 in ((wg_s, 0), (wu_s, 2)):
                    for fh in range(2):
                        for k in range(KT):
                            last = mm(ps[:, b0 + fh, :], xcur[:, k, :],
                                      w[:, bass.ds((e * KT + k) * DFF + fh * HALF, HALF)], start=(k == 0),
                                      stop=(k == KT - 1))
                last.then_inc(gu_done, 1)

            def turn_h(s):
                pe.wait_ge(h_ready, s + 1)
                for f in range(FT):
                    last = nc.tensor.transpose(ps[:, 4 + f // 4, (f % 4) * P:(f % 4 + 1) * P],
                                               hcur[:, f * P:(f + 1) * P], identf[:, :])
                last.then_inc(ht_pe, 1)

            def down(s, e):
                pe.wait_ge(ht_ready, s + 1)
                pe.wait_ge(z_ready, s + 1)
                for f in range(FT):
                    last = mm(ps[:, 6, 0:DM], hT[:, f, :], wd_s[:, bass.ds((e * FT + f) * DM, DM)], start=(f == 0),
                              stop=(f == FT - 1))
                last.then_inc(y_done, 1)

            def expert_of(s):
                return pe.value_load(e_int[0:1, bass.ds(s, 1)], min_val=0, max_val=EXPERTS - 1)

            keep_warm(16, 4)
            pe.wait_ge(idx_ready, 1)
            turn_x(0)
            pe.wait_ge(w_in, 16 * 20)
            gate_up(0, expert_of(0))
            turn_x(1)
            keep_warm(8, 4)
            turn_h(0)
            with pe.Fori(1, SLOTS - 1) as s:
                gate_up(s, expert_of(s))
                turn_x(s + 1)
                down(s - 1, expert_of(s - 1))
                turn_h(s)
            gate_up(SLOTS - 1, expert_of(SLOTS - 1))
            down(SLOTS - 2, expert_of(SLOTS - 2))
            turn_h(SLOTS - 1)
            down(SLOTS - 1, expert_of(SLOTS - 1))

        @block.scalar
        def _(act):
            A = nc.scalar.activation

            def filled(j):
                act.wait_ge(pe_fill, j + 1)
                return j % 8

            act.wait_ge(ld_ctx, N_CTX)
            A(acol, alog, ACT.Exp).then_inc(a_exp, 1)
            for j in range(2):
                bank = filled(F_CTX + j)
                A(ctxT[:, j * HALF:(j + 1) * HALF], ps[:, bank, :], ACT.Copy).then_inc(act_evac, 1)
            bank = filled(F_DTW)
            A(dtwT, ps[0:RANK, bank, 0:DM], ACT.Copy).then_inc(act_evac, 1)
            act.wait_ge(consts, 2)
            for k in range(KT):
                for hf in range(2):
                    bank = filled(F_XIN + 2 * k + hf)
                    A(xin[:, k, 2 * hf:2 * hf + 2, PAD:PB], ps[:, bank, :].rearrange("p (b l) -> p b l", b=2),
                      ACT.Copy).then_inc(act_evac, 1)
            for k in range(KT):
                for hf in range(2):
                    bank = filled(F_XT + 2 * k + hf)
                    A(xT[:, k, hf * HALF:(hf + 1) * HALF], ps[:, bank, :], ACT.Copy).then_inc(act_evac, 1)
            for w in range(4):
                bank = filled(F_WT + w)
                dst = wT[:, w * KT:(w + 1) * KT, :] if w < 3 else woT[:, :, :]
                A(dst.rearrange("p k o -> p (k o)"), ps[:, bank, :], ACT.Copy).then_inc(act_evac, 1)
            def first_parts(n, f, sc):
                for m in range(KT):
                    for hf in range(2):
                        bank = filled(f + 2 * m + hf)
                        A(parts[n][0][:, m, hf * HALF:(hf + 1) * HALF], ps[:, bank, :], ACT.Copy,
                          scale=sc).then_inc(part_ready[n][0], 1)

            def second_part(n):
                act.wait_ge(dve_evac, 1 + 4 * (n + 1))
                A(parts[n][1], rest[n], ACT.Copy).then_inc(part_ready[n][1], 1)

            first_parts(0, F_Q, SCALE)
            act.wait_ge(consts, 3)
            for j in range(4):
                if j < KT:
                    act.wait_ge(conv_done, j + 1)
                    A(tb[:, j, :], ta[:, j, :], ACT.Tanh).then_inc(conv_tanh, 1)
                bank = filled(F_V + j)
                A(vaug[:, 2 * j:2 * j + 2, :, 0:DH].rearrange("p t h d -> p (t h) d"),
                  ps[:, bank, :].rearrange("p (h d) -> p h d", d=DH), ACT.Copy).then_inc(act_evac, 1)
            for hf in range(2):
                bank = filled(F_LOW + hf)
                A(dtlow[:, hf * HALF:(hf + 1) * HALF], ps[0:RANK, bank, :], ACT.Copy).then_inc(act_evac, 1)
            second_part(0)
            for k in range(KT):
                for hf in range(2):
                    bank = filled(F_DT + 2 * k + hf)
                    cols = slice(hf * HALF, (hf + 1) * HALF)
                    A(spt[:, k, cols], ps[:, bank, :], ACT.Abs, bias=dtb[:, k:k + 1]).then_inc(act_order, 1)
                    A(dts[:, k, cols], ps[:, bank, :], ACT.Relu, bias=dtb[:, k:k + 1]).then_inc(act_evac, 1)
            for k in range(KT):
                act.wait_ge(act_order, 2 * k + 2)
                A(spt[:, k, :], spt[:, k, :], ACT.Exp, scale=-1.0).then_inc(sp_exp, 1)
            first_parts(1, F_K, 1.0)
            second_part(1)
            for i, f in enumerate((F_B, F_C)):
                for hf in range(2):
                    bank = filled(f + hf)
                    cols = slice(hf * HALF, (hf + 1) * HALF)
                    A(bc3[:, i, cols], ps[0:96, bank, :], ACT.Copy).then_inc(act_order, 1)
                    A(bcf[:, i, cols], ps[0:96, bank, :], ACT.Copy).then_inc(act_evac, 1)

            def decay(m):
                b, n = m // STATES, m % STATES
                act.wait_ge(scanned, m + 1 if m >= 4 else 4)
                for k in range(KT):
                    A(dA[m % 4][:, k, 1:SEQ], dts[:, k, b * SEQ + 1:(b + 1) * SEQ], ACT.Exp,
                      scale=acol[:, k, n:n + 1]).then_inc(da_ready, 1)

            act.wait_ge(scan_in, 1)
            decay(0)
            decay(1)
            def take_bc(m):
                act.wait_ge(bc_ready, m + 1)
                if m >= 3:
                    act.wait_ge(hc_ready, m - 2)
                A(bcs[m % 3].rearrange("p i l -> p (i l)"), ps[:, 5, :], ACT.Copy).then_inc(bc_taken, 1)

            def copy_context(n):
                act.wait_ge(pv_done, n + 1)
                if n >= 2 * QUADS and n % QUADS == 0:
                    act.wait_ge(x1_ready, n // QUADS - 1)
                A(ctxS[n // QUADS % 2][:, n % QUADS, :], ps[:, 6, 0:SEQ], ACT.Copy).then_inc(pv_out, 1)

            def squash(b):
                act.wait_ge(x1_ready, b + 1)
                A(sg, xres[:, 2 * b:2 * b + 2, :], ACT.Tanh, scale=0.5).then_inc(sg_ready, 1)

            take_bc(0)
            for n in range(4 * QUADS * BATCH):
                slot, kt, pr = n // 4, n // 2 % 2, n % 2
                act.wait_ge(b_scores, n + 1)
                if slot >= 2:
                    act.wait_ge(pv_done, slot - 1)
                A(prob[2 * (slot % 2) + kt][:, pr * HALF:(pr + 1) * HALF], ps[:, 2 + n % 3, :],
                  ACT.Exp).then_inc(p_ready, 1)
                if n % 2 == 0 and n // 2 + 1 < STATES * BATCH:
                    take_bc(n // 2 + 1)
                if n % 2 == 1 and n // 2 + 2 < STATES * BATCH:
                    decay(n // 2 + 2)
                if n % 4 == 2 and slot:
                    copy_context(slot - 1)
                if slot // QUADS and slot % QUADS == 6 and n % 4 == 0:
                    squash(slot // QUADS - 1)
            copy_context(QUADS * BATCH - 1)
            squash(BATCH - 1)
            act.wait_ge(logit_dve, 1)
            A(ex, lg, ACT.Exp).then_inc(gate_exp, 1)
            act.wait_ge(hot_ready, TT)
            A(zrow[:, 0:1], identf[:, 0:1], ACT.Silu).then_inc(act_order, 1)

            def take_x(s):
                act.wait_ge(xt_pe, s + 1)
                act.wait_ge(gu_done, s + 1)
                A(xcur.rearrange("p k t -> p (k t)"), ps[:, 7, 0:DM], ACT.Copy).then_inc(xcur_ready, 1)

            def silu_gate(s):
                act.wait_ge(gu_done, s + 2)
                A(ge, ps[:, 0:2, :].rearrange("p b c -> p (b c)"), ACT.Silu).then_inc(ge_ready, 1)

            def put_hT(s):
                act.wait_ge(ht_pe, s + 1)
                A(hT.rearrange("p f t -> p (f t)"), ps[:, 4:6, :].rearrange("p b c -> p (b c)"),
                  ACT.Copy).then_inc(ht_ready, 1)

            act.sem_inc(xcur_ready, 1)
            act.sem_inc(gu_done, 1)
            take_x(0)
            silu_gate(0)
            take_x(1)
            put_hT(0)
            with act.Fori(1, SLOTS - 1) as s:
                silu_gate(s)
                take_x(s + 1)
                put_hT(s)
            silu_gate(SLOTS - 1)
            put_hT(SLOTS - 1)

        @block.vector
        def _(dve):
            v = nc.vector
            order = [0]

            def link(ins):
                order[0] += 1
                ins.then_inc(dve_order, 1)
                dve.wait_ge(dve_order, order[0])

            R = RANK + 2 * STATES
            dve.wait_ge(consts, 2)
            dve.wait_ge(pe_fill, F_INW + 1)
            xpt = ps[:, 2, DM:DM + KT * R].rearrange("p (k r) -> p k r", k=KT)
            v.tensor_copy(inwT, ps[:, 2, 0:DM])
            for c in range(3):
                v.tensor_copy(xpB[:, :, 32 * c:32 * c + STATES], xpt[:, :, RANK:RANK + STATES])
                v.tensor_copy(xpC[:, :, 32 * c:32 * c + STATES], xpt[:, :, RANK + STATES:R])
            v.tensor_copy(xpD, xpt[:, :, 0:RANK]).then_inc(dve_evac, 1)
            dve.wait_ge(ld_misc, 48)
            mid = diag[:, SEQ - 64:SEQ - 64 + TABLE]
            link(v.tensor_reduce(mid, relrow, axis=AX.X, op=ALU.add))
            link(v.tensor_scalar_mul(mid, mid, 1.0 / DH))
            lo = SEQ - 64
            v.tensor_copy(diag[:, 0:lo], diag[:, lo:lo + 1].broadcast_to([1, lo]))
            link(v.tensor_copy(diag[:, lo + TABLE:SPREAD],
                               diag[:, lo + TABLE - 1:lo + TABLE].broadcast_to([1, SPREAD - lo - TABLE])))
            v.tensor_copy(diag[:, SPREAD:SPREAD + 1], diag[:, 0:1]).then_inc(diag_ready, 1)
            v.tensor_scalar_mul(cw, cw, 0.5)
            link(v.tensor_scalar_mul(cb, cb, 0.5))
            for k in range(KT):
                dve.wait_ge(act_evac, F_XIN + 2 * k + 1)
                o = ta[:, k, :].rearrange("p (b l) -> p b l", b=BATCH)
                link(v.tensor_scalar(o, xin[:, k, :, PAD:PB], cw[:, k, PAD:TAPS], cb[:, k:k + 1], ALU.mult, ALU.add))
                for j in range(PAD):
                    ins = v.scalar_tensor_tensor(out=o, in0=xin[:, k, :, j:j + SEQ], scalar=cw[:, k, j:j + 1],
                                                 in1=o, op0=ALU.mult, op1=ALU.add)
                    if j < PAD - 1:
                        link(ins)
                    else:
                        ins.then_inc(conv_done, 1)
            for k in range(KT):
                dve.wait_ge(conv_tanh, k + 1)
                v.scalar_tensor_tensor(out=u[:, k, :], in0=tb[:, k, :], scalar=1.0, in1=ta[:, k, :], op0=ALU.add,
                                       op1=ALU.mult).then_inc(u_ready, 1)
            def leave(n, i):
                f, sc = ((F_Q, SCALE), (F_K, 1.0))[n]
                m, cols = i // 2, slice(i % 2 * HALF, (i % 2 + 1) * HALF)
                dve.wait_ge(part_ready[n][0], i + 1)
                v.scalar_tensor_tensor(out=rest[n][:, m, cols], in0=ps[:, (f + i) % 8, :], scalar=sc,
                                       in1=parts[n][0][:, m, cols], op0=ALU.mult,
                                       op1=ALU.subtract).then_inc(dve_evac, 1)

            def third_part(n):
                dve.wait_ge(part_ready[n][1], 1)
                v.tensor_tensor(parts[n][2], rest[n], parts[n][1], ALU.subtract).then_inc(part_ready[n][2], 1)

            for i in range(4):
                leave(0, i)
            dve.wait_ge(hank_in, 64)
            v.tensor_copy(hank_hi[:, :, :], hankel)
            link(v.tensor_copy(hank2[:, :, :], hankel2))
            link(v.tensor_tensor(hank2[QB:P, :, :], hankel2[QB:P, :, :], hank2[QB:P, :, :], ALU.subtract))
            dve.sem_inc(hank_ready, 1)
            def maxima(b, pair, qt, n):
                dve.wait_ge(a_scores, n + 1)
                v.tensor_reduce(negm[b % 2][:, qt, 2 * pair:2 * pair + 2],
                                ps[:, n % 2, :].rearrange("p (h k) -> p h k", h=2), axis=AX.X,
                                op=ALU.max).then_inc(a_max, 1)

            third_part(0)
            dve.wait_ge(a_exp, 1)
            v.tensor_scalar_mul(acol, acol, -1.0)
            wait_evac(dve, F_DT + 3)
            units = list(A_UNITS[0, -2])
            for k in range(KT):
                dve.wait_ge(sp_exp, k + 1)
                link(v.tensor_scalar_mul(tb[:, k, :], spt[:, k, :], LOG1P[-1]))
                for step, c in enumerate(LOG1P[-2::-1]):
                    v.scalar_tensor_tensor(out=tb[:, k, :], in0=tb[:, k, :], scalar=c, in1=spt[:, k, :],
                                           op0=ALU.add, op1=ALU.mult).then_inc(dve_order, 1)
                    order[0] += 1
                    if k == 0 and 1 <= step <= 4:
                        leave(1, step - 1)
                    if (k, step) == (0, 6):
                        third_part(1)
                    if k == 1 and step >= 5:
                        for _ in range(2):
                            maxima(*units.pop(0))
                    dve.wait_ge(dve_order, order[0])
                link(v.tensor_tensor(dts[:, k, :], dts[:, k, :], tb[:, k, :], ALU.add))
            dve.wait_ge(pe_fill, FILLS)
            dve.sem_inc(dt_ready, 1)
            link(v.tensor_tensor(dtu[:, :, 0:SEQ], dts[:, :, 0:SEQ], u[:, :, 0:SEQ], ALU.mult))
            for i in range(4):
                v.memset(dA[i][:, :, 0:1], 0.0).then_inc(scanned, 1)
            wait_evac(dve, F_B)
            link(v.memset(ps[:, 6, :], 0.0))
            dve.sem_inc(pv_out, 1)
            dve.sem_inc(scan_in, 1)

            def inject(m):
                b = m // STATES
                dve.wait_ge(bc_taken, m + 1)
                if m % STATES == 0:
                    dve.wait_ge(split_ready, b + 1)
                v.tensor_tensor(dBu[m % 2], dtu[:, :, b * SEQ:(b + 1) * SEQ],
                                bcs[m % 3][:, 0:1, :].broadcast_to([P, KT, SEQ]), ALU.mult).then_inc(dbu_ready, 1)

            def scan(m):
                flat = "p k l -> p (k l)"
                wait_dbu(dve, m)
                dve.wait_ge(da_ready, 2 * m + 2)
                if m >= 4:
                    dve.wait_ge(y_added, m - 3)
                v.tensor_tensor_scan(out=hst[m % 4].rearrange(flat), data0=dA[m % 4].rearrange(flat),
                                     data1=dBu[m % 2].rearrange(flat), initial=0.0, op0=ALU.mult,
                                     op1=ALU.add).then_inc(scanned, 1)

            misc, ending = [0], [0]

            def misc_filled():
                if ending[0]:
                    ending[0] += 1
                misc[0] += 1
                dve.wait_ge(tail_pe, misc[0])

            def bank():
                return END_BANKS[(ending[0] - 2) % len(END_BANKS)] if ending[0] else 7

            def ctx_rows(qt):
                return (prob[0] if qt and ending[0] else ctxn)[:, 0:DM]

            def ctx_cols(qt):
                return prob[0][:, DM:2 * DM] if qt and ending[0] else ctxnT

            def put_max(b, hh):
                misc_filled()
                if b:
                    dve.wait_ge(m_in[hh], 16 * b)
                link(v.tensor_scalar_mul(negmT[hh], ps[0:HEADS // 2, bank(), 0:SEQ], -1.0))
                dve.sem_inc(m_ready[hh], 1)
                dve.sem_inc(tail_dve, 1)

            def tail(b, step):
                qt, k = step // 4, step % 4
                misc_filled()
                if k < 2:
                    dve.wait_ge(tail_dve, misc[0] - 1)
                    quad = ps[:, bank(), :].rearrange("p (h c) -> p h c", c=32)
                    link(v.reciprocal(rcp.rearrange("p (h o) -> p h o", o=1), quad[:, :, DH:VW]))
                    v.tensor_tensor(ctx_rows(qt)[:, k * P:(k + 1) * P].rearrange("p (h d) -> p h d", d=DH),
                                    quad[:, :, 0:DH],
                                    rcp.rearrange("p (h o) -> p h o", o=1).broadcast_to([P, 16, DH]),
                                    ALU.mult).then_inc(tail_dve, 1)
                elif k == 2:
                    v.tensor_copy(ctx_cols(qt), ps[:, bank(), 0:DM]).then_inc(tail_dve, 1)
                else:
                    t = 2 * b + qt
                    v.tensor_tensor(xres[:, t, :], xres[:, t, :], ps[:, bank(), 0:DM], ALU.add).then_inc(tail_dve, 1)
                    dve.wait_ge(tail_dve, misc[0])
                    link(v.bn_stats(stats[:, t, :], xres[:, t, :]))
                    link(v.bn_aggr(mv[:, t, :], stats[:, t, :]))

            def seed(b):
                two = slice(2 * b, 2 * b + 2)
                vb, rb = veps[:, two], rstd[:, two]
                link(v.tensor_scalar_add(vb, mv[:, two, 1], EPS))
                link(v.tensor_scalar(rb.bitcast(I32), vb.bitcast(I32), 1, None, ALU.logical_shift_right))
                link(v.tensor_scalar(rb.bitcast(I32), rb.bitcast(I32), -1.0, float(RSQRT_SEED), ALU.mult, ALU.add))
                link(v.tensor_scalar_mul(vb, vb, -0.5))

            def newton(b):
                two = slice(2 * b, 2 * b + 2)
                vb, rb, wb = veps[:, two], rstd[:, two], nwt[:, two]
                link(v.tensor_tensor(wb, rb, rb, ALU.mult))
                link(v.tensor_tensor(wb, wb, vb, ALU.mult))
                link(v.scalar_tensor_tensor(out=rb, in0=wb, scalar=1.5, in1=rb, op0=ALU.add, op1=ALU.mult))

            def centre(b, ready):
                for t in (2 * b, 2 * b + 1):
                    link(v.tensor_scalar(xres[:, t, :], xres[:, t, :], mv[:, t, 0:1], rstd[:, t:t + 1],
                                         ALU.subtract, ALU.mult))
                dve.sem_inc(ready, 1)

            def normalise(b, ready):
                seed(b)
                for _ in range(3):
                    newton(b)
                centre(b, ready)

            def gate(b):
                dve.wait_ge(sg_ready, b + 1)
                dve.wait_ge(y_added, STATES * (b + 1))
                link(v.scalar_tensor_tensor(out=sg, in0=sg, scalar=1.0, in1=xres[:, 2 * b:2 * b + 2, :], op0=ALU.add,
                                            op1=ALU.mult))
                v.scalar_tensor_tensor(out=gated, in0=sg, scalar=0.5, in1=yT[:, :, b * SEQ:(b + 1) * SEQ],
                                       op0=ALU.mult, op1=ALU.mult).then_inc(gated_ready, 1)

            def add_mixed(b):
                misc_filled()
                both = xres[:, 2 * b:2 * b + 2, :].rearrange("p t d -> p (t d)")
                link(v.tensor_tensor(both, both, ps[:, bank(), :], ALU.add))
                dve.sem_inc(tail_dve, 1)
                for t in (2 * b, 2 * b + 1):
                    link(v.bn_stats(stats[:, t, :], xres[:, t, :]))
                for t in (2 * b, 2 * b + 1):
                    link(v.bn_aggr(mv[:, t, :], stats[:, t, :]))

            def put_x2(b):
                misc_filled()
                v.tensor_copy(x2T.rearrange("p k t -> p (k t)"), ps[:, bank(), :]).then_inc(tail_dve, 1)

            def put_logits(b):
                misc_filled()
                v.tensor_tensor(lg[:, 2 * b:2 * b + 2, :],
                                ps[:, bank(), 0:2 * EXPERTS].rearrange("p (t e) -> p t e", e=EXPERTS),
                                br_s[:, :].rearrange("p (o e) -> p o e", o=1).broadcast_to([P, 2, EXPERTS]),
                                ALU.add).then_inc(tail_dve, 1)

            for unit in units:
                maxima(*unit)
            put_max(0, 0)
            for unit in A_UNITS[0, -1]:
                maxima(*unit)
            for b in range(BATCH):
                for qd in range(QUADS):
                    for i in range(4):
                        m = 2 * (QUADS * b + qd) + i // 2
                        if i % 2 == 0:
                            if not by_pool(m):
                                inject(m)
                        for unit in quarter(A_UNITS[b, qd], i):
                            maxima(*unit)
                        if i % 2 == 0:
                            scan(m)
                        if b >= 2 and (qd, i) == (1, 3):
                            put_logits(b - 2)
                        if b and 1 <= qd <= 4 and i % 2 == 1:
                            tail(b - 1, 2 * (qd - 1) + i // 2)
                        if b and (qd, i) == (7, 0):
                            add_mixed(b - 1)
                        if b and (qd, i) in ((4, 3), (7, 0)):
                            seed(b - 1)
                        if b and (qd, i) in ((5, 0), (5, 1), (5, 2), (7, 1), (7, 2), (7, 3)):
                            newton(b - 1)
                        if b and (qd, i) == (5, 3):
                            centre(b - 1, x1_ready)
                        if b and (qd, i) == (6, 1):
                            gate(b - 1)
                        if (b, qd, i) == (0, 2, 3):
                            put_max(0, 1)
                        if b + 1 < BATCH and (qd, i) in ((5, 1), (7, 1)):
                            put_max(b + 1, qd // 7)
                        if b >= 2 and (qd, i) == (0, 0):
                            centre(b - 2, x2_ready)
                        if b >= 2 and (qd, i) == (1, 0):
                            put_x2(b - 2)
            ending[0] = 1
            centre(BATCH - 2, x2_ready)
            for step in (0, 1, 4, 5):
                tail(BATCH - 1, step)
            put_x2(BATCH - 2)
            for step in (2, 6, 3, 7):
                tail(BATCH - 1, step)
            put_logits(BATCH - 2)
            normalise(BATCH - 1, x1_ready)
            gate(BATCH - 1)
            add_mixed(BATCH - 1)
            normalise(BATCH - 1, x2_ready)
            put_x2(BATCH - 1)
            put_logits(BATCH - 1)

            dve.wait_ge(tail_dve, misc[0])
            link(v.tensor_reduce(lmax, lg, axis=AX.X, op=ALU.max))
            lmax3 = lmax.rearrange("p (t o) -> p t o", o=1).broadcast_to([P, TT, EXPERTS])
            link(v.tensor_tensor(oh, lg, lmax3, ALU.is_ge))
            link(v.tensor_tensor(lg, lg, lmax3, ALU.subtract))
            link(v.tensor_copy(run, oh[:, :, 0]))
            v.tensor_copy(ohb[:, 0, :], oh[:, :, 0]).then_inc(logit_dve, 1)
            for e in range(1, EXPERTS):
                link(v.tensor_tensor(ohb[:, e, :], oh[:, :, e], run, ALU.is_gt))
                link(v.tensor_tensor(run, run, oh[:, :, e], ALU.max))
            dve.sem_inc(oh_ready, 1)
            dve.wait_ge(gate_exp, 1)
            link(v.tensor_reduce(lsum, ex, axis=AX.X, op=ALU.add))
            link(v.reciprocal(gate_w, lsum))
            link(v.tensor_copy(tokg[:, :, 1], gate_w))
            link(v.tensor_tensor(tokg[:, :, 2], gate_w, tokg[:, :, 1], ALU.subtract))
            dve.wait_ge(count_pe, 1)
            dve.wait_ge(consts, 4)
            v.tensor_copy(within.rearrange("p e t -> p (e t)"), ps[:, 5, 0:EXPERTS * TT])
            link(v.tensor_copy(total.rearrange("p e t -> p (e t)"), ps[:, 6, 0:EXPERTS * TT]))
            for e in range(EXPERTS):
                link(v.tensor_tensor_scan(out=incl[:, e, :], data0=ones32[:, 0:TT], data1=total[:, e, :],
                                          initial=0.0, op0=ALU.mult, op1=ALU.add))
            link(v.tensor_tensor(over, incl[:, :, TT - 1:TT].broadcast_to([P, EXPERTS, TT]),
                                 thr.rearrange("p (o t) -> p o t", o=1).broadcast_to([P, EXPERTS, TT]), ALU.is_gt))
            link(v.tensor_reduce(ntile, over, axis=AX.X, op=ALU.add))
            link(v.tensor_tensor_scan(out=tile_incl, data0=ones32[:, 0:EXPERTS], data1=ntile, initial=0.0,
                                      op0=ALU.mult, op1=ALU.add))
            link(v.tensor_tensor(tile0, tile_incl, ntile, ALU.subtract))
            link(v.tensor_tensor(within, within, incl, ALU.add))
            link(v.tensor_tensor(within, within, total, ALU.subtract))
            link(v.scalar_tensor_tensor(out=within, in0=tile0.rearrange("p (e o) -> p e o", o=1)
                                        .broadcast_to([P, EXPERTS, TT]), scalar=float(P), in1=within,
                                        op0=ALU.mult, op1=ALU.add))
            link(v.tensor_tensor(within, within, ohb, ALU.mult))
            link(v.tensor_reduce(pos, within.rearrange("p e t -> p t e"), axis=AX.X, op=ALU.add))
            for t in range(TT):
                v.tensor_scalar(onehot[t], iota16, pos[:, t:t + 1], None, ALU.is_equal).then_inc(hot_ready, 1)
            link(v.tensor_scalar(e_of, tile_no, tile0[:, 1:2], None, ALU.is_ge))
            for e in range(2, EXPERTS):
                link(v.scalar_tensor_tensor(out=e_of, in0=tile_no, scalar=tile0[:, e:e + 1], in1=e_of,
                                            op0=ALU.is_ge, op1=ALU.add))
            link(v.tensor_copy(e_int, e_of))
            dve.wait_ge(idx_pe, 1)
            found = ps[:, 7, 0:4 * SLOTS].rearrange("p (s c) -> p s c", c=4)
            link(v.tensor_scalar_add(idx, found[:, :, 0], float(FAR)))
            link(v.tensor_copy(gslot, found[:, :, 1]))
            link(v.tensor_tensor(gslot, gslot, found[:, :, 2], ALU.add))
            dve.sem_inc(idx_ready, 1)

            def make_h(s):
                dve.wait_ge(ge_ready, s + 1)
                v.tensor_tensor(hcur, ge, ps[:, 2:4, :].rearrange("p b c -> p (b c)"), ALU.mult).then_inc(h_ready, 1)

            def finish_rows(s):
                row = rows_s[:, bass.ds(s, 1), :].rearrange("p o d -> p (o d)")
                at = [ROW_STEPS * s]

                def step(ins):
                    at[0] = at[0] + 1
                    ins.then_inc(row_order, 1)
                    dve.wait_ge(row_order, at[0])

                dve.wait_ge(row_ready, s + 1)
                dve.wait_ge(y_done, s + 1)
                step(v.scalar_tensor_tensor(out=zrow, in0=ps[:, 6, 0:DM], scalar=gslot[:, bass.ds(s, 1)], in1=row,
                                            op0=ALU.mult, op1=ALU.add))
                step(v.bn_stats(stats[:, 0, :], zrow))
                dve.sem_inc(dve_mark, 1)
                step(v.bn_aggr(mv[:, 0, :], stats[:, 0, :]))
                dve.sem_inc(z_ready, 1)
                v.tensor_scalar(minus_half, mv[:, 0, 1:2], EPS, -0.5, ALU.add, ALU.mult).then_inc(row_order, 1)
                at[0] = at[0] + 1
                step(v.tensor_scalar_add(ve, mv[:, 0, 1:2], EPS))
                step(v.tensor_scalar(rs.bitcast(I32), ve.bitcast(I32), 1, None, ALU.logical_shift_right))
                step(v.tensor_scalar(rs.bitcast(I32), rs.bitcast(I32), -1.0, float(RSQRT_SEED), ALU.mult, ALU.add))
                for _ in range(3):
                    step(v.scalar_tensor_tensor(out=nw, in0=rs, scalar=minus_half, in1=rs, op0=ALU.mult, op1=ALU.mult))
                    step(v.scalar_tensor_tensor(out=rs, in0=nw, scalar=1.5, in1=rs, op0=ALU.add, op1=ALU.mult))
                v.tensor_scalar(row, zrow, mv[:, 0, 0:1], rs, ALU.subtract, ALU.mult).then_inc(row_ready, 1)

            dve.wait_ge(act_order, 9)
            dve.sem_inc(row_ready, 1)
            dve.sem_inc(z_ready, 1)
            ve, minus_half, rs, nw = veps[:, 0:1], veps[:, 1:2], rstd[:, 0:1], nwt[:, 0:1]
            ROW_STEPS = 13
            make_h(0)
            with dve.Fori(1, SLOTS) as s:
                make_h(s)
                finish_rows(s - 1)
            finish_rows(SLOTS - 1)


_INS = ["x", "ctx_1024", "L0_attn_wq", "L0_attn_wk", "L0_attn_wv", "L0_attn_wo", "L0_attn_rel_pos",
        "L0_xattn_in_proj_w", "L0_xattn_conv_w", "L0_xattn_conv_b", "L0_xattn_x_proj_w", "L0_xattn_dt_proj_w",
        "L0_xattn_dt_proj_b", "L0_xattn_A_log", "L0_xattn_D", "L0_ffn_Wr", "L0_ffn_br", "L0_ffn_Wg", "L0_ffn_Wu",
        "L0_ffn_Wd"]


def kernel(**inputs):
    import numpy as _np
    import concourse.bacc as _bacc
    from concourse.bass_utils import run_bass_kernel_spmd as _run

    nc = _bacc.Bacc("TRN2", target_bir_lowering=False, num_devices=1)
    arrays, args = {}, []
    for name in _INS:
        a = _np.ascontiguousarray(inputs[name])
        arrays[f"in_{name}"] = a
        args.append(nc.dram_tensor(f"in_{name}", a.shape, mybir.dt.from_np(a.dtype), kind="ExternalInput").ap())
    args.append(nc.dram_tensor("out_0", (BATCH, SEQ, DM), F32, kind="ExternalOutput").ap())
    decoder_layer(nc, *args)
    r = _run(nc, [arrays], core_ids=[0])
    return r.results[0]["out_0"]
```
